# Optimizing a Trainium2 kernel written in Bass

```python
import numpy as np
import jax
import jax.numpy as jnp

def _softmax(x, axis=-1):
    return jax.nn.softmax(x, axis=axis)

def _gelu(x):
    return jax.nn.gelu(x, approximate=True)

def _silu(x):
    return jax.nn.silu(x)

def _sigmoid(x):
    return jax.nn.sigmoid(x)

def _layernorm(x, axis=-1, eps=1e-05):
    m = jnp.mean(x, axis=axis, keepdims=True)
    v = jnp.var(x, axis=axis, keepdims=True)
    return (x - m) / jnp.sqrt(v + eps)

def _scatter_add(tgt, idx, src, axis=0):
    return tgt.at[idx].add(src)

def _segment_sum(src, seg, n):
    return jax.ops.segment_sum(src, seg, n)
kernel_name = 'mk_lm_tower_d1_tok_ids1024_r4_e086c0'

def setup_inputs(seed: int=0):
    np.random.seed(seed)
    _w = jnp.asarray

    def _rec_inputs():
        import jax
        import jax.numpy as jnp
        _rk = jax.random.key(seed)
        x = jax.random.randint(jax.random.fold_in(_rk, 1), (4, 2048), 0, 127998, jnp.int32)
        return x
    x = _rec_inputs()

    def _L0_tok_setup():
        import jax, jax.numpy as jnp
        import numpy as np
        VOCAB = 32000
        D_EMBED = 256
        D_PROJ = 256
        DIV_VAL = 4
        CUTOFFS = [5000, 10000, 25000, VOCAB]
        CUT_ENDS = [0] + CUTOFFS
        key = jax.random.key(seed)
        ks = jax.random.split(key, 2 * len(CUTOFFS) + 1)
        inp = jax.random.randint(ks[0], (8, 512), 0, VOCAB, dtype=jnp.int64 if jax.config.jax_enable_x64 else jnp.int32)
        d = {'inp': inp}
        for i in range(len(CUTOFFS)):
            l, r = (CUT_ENDS[i], CUT_ENDS[i + 1])
            de = D_EMBED // DIV_VAL ** i
            d[f'emb_{i}'] = jax.random.normal(ks[2 * i + 1], (r - l, de), jnp.float32) * 0.02
            d[f'proj_{i}'] = jax.random.normal(ks[2 * i + 2], (D_PROJ, de), jnp.float32) * 0.02
        return d
    _L0_tok_all = _L0_tok_setup()
    _L0_tok_in = {k: v for k, v in _L0_tok_all.items() if k in ('emb_0', 'proj_0', 'emb_1', 'proj_1', 'emb_2', 'proj_2', 'emb_3', 'proj_3')}
    del _L0_tok_all

    def _L0_attn_setup():
        import jax, jax.numpy as jnp
        import numpy as np
        B, N, D = (4, 512, 256)
        H = 8
        DK = D // H
        DV = D // H
        DF = 2 * DK
        CHUNK = 64
        RMS_EPS = 1e-05

        def _hedgehog(x, w, b):
            y = jnp.einsum('bhnd,ed->bhne', x, w) + b
            return jnp.concatenate([jnp.exp(y), jnp.exp(-y)], axis=-1)

        def _fused_chunk_linear_attn(q, k, v):
            b, h, n, df = q.shape
            dv = v.shape[-1]
            nc = n // CHUNK

            def to_chunks(t):
                d = t.shape[-1]
                return t.reshape(b, h, nc, CHUNK, d).transpose(2, 0, 1, 3, 4)
            qc, kc, vc = (to_chunks(q), to_chunks(k), to_chunks(v))
            mask = jnp.tril(jnp.ones((CHUNK, CHUNK), dtype=bool))

            def step(S, inp):
                qi, ki, vi = inp
                attn = jnp.einsum('bhcd,bhed->bhce', qi, ki)
                attn = jnp.where(mask, attn, 0.0)
                intra = jnp.einsum('bhce,bhev->bhcv', attn, vi)
                inter = jnp.einsum('bhcd,bhdv->bhcv', qi, S)
                S = S + jnp.einsum('bhcd,bhcv->bhdv', ki, vi)
                return (S, intra + inter)
            S0 = jnp.zeros((b, h, df, dv), dtype=q.dtype)
            _, oc = jax.lax.scan(step, S0, (qc, kc, vc))
            return oc.transpose(1, 2, 0, 3, 4).reshape(b, h, n, dv)
        key = jax.random.key(seed)
        ks = jax.random.split(key, 10)
        s = D ** (-0.5)
        x = jax.random.normal(ks[0], (B, N, D), dtype=jnp.float32)
        Wq = jax.random.normal(ks[1], (D, D), dtype=jnp.float32) * s
        Wk = jax.random.normal(ks[2], (D, D), dtype=jnp.float32) * s
        Wv = jax.random.normal(ks[3], (D, D), dtype=jnp.float32) * s
        Wo = jax.random.normal(ks[4], (D, D), dtype=jnp.float32) * s
        eye = jnp.eye(DK, dtype=jnp.float32)
        fmq_w = eye + 0.02 * jax.random.normal(ks[5], (DK, DK), dtype=jnp.float32)
        fmq_b = 0.02 * jax.random.normal(ks[6], (DK,), dtype=jnp.float32)
        fmk_w = eye + 0.02 * jax.random.normal(ks[7], (DK, DK), dtype=jnp.float32)
        fmk_b = 0.02 * jax.random.normal(ks[8], (DK,), dtype=jnp.float32)
        rms_w = 1.0 + 0.1 * jax.random.normal(ks[9], (DV,), dtype=jnp.float32)
        return {'x': x, 'Wq': Wq, 'Wk': Wk, 'Wv': Wv, 'Wo': Wo, 'fmq_w': fmq_w, 'fmq_b': fmq_b, 'fmk_w': fmk_w, 'fmk_b': fmk_b, 'rms_w': rms_w}
    _L0_attn_all = _L0_attn_setup()
    _L0_attn_in = {k: v for k, v in _L0_attn_all.items() if k in ('Wq', 'Wk', 'Wv', 'Wo', 'fmq_w', 'fmq_b', 'fmk_w', 'fmk_b', 'rms_w')}
    del _L0_attn_all

    def _L0_ffn_setup():
        import jax, jax.numpy as jnp
        import numpy as np
        B, T, D, E, H = (4, 512, 256, 4, 8)
        EPS = 1e-05

        def _uniform(k, shape, bound):
            return jax.random.uniform(k, shape, jnp.float32, -bound, bound)

        def _layernorm(x, w, b):
            mu = jnp.mean(x, axis=-1, keepdims=True)
            var = jnp.mean(jnp.square(x - mu), axis=-1, keepdims=True)
            return (x - mu) * jax.lax.rsqrt(var + EPS) * w + b
        key = jax.random.key(seed)
        ks = jax.random.split(key, 12)
        wb = np.sqrt(6.0 / D) / np.sqrt(6.0)
        wb = 1.0 / np.sqrt(D)
        return {'x': jax.random.normal(ks[0], (B, T, D), jnp.float32), 'router_prob': jax.random.uniform(ks[1], (B, T, E), jnp.float32), 'norm_w': jnp.ones((D,), jnp.float32), 'norm_b': jnp.zeros((D,), jnp.float32), 'q_w': _uniform(ks[2], (D, D), wb), 'q_b': _uniform(ks[3], (D,), wb), 'k_w': _uniform(ks[4], (D, D), wb), 'k_b': _uniform(ks[5], (D,), wb), 'v_w': _uniform(ks[6], (D, D), wb), 'v_b': _uniform(ks[7], (D,), wb), 'o_w': _uniform(ks[8], (D, D), wb), 'o_b': _uniform(ks[9], (D,), wb)}
    _L0_ffn_all = _L0_ffn_setup()
    _L0_ffn_in = {k: v for k, v in _L0_ffn_all.items() if k in ('router_prob', 'norm_w', 'norm_b', 'q_w', 'q_b', 'k_w', 'k_b', 'v_w', 'v_b', 'o_w', 'o_b')}
    del _L0_ffn_all
    return {'x': x, 'L0_tok_emb_0': _L0_tok_in['emb_0'], 'L0_tok_proj_0': _L0_tok_in['proj_0'], 'L0_tok_emb_1': _L0_tok_in['emb_1'], 'L0_tok_proj_1': _L0_tok_in['proj_1'], 'L0_tok_emb_2': _L0_tok_in['emb_2'], 'L0_tok_proj_2': _L0_tok_in['proj_2'], 'L0_tok_emb_3': _L0_tok_in['emb_3'], 'L0_tok_proj_3': _L0_tok_in['proj_3'], 'L0_attn_Wq': _L0_attn_in['Wq'], 'L0_attn_Wk': _L0_attn_in['Wk'], 'L0_attn_Wv': _L0_attn_in['Wv'], 'L0_attn_Wo': _L0_attn_in['Wo'], 'L0_attn_fmq_w': _L0_attn_in['fmq_w'], 'L0_attn_fmq_b': _L0_attn_in['fmq_b'], 'L0_attn_fmk_w': _L0_attn_in['fmk_w'], 'L0_attn_fmk_b': _L0_attn_in['fmk_b'], 'L0_attn_rms_w': _L0_attn_in['rms_w'], 'L0_ffn_router_prob': _L0_ffn_in['router_prob'], 'L0_ffn_norm_w': _L0_ffn_in['norm_w'], 'L0_ffn_norm_b': _L0_ffn_in['norm_b'], 'L0_ffn_q_w': _L0_ffn_in['q_w'], 'L0_ffn_q_b': _L0_ffn_in['q_b'], 'L0_ffn_k_w': _L0_ffn_in['k_w'], 'L0_ffn_k_b': _L0_ffn_in['k_b'], 'L0_ffn_v_w': _L0_ffn_in['v_w'], 'L0_ffn_v_b': _L0_ffn_in['v_b'], 'L0_ffn_o_w': _L0_ffn_in['o_w'], 'L0_ffn_o_b': _L0_ffn_in['o_b']}

def reference(x, L0_tok_emb_0, L0_tok_proj_0, L0_tok_emb_1, L0_tok_proj_1, L0_tok_emb_2, L0_tok_proj_2, L0_tok_emb_3, L0_tok_proj_3, L0_attn_Wq, L0_attn_Wk, L0_attn_Wv, L0_attn_Wo, L0_attn_fmq_w, L0_attn_fmq_b, L0_attn_fmk_w, L0_attn_fmk_b, L0_attn_rms_w, L0_ffn_router_prob, L0_ffn_norm_w, L0_ffn_norm_b, L0_ffn_q_w, L0_ffn_q_b, L0_ffn_k_w, L0_ffn_k_b, L0_ffn_v_w, L0_ffn_v_b, L0_ffn_o_w, L0_ffn_o_b):
    import jax
    import jax.numpy as jnp

    def _L0_tok_ref(inp, emb_0, proj_0, emb_1, proj_1, emb_2, proj_2, emb_3, proj_3):
        import jax, jax.numpy as jnp
        import numpy as np
        VOCAB = 32000
        D_EMBED = 256
        D_PROJ = 256
        DIV_VAL = 4
        CUTOFFS = [5000, 10000, 25000, VOCAB]
        CUT_ENDS = [0] + CUTOFFS
        embs = [emb_0, emb_1, emb_2, emb_3]
        projs = [proj_0, proj_1, proj_2, proj_3]
        flat = inp.reshape(-1)
        out = jnp.zeros((flat.shape[0], D_PROJ), jnp.float32)
        for i in range(len(CUTOFFS)):
            l, r = (CUT_ENDS[i], CUT_ENDS[i + 1])
            mask = (flat >= l) & (flat < r)
            idx = jnp.clip(flat - l, 0, r - l - 1)
            e = jnp.einsum('nd,pd->np', embs[i][idx], projs[i])
            out = out + jnp.where(mask[:, None], e, jnp.zeros((), e.dtype))
        emb_scale = jnp.asarray(D_PROJ ** 0.5, out.dtype)
        return (out * emb_scale).reshape(inp.shape + (D_PROJ,))

    def _L0_attn_ref(x, Wq, Wk, Wv, Wo, fmq_w, fmq_b, fmk_w, fmk_b, rms_w):
        import jax, jax.numpy as jnp
        import numpy as np
        B, N, D = (4, 512, 256)
        H = 8
        DK = D // H
        DV = D // H
        DF = 2 * DK
        CHUNK = 64
        RMS_EPS = 1e-05

        def _hedgehog(x, w, b):
            y = jnp.einsum('bhnd,ed->bhne', x, w) + b
            return jnp.concatenate([jnp.exp(y), jnp.exp(-y)], axis=-1)

        def _fused_chunk_linear_attn(q, k, v):
            b, h, n, df = q.shape
            dv = v.shape[-1]
            nc = n // CHUNK

            def to_chunks(t):
                d = t.shape[-1]
                return t.reshape(b, h, nc, CHUNK, d).transpose(2, 0, 1, 3, 4)
            qc, kc, vc = (to_chunks(q), to_chunks(k), to_chunks(v))
            mask = jnp.tril(jnp.ones((CHUNK, CHUNK), dtype=bool))

            def step(S, inp):
                qi, ki, vi = inp
                attn = jnp.einsum('bhcd,bhed->bhce', qi, ki)
                attn = jnp.where(mask, attn, 0.0)
                intra = jnp.einsum('bhce,bhev->bhcv', attn, vi)
                inter = jnp.einsum('bhcd,bhdv->bhcv', qi, S)
                S = S + jnp.einsum('bhcd,bhcv->bhdv', ki, vi)
                return (S, intra + inter)
            S0 = jnp.zeros((b, h, df, dv), dtype=q.dtype)
            _, oc = jax.lax.scan(step, S0, (qc, kc, vc))
            return oc.transpose(1, 2, 0, 3, 4).reshape(b, h, n, dv)
        b, n, d = x.shape
        split = lambda t: t.reshape(b, n, H, -1).transpose(0, 2, 1, 3)
        q = split(x @ Wq.T)
        k = split(x @ Wk.T)
        v = split(x @ Wv.T)
        q = _hedgehog(q, fmq_w, fmq_b)
        k = _hedgehog(k, fmk_w, fmk_b)
        scale = q.shape[-1] ** (-0.5)
        o = _fused_chunk_linear_attn(q * scale, k, v)
        o = o * jax.lax.rsqrt(jnp.mean(o * o, axis=-1, keepdims=True) + RMS_EPS) * rms_w
        o = o.transpose(0, 2, 1, 3).reshape(b, n, H * DV)
        return o @ Wo.T

    def _L0_ffn_ref(x, router_prob, norm_w, norm_b, q_w, q_b, k_w, k_b, v_w, v_b, o_w, o_b):
        import jax, jax.numpy as jnp
        import numpy as np
        B, T, D, E, H = (4, 512, 256, 4, 8)
        EPS = 1e-05

        def _uniform(k, shape, bound):
            return jax.random.uniform(k, shape, jnp.float32, -bound, bound)

        def _layernorm(x, w, b):
            mu = jnp.mean(x, axis=-1, keepdims=True)
            var = jnp.mean(jnp.square(x - mu), axis=-1, keepdims=True)
            return (x - mu) * jax.lax.rsqrt(var + EPS) * w + b
        e_cnt = router_prob.shape[2]
        b, t, d = x.shape
        n = t // e_cnt
        h = H
        scale = d ** (-0.5)
        qs, ks_, vs = ([], [], [])
        for e in range(e_cnt):
            xe = x[:, e * n:(e + 1) * n, :]
            xn = _layernorm(xe, norm_w, norm_b)
            m = d // 2 ** e
            xm = xn[..., :m]
            qs.append(jnp.einsum('bnm,dm->bnd', xm, q_w[:, :m]) + q_b)
            ks_.append(jnp.einsum('bnm,dm->bnd', xm, k_w[:, :m]) + k_b)
            vs.append(jnp.einsum('bnm,dm->bnd', xm, v_w[:, :m]) + v_b)
        q = jnp.concatenate(qs, axis=1)
        k = jnp.concatenate(ks_, axis=1)
        v = jnp.concatenate(vs, axis=1)
        dh = d // h
        q = q.reshape(b, t, h, dh).transpose(0, 2, 1, 3)
        k = k.reshape(b, t, h, dh).transpose(0, 2, 1, 3)
        v = v.reshape(b, t, h, dh).transpose(0, 2, 1, 3)
        attn = jnp.einsum('bhqd,bhkd->bhqk', q, k) * scale
        attn = jax.nn.softmax(attn, axis=-1)
        attn_out = jnp.einsum('bhqk,bhkd->bhqd', attn, v)
        attn_out = attn_out.transpose(0, 2, 1, 3).reshape(b, t, d)
        outs = []
        for e in range(e_cnt):
            sl = slice(e * n, (e + 1) * n)
            m = d // 2 ** e
            xm = attn_out[:, sl, :m]
            out = jnp.einsum('bnm,om->bno', xm, o_w[:m, :m]) + o_b[:m]
            pad = d - m
            if pad:
                out = jnp.pad(out, ((0, 0), (0, 0), (0, pad)))
            outs.append(out + x[:, sl, :])
        return jnp.concatenate(outs, axis=1)
    h = _L0_tok_ref(x, L0_tok_emb_0, L0_tok_proj_0, L0_tok_emb_1, L0_tok_proj_1, L0_tok_emb_2, L0_tok_proj_2, L0_tok_emb_3, L0_tok_proj_3)
    h = h + _L0_attn_ref(_layernorm(h, axis=-1), L0_attn_Wq, L0_attn_Wk, L0_attn_Wv, L0_attn_Wo, L0_attn_fmq_w, L0_attn_fmq_b, L0_attn_fmk_w, L0_attn_fmk_b, L0_attn_rms_w)
    h = h + _L0_ffn_ref(_layernorm(h, axis=-1), L0_ffn_router_prob, L0_ffn_norm_w, L0_ffn_norm_b, L0_ffn_q_w, L0_ffn_q_b, L0_ffn_k_w, L0_ffn_k_b, L0_ffn_v_w, L0_ffn_v_b, L0_ffn_o_w, L0_ffn_o_b)
    return h

_drawn_inputs = setup_inputs


def setup_inputs(seed=0):
    import zlib

    import numpy as np

    out = dict(_drawn_inputs(seed))
    spreads = {'L0_ffn_norm_w': (1.0, 0.6), 'L0_ffn_norm_b': (0.0, 0.8)}
    factors = {'L0_attn_fmq_b': 5.056,
     'L0_attn_fmk_b': 5.543,
     'L0_ffn_q_w': 8.0,
     'L0_ffn_q_b': 39.865,
     'L0_ffn_k_w': 8.0,
     'L0_ffn_k_b': 64.0,
     'L0_ffn_v_b': 8.0,
     'L0_ffn_o_b': 4.442}
    for name, (base, spread) in spreads.items():
        noise = np.random.default_rng([zlib.crc32(name.encode()), seed]).standard_normal(out[name].shape)
        drawn = base * np.exp(spread * noise) if base else spread * noise
        out[name] = jnp.asarray(drawn.astype(out[name].dtype))
    for name, factor in factors.items():
        out[name] = (out[name] * factor).astype(out[name].dtype)
    return out
```

```python
import concourse.bass as bass
from concourse import mybir
from contextlib import ExitStack
import numpy as np

F32 = mybir.dt.float32
F32R = mybir.dt.float32r
I32 = mybir.dt.int32
ALU = mybir.AluOpType
ACT = mybir.ActivationFunctionType
AX = mybir.AxisListType

P = 128
B, T, D, H, E = 4, 2048, 256, 8, 4
DH = D // H
KD = D // P
NB = T // E
TB = NB // P
CUT = [0, 5000, 10000, 25000, 32000]
DE = [256, 64, 16, 4]
ECOL = [0, 256, 320, 336, 340]
TAIL = ECOL[4] - 256
EPS = 1e-5
QSCALE = float(2 * DH) ** -0.5
PAIRS = H // 2
NK = [2, 1, 1, 1]
MK = [[128, 128], [128], [64], [32]]
NKSUM = [0, 2, 3, 4, 5]


class Chain:

    def __init__(self, eng, sem, base=0):
        self.eng, self.sem, self.base, self.k = eng, sem, base, 0

    def link(self, ins):
        self.k += 1
        ins.then_inc(self.sem, 1)
        self.eng.wait_ge(self.sem, self.base + self.k)


def token_stage(nc, a, scr):
    ctx = ExitStack()
    with ctx:
        def sb(name, shape, dt=F32):
            return ctx.enter_context(nc.sbuf_tensor(name, shape, dt))

        sems = {}

        def sem(name):
            if name not in sems:
                sems[name] = ctx.enter_context(nc.semaphore("s1_" + name))
            return sems[name]

        bank = [ctx.enter_context(nc.psum_tensor(f"tb{i}", [P, 512], F32)) for i in range(8)]

        ident = sb("ident", [P, P])
        mask = sb("mask", [P, 4, P])
        tokens = sb("tokens", [P, B * T // P], I32)
        proj_t = sb("proj_t", [P, 3, D])
        wq_rows = sb("wq_rows", [P, KD, D])
        wk_rows = sb("wk_rows", [P, KD, D])
        fm_q = sb("fm_q", [P, 4, 2, DH])
        fm_k = sb("fm_k", [P, 4, 2, DH])
        wq_feat = sb("wq_feat", [P, KD, 2 * D])
        wk_feat = sb("wk_feat", [P, KD, 2 * D])
        bq_feat = sb("bq_feat", [P, 1])
        bk_feat = sb("bk_feat", [P, 1])
        wv_t = sb("wv_t", [P, KD, D])
        wo_t = sb("wo_t", [P, KD, D])
        wo_s = sb("wo_s", [P, KD, D])
        rms_col = sb("rms_col", [P, 1])
        fq_t = sb("fq_t", [P, KD, D])
        fk_t = sb("fk_t", [P, KD, D])
        fv_t = sb("fv_t", [P, KD, D])
        fq_b = sb("fq_b", [P, KD])
        fk_b = sb("fk_b", [P, KD])
        fv_b = sb("fv_b", [P, D])
        nw = sb("nw", [P, KD])
        nb = sb("nb", [P, KD])
        minus_half = sb("minus_half", [P, 4 * H])
        index = sb("index", [P, 4, B * T // P], I32)
        member = sb("member", [P, 4, B * T // P])
        lower = sb("lower", [P, B * T // P])
        idx_blk = sb("idx_blk", [P, 2, 4, TB], I32)
        emb = sb("emb", [P, 2, TB, ECOL[4]])
        emb_t = sb("emb_t", [P, 3, NB])
        h_sb = sb("h_sb", [P, 2, TB, D])
        stats = sb("stats", [P, TB, 6])
        both = sb("both", [P, 3, TB])
        mean = sb("mean", [P, TB])
        veps = sb("veps", [P, TB])
        rstd = sb("rstd", [P, TB])
        x1 = sb("x1", [P, TB, D])
        x1_t = sb("x1_t", [P, KD, NB])
        feat_q = sb("feat_q", [P, 2, PAIRS, NB])
        feat_k = sb("feat_k", [P, 2, PAIRS, NB])
        v_sb = sb("v_sb", [P, 2, TB, D])
        k_tok = sb("k_tok", [P, 2, 512])
        attn_t = sb("attn_t", [P, H, P])
        state = sb("state", [P, PAIRS, 2 * DH])
        o_sb = sb("o_sb", [P, TB, D])
        o_sq = sb("o_sq", [P, TB, D])
        ss = sb("ss", [P, TB * H])
        rrms = sb("rrms", [P, TB * H])
        o_n = sb("o_n", [P, TB, D])
        o_nt = sb("o_nt", [P, KD, NB])
        h1 = sb("h1", [P, TB, D])
        x2 = sb("x2", [P, TB, D])
        resid = sb("resid", [P, TB, D])
        xn = sb("xn", [P, TB, D])
        xn_t = sb("xn_t", [P, KD, NB])
        hi = sb("hi", [P, 4, NB], F32R)
        lo = sb("lo", [P, 4, NB], F32R)
        v2 = sb("v2", [P, TB, D])

        with nc.Block() as block:
            @block.sync
            def _(sp):
                def load(dst, src):
                    sp.dma_start(dst, src).then_inc(sem("loaded"), 16)
                n = 0
                rows = lambda w: w.rearrange("(k p) n -> p k n", p=P)
                sp.wait_ge(sem("zeroed"), 3)
                for dst, src in [(tokens[:, :], a["tokens"]),
                                 (proj_t[:, 0:2, :], rows(a["proj_0_t"])),
                                 (proj_t[0:64, 2, :], a["proj_1_t"]),
                                 (proj_t[64:80, 2, :], a["proj_2_t"]),
                                 (proj_t[80:84, 2, :], a["proj_3_t"]),
                                 (wq_rows[:, :, :], rows(a["Wq"])), (wk_rows[:, :, :], rows(a["Wk"])),
                                 (wv_t[:, :, :], rows(a["Wv_t"])), (wo_t[:, :, :], rows(a["Wo_t"])),
                                 (fq_t[:, :, :], rows(a["q_w_t"])), (fk_t[:, :, :], rows(a["k_w_t"])),
                                 (fv_t[:, :, :], rows(a["v_w_t"])),
                                 (fv_b[:, :], a["v_b"].rearrange("(a n) -> a n", a=1).broadcast_to([P, D]))]:
                    load(dst, src)
                    n += 1
                for dst, src in [(fq_b, "q_b"), (fk_b, "k_b"), (nw, "norm_w"), (nb, "norm_b")]:
                    for k in range(KD):
                        load(dst[:, k:k + 1], a[src][k * P:(k + 1) * P].rearrange("(p a) -> p a", a=1))
                        n += 1
                for j in range(4):
                    rows32 = slice(DH * j, DH * j + DH)
                    load(rms_col[rows32, :], a["rms_w"].rearrange("(p a) -> p a", a=1))
                    load(bq_feat[rows32, :], a["fmq_b"].rearrange("(p a) -> p a", a=1))
                    load(bk_feat[rows32, :], a["fmk_b"].rearrange("(p a) -> p a", a=1))
                    n += 3
                assert n == 33
                for j in range(4):
                    rows32 = slice(DH * j, DH * j + DH)
                    sp.dma_start(fm_q[rows32, j, 0, :], a["fmq_w_t"]).then_inc(sem("fm_loaded"), 16)
                    sp.dma_start(fm_k[rows32, j, 0, :], a["fmk_w_t"]).then_inc(sem("fm_loaded"), 16)

            @block.gpsimd
            def _(pool):
                pool.memset(ident[:, :], 0.0).then_inc(sem("const"), 1)
                pool.memset(mask[:, :, :], 1.0).then_inc(sem("const"), 1)
                pool.memset(minus_half[:, :], -0.5)
                pool.wait_ge(sem("const"), 2)
                pool.affine_select(out=ident[:, :], in_=ident[:, :], compare_op=ALU.not_equal, fill=1.0,
                                   base=0, pattern=[[-1, P]], channel_multiplier=1).then_inc(sem("const"), 1)
                pool.affine_select(out=mask[:, :, :], in_=mask[:, :, :], compare_op=ALU.is_ge, fill=0.0,
                                   base=0, pattern=[[0, 4], [1, P]], channel_multiplier=-1)\
                    .then_inc(sem("const"), 1)

            @block.vector
            def _(dve):
                dve.memset(fm_q[:, :, :, :], 0.0).then_inc(sem("zeroed"), 1)
                dve.memset(fm_k[:, :, :, :], 0.0).then_inc(sem("zeroed"), 1)
                dve.memset(state[:, :, :], 0.0).then_inc(sem("zeroed"), 1)
                dve.wait_ge(sem("loaded"), 33 * 16)
                dve.wait_ge(sem("fm_loaded"), 8 * 16)
                c = Chain(dve, sem("setup_dve"))
                for fm in (fm_q, fm_k):
                    c.link(dve.tensor_scalar(fm[:, :, 1, :], fm[:, :, 0, :], -1.0, None, ALU.mult))
                for b in (bq_feat, bk_feat):
                    for r in (DH, 3 * DH):
                        c.link(dve.tensor_scalar(b[r:r + DH, :], b[r:r + DH, :], -1.0, None, ALU.mult))
                for k in range(KD):
                    c.link(dve.tensor_scalar(wo_s[:, k, :], wo_t[:, k, :], rms_col[:, 0:1], QSCALE,
                                             ALU.mult, ALU.mult))
                for i in range(4):
                    c.link(dve.tensor_scalar(lower[:, :], tokens[:, :], float(CUT[i]), 0.0,
                                             ALU.subtract, ALU.max))
                    c.link(dve.tensor_scalar(index[:, i, :], lower[:, :], float(CUT[i + 1] - CUT[i] - 1), None,
                                             ALU.min))
                    c.link(dve.tensor_scalar(lower[:, :], tokens[:, :], float(CUT[i]), None, ALU.is_ge))
                    c.link(dve.tensor_scalar(member[:, i, :], tokens[:, :], float(CUT[i + 1]), None, ALU.is_lt))
                    c.link(dve.tensor_tensor(member[:, i, :], member[:, i, :], lower[:, :], ALU.mult))
                for k in range(KD):
                    dve.wait_ge(sem("feat_w"), k + 1)
                    dve.tensor_copy(wq_feat[:, k, :], bank[2 * k][:, :])
                    dve.tensor_copy(wk_feat[:, k, :], bank[2 * k + 1][:, :])

            @block.tensor
            def _(pe):
                pe.wait_ge(sem("setup_dve"), 2)
                for k in range(KD):
                    for j in range(KD):
                        pe.matmul(bank[2 * k][:, j * 256:j * 256 + 256], wq_rows[:, j, k * P:k * P + P],
                                  fm_q[:, :, :, :].rearrange("p a b c -> p (a b c)"), start=True, stop=True)
                        last = pe.matmul(bank[2 * k + 1][:, j * 256:j * 256 + 256],
                                         wk_rows[:, j, k * P:k * P + P],
                                         fm_k[:, :, :, :].rearrange("p a b c -> p (a b c)"),
                                         start=True, stop=True)
                    last.then_inc(sem("feat_w"), 1)

        LINKS = 64
        with nc.Block() as block:
            @block.gpsimd
            def _(pool):
                tables = [a[f"emb_{i}"] for i in range(4)]

                def gather(f, par, tiles):
                    for tile in tiles:
                        for i in range(4):
                            pool.indirect_dma_start(
                                emb[:, par, tile, ECOL[i]:ECOL[i + 1]], None, tables[i],
                                bass.IndirectOffsetOnAxis(ap=idx_blk[:, par, i, tile:tile + 1], axis=0),
                            ).then_inc(sem(f"gathered{par}"), 16)

                def power(k, width, dst, count):
                    pool.wait_ge(sem("var_ready"), count)
                    pool.tensor_tensor(dst, k, minus_half[:, 0:width], ALU.pow).then_inc(sem("rstd_ready"), 1)

                pool.wait_ge(sem("indexed"), 2)
                gather(0, 0, range(TB))
                gather(1, 1, range(TB))
                power(veps[:, :], TB, rstd[:, :], 1)

                def body(t, last):
                    for e in range(E):
                        n = 4 * t + e
                        fwd = not (last and e == E - 1)
                        fwd2 = not (last and e >= E - 2)
                        if fwd:
                            power(veps[:, :], TB, rstd[:, :], 4 * n + 2)
                        if fwd2:
                            gather(n + 2, e % 2, (0, 1))
                        c = 1 if fwd else 0
                        power(ss[:, :], TB * H, rrms[:, :], 4 * n + 2 + c)
                        if fwd2:
                            gather(n + 2, e % 2, (2, 3))
                        power(veps[:, :], TB, rstd[:, :], 4 * n + 3 + c)
                        power(veps[:, :], TB, rstd[:, :], 4 * n + 4 + c)
                with pool.Fori(0, B - 1) as t:
                    body(t, False)
                body(B - 1, True)

            @block.sync
            def _(sp):
                def body(t):
                    for e in range(E):
                        n = 4 * t + e
                        sp.wait_ge(sem("resid_ready"), n + 1)
                        sp.dma_start(scr["resid"][bass.ds(n, 1)].rearrange("a p t d -> (a p) t d"),
                                     resid[:, :, :]).then_inc(sem("resid_stored"), 16)
                        for j in range(4):
                            sp.wait_ge(sem("hi_ready"), 4 * n + j + 1)
                            sp.dma_start(scr["hi"][bass.ds(4 * t + 2 * (j % 2) + j // 2, 1), :, e * NB:e * NB + NB]
                                         .rearrange("a p c -> (a p) c"), hi[:, j, :].bitcast(F32))\
                                .then_inc(sem("hi_stored"), 16)
                            sp.wait_ge(sem("lo_ready"), 4 * n + j + 1)
                            sp.dma_start(scr["lo"][bass.ds(4 * t + 2 * (j % 2) + j // 2, 1), :, e * NB:e * NB + NB]
                                         .rearrange("a p c -> (a p) c"), lo[:, j, :].bitcast(F32))\
                                .then_inc(sem("lo_stored"), 16)
                        sp.wait_ge(sem("v2_ready"), n + 1)
                        for k in range(KD):
                            sp.dma_start(scr["v"][bass.ds(8 * t + 4 * k + e, 1)].rearrange("a p t d -> (a p) t d"),
                                         v2[:, :, k * P:k * P + P]).then_inc(sem("v2_stored"), 16)
                with sp.Fori(0, B - 1) as t:
                    body(t)
                body(B - 1)
                sp.wait_ge(sem("resid_stored"), 16 * 4 * B)
                sp.wait_ge(sem("hi_stored"), 64 * 4 * B)
                sp.wait_ge(sem("lo_stored"), 64 * 4 * B)
                sp.wait_ge(sem("v2_stored"), 32 * 4 * B)

            @block.tensor
            def _(pe):
                def front_a(f, par, first):
                    pe.wait_ge(sem("masked"), f + 1)
                    if not first:
                        pe.wait_ge(sem("exp_done"), 8 * f)
                        pe.wait_ge(sem("v_ready"), f)
                    for k in range(3):
                        w = P if k < 2 else TAIL
                        for tile in range(TB):
                            mm = pe.transpose(bank[k][0:w, tile * P:tile * P + P],
                                              emb[:, par, tile, k * P:k * P + w], ident[:, :])
                        mm.then_inc(sem("emb_t_done"), 1)

                def front_b(f):
                    pe.wait_ge(sem("emb_t_act"), f + 1)
                    pe.wait_ge(sem("emb_t_dve"), f + 1)
                    for tile in range(TB):
                        out = bank[tile // 2][:, (tile % 2) * D:(tile % 2) * D + D]
                        for k in range(3):
                            w = P if k < 2 else TAIL
                            mm = pe.matmul(out, emb_t[0:w, k, tile * P:tile * P + P], proj_t[0:w, k, :],
                                           start=(k == 0), stop=(k == 2))
                        if tile % 2:
                            mm.then_inc(sem("h_done"), 1)

                def front_c(f):
                    pe.wait_ge(sem("x1_ready"), f + 1)
                    for k in range(KD):
                        for tile in range(TB):
                            mm = pe.transpose(bank[k][:, tile * P:tile * P + P], x1[:, tile, k * P:k * P + P],
                                              ident[:, :])
                        mm.then_inc(sem("x1_t_done"), 1)

                def front_d(f, first):
                    pe.wait_ge(sem("x1_t_act"), f + 1)
                    pe.wait_ge(sem("x1_t_dve"), f + 1)
                    for j in range(2 * PAIRS):
                        if j >= 3:
                            pe.wait_ge(sem("exp_done"), 8 * f + j - 2)
                        w = wq_feat if j < PAIRS else wk_feat
                        pair = j % PAIRS
                        for k in range(KD):
                            mm = pe.matmul(bank[j % 3][:, :], w[:, k, pair * P:pair * P + P], x1_t[:, k, :],
                                           start=(k == 0), stop=(k == KD - 1))
                        mm.then_inc(sem("y_done"), 1)
                    for half in range(2):
                        pe.wait_ge(sem("exp_done"), 8 * f + 6 + half)
                        for tile in (2 * half, 2 * half + 1):
                            out = bank[(8 + half) % 3][:, (tile % 2) * D:(tile % 2) * D + D]
                            for k in range(KD):
                                mm = pe.matmul(out, x1_t[:, k, tile * P:tile * P + P], wv_t[:, k, :],
                                               start=(k == 0), stop=(k == KD - 1))
                        mm.then_inc(sem("v_done"), 1)

                def chunk_scores(n, e, c, first):
                    par = e % 2
                    if c == 0:
                        pe.wait_ge(sem("exp_done"), 8 * n + 8)
                        pe.wait_ge(sem("v_ready"), n + 1)
                        if not first:
                            pe.wait_ge(sem("lo_ready"), 4 * n)
                            pe.wait_ge(sem("v2_ready"), n)
                    else:
                        pe.wait_ge(sem("k_tok_ready"), 4 * n + c)
                        pe.wait_ge(sem("attn_ready"), 8 * n + 2 * c)
                    cols = slice(c * P, c * P + P)
                    for pair in range(PAIRS):
                        mm = pe.transpose(bank[3][:, pair * P:pair * P + P], feat_k[:, par, pair, cols],
                                          ident[:, :])
                    mm.then_inc(sem("k_tok_done"), 1)
                    for h in range(H):
                        r = slice(64 * (h % 2), 64 * (h % 2) + 64)
                        mm = pe.matmul(bank[4 + h % 2][:, (h // 2) * P:(h // 2) * P + P],
                                       feat_k[r, par, h // 2, cols], feat_q[r, par, h // 2, cols],
                                       start=True, stop=True)
                        if h >= H - 2:
                            mm.then_inc(sem("attn_done"), 1)

                def chunk_outputs(n, t, e, c):
                    par = e % 2
                    pe.wait_ge(sem("attn_ready"), 8 * n + 2 * c + 2)
                    pe.wait_ge(sem("k_tok_ready"), 4 * n + c + 1)
                    pe.wait_ge(sem("state_ready"), 17 * t + 4 * e + c + 1)
                    if c:
                        pe.wait_ge(sem("o_ready"), 4 * n + c)
                    for pair in range(PAIRS):
                        out = bank[6][:, pair * 64:pair * 64 + 64]
                        pe.matmul(out, feat_q[:, par, pair, c * P:c * P + P], state[:, pair, :],
                                  start=True, stop=False)
                        for h in (2 * pair, 2 * pair + 1):
                            mm = pe.matmul(bank[6][:, h * DH:h * DH + DH], attn_t[:, (h % 2) * 4 + h // 2, :],
                                           v_sb[:, par, c, h * DH:h * DH + DH],
                                           start=False, stop=(h == 2 * pair + 1))
                    mm.then_inc(sem("o_done"), 1)
                    for pair in range(PAIRS):
                        mm = pe.matmul(bank[7][:, pair * 64:pair * 64 + 64],
                                       k_tok[:, c % 2, pair * P:pair * P + P],
                                       v_sb[:, par, c, pair * 64:pair * 64 + 64], start=True, stop=True)
                    mm.then_inc(sem("state_done"), 1)

                def back_f(n):
                    pe.wait_ge(sem("o_n_ready"), n + 1)
                    for k in range(KD):
                        for tile in range(TB):
                            mm = pe.transpose(bank[4 + k][:, tile * P:tile * P + P],
                                              o_n[:, tile, k * P:k * P + P], ident[:, :])
                        mm.then_inc(sem("o_nt_done"), 1)

                def back_g(n, t, e):
                    pe.wait_ge(sem("o_nt_act"), n + 1)
                    pe.wait_ge(sem("o_nt_dve"), n + 1)
                    pe.wait_ge(sem("o_ready"), 4 * n + 4)
                    pe.wait_ge(sem("state_ready"), 17 * t + 4 * e + 5)
                    for tile in range(TB):
                        out = bank[6 + tile // 2][:, (tile % 2) * D:(tile % 2) * D + D]
                        for k in range(KD):
                            mm = pe.matmul(out, o_nt[:, k, tile * P:tile * P + P], wo_s[:, k, :],
                                           start=(k == 0), stop=(k == KD - 1))
                        if tile % 2:
                            mm.then_inc(sem("attn_out_done"), 1)

                def back_h(n, e):
                    pe.wait_ge(sem("xn_ready"), n + 1)
                    for k in range(NK[e]):
                        for tile in range(TB):
                            mm = pe.transpose(bank[4 + k][:, tile * P:tile * P + P],
                                              xn[:, tile, k * P:k * P + P], ident[:, :])
                        mm.then_inc(sem("xn_t_done"), 1)

                def back_i(n, t, e):
                    pe.wait_ge(sem("xn_t_ready"), 5 * t + NKSUM[e + 1])
                    for j, bk in enumerate((3, 5, 6, 7)):
                        w = fq_t if j < 2 else fk_t
                        for k, m in enumerate(MK[e]):
                            mm = pe.matmul(bank[bk][:, :], w[0:m, k, (j % 2) * P:(j % 2) * P + P],
                                           xn_t[0:m, k, :], start=(k == 0), stop=(k == NK[e] - 1))
                        mm.then_inc(sem("qk_done"), 1)
                    for half, bk in enumerate((4, 3)):
                        if half:
                            pe.wait_ge(sem("lo_ready"), 4 * n + 1)
                        for tile in (2 * half, 2 * half + 1):
                            out = bank[bk][:, (tile % 2) * D:(tile % 2) * D + D]
                            for k, m in enumerate(MK[e]):
                                mm = pe.matmul(out, xn_t[0:m, k, tile * P:tile * P + P], fv_t[0:m, k, :],
                                               start=(k == 0), stop=(k == NK[e] - 1))
                        mm.then_inc(sem("v2_done"), 1)

                front_a(0, 0, True)
                front_b(0)
                front_c(0)
                front_d(0, True)

                def body(t, last):
                    for e in range(E):
                        n = 4 * t + e
                        fwd = not (last and e == E - 1)
                        chunk_scores(n, e, 0, e == 0)
                        if fwd:
                            front_a(n + 1, (e + 1) % 2, False)
                        chunk_outputs(n, t, e, 0)
                        chunk_scores(n, e, 1, False)
                        if fwd:
                            front_b(n + 1)
                        chunk_outputs(n, t, e, 1)
                        chunk_scores(n, e, 2, False)
                        chunk_outputs(n, t, e, 2)
                        chunk_scores(n, e, 3, False)
                        if fwd:
                            front_c(n + 1)
                        chunk_outputs(n, t, e, 3)
                        back_f(n)
                        back_g(n, t, e)
                        if fwd:
                            front_d(n + 1, False)
                        back_h(n, e)
                        back_i(n, t, e)
                    pe.wait_ge(sem("lo_ready"), 16 * t + 16)
                    pe.wait_ge(sem("v2_ready"), 4 * t + 4)
                with pe.Fori(0, B - 1) as t:
                    body(t, False)
                body(B - 1, True)

            @block.scalar
            def _(act):
                def front_a(f):
                    act.wait_ge(sem("emb_t_done"), 3 * f + 1)
                    act.copy(emb_t[:, 0, :], bank[0][:, :])
                    act.wait_ge(sem("emb_t_done"), 3 * f + 2)
                    act.copy(emb_t[:, 1, :], bank[1][:, :]).then_inc(sem("emb_t_act"), 1)

                def front_b(f, par):
                    for half in range(2):
                        act.wait_ge(sem("h_done"), 2 * f + half + 1)
                        act.mul(h_sb[:, par, 2 * half:2 * half + 2, :].rearrange("p a b -> p (a b)"),
                                bank[half][:, :], float(D) ** 0.5).then_inc(sem("h_ready"), 1)

                def front_c(f):
                    act.wait_ge(sem("x1_t_done"), 2 * f + 1)
                    act.copy(x1_t[:, 0, :], bank[0][:, :]).then_inc(sem("x1_t_act"), 1)

                def front_d(f, par):
                    for j in range(2 * PAIRS):
                        act.wait_ge(sem("y_done"), 8 * f + j + 1)
                        feat, b = (feat_q, bq_feat) if j < PAIRS else (feat_k, bk_feat)
                        act.activation(feat[:, par, j % PAIRS, :], bank[j % 3][:, :], ACT.Exp,
                                       bias=b[:, 0:1]).then_inc(sem("exp_done"), 1)

                def keys(n, c):
                    act.wait_ge(sem("k_tok_done"), 4 * n + c + 1)
                    act.copy(k_tok[:, c % 2, :], bank[3][:, :]).then_inc(sem("k_tok_ready"), 1)

                def outputs(n, c):
                    act.wait_ge(sem("o_done"), 4 * n + c + 1)
                    act.copy(o_sb[:, c, :], bank[6][:, 0:D]).then_inc(sem("o_ready"), 1)

                def back_f(n):
                    act.wait_ge(sem("o_nt_done"), 2 * n + 1)
                    act.copy(o_nt[:, 0, :], bank[4][:, :]).then_inc(sem("o_nt_act"), 1)

                def back_h(n, t, e):
                    for k, m in enumerate(MK[e]):
                        act.wait_ge(sem("xn_t_done"), 5 * t + NKSUM[e] + k + 1)
                        act.activation(xn_t[0:m, k, :], bank[4 + k][0:m, :], ACT.Identity,
                                       scale=nw[0:m, k:k + 1], bias=nb[0:m, k:k + 1])\
                            .then_inc(sem("xn_t_ready"), 1)

                def back_i(n):
                    for j, bk in enumerate((3, 5, 6, 7)):
                        act.wait_ge(sem("qk_done"), 4 * n + j + 1)
                        b = fq_b if j < 2 else fk_b
                        act.activation(hi[:, j, :], bank[bk][:, :], ACT.Identity,
                                       bias=b[:, j % 2:j % 2 + 1]).then_inc(sem("hi_ready"), 1)

                front_a(0)
                front_b(0, 0)
                front_c(0)
                front_d(0, 0)

                def body(t, last):
                    for e in range(E):
                        n = 4 * t + e
                        par = (e + 1) % 2
                        fwd = not (last and e == E - 1)
                        keys(n, 0)
                        if fwd:
                            front_a(n + 1)
                        outputs(n, 0)
                        keys(n, 1)
                        if fwd:
                            front_b(n + 1, par)
                        outputs(n, 1)
                        keys(n, 2)
                        outputs(n, 2)
                        keys(n, 3)
                        if fwd:
                            front_c(n + 1)
                        outputs(n, 3)
                        back_f(n)
                        if fwd:
                            front_d(n + 1, par)
                        back_h(n, t, e)
                        back_i(n)
                        act.wait_ge(sem("hi_stored"), 64 * (n + 1))
                with act.Fori(0, B - 1) as t:
                    body(t, False)
                body(B - 1, True)

            @block.vector
            def _(dve):
                def layernorm(c, out, src, count):
                    for tile in range(TB):
                        ins = dve.bn_stats(stats[:, tile, :], src[:, tile, :])
                    c.link(ins)
                    dve.tensor_tensor(both[:, 0, :], stats[:, :, 1], stats[:, :, 4], ALU.add)
                    dve.tensor_tensor(both[:, 1, :], stats[:, :, 1], stats[:, :, 4], ALU.subtract)
                    c.link(dve.tensor_tensor(both[:, 2, :], stats[:, :, 2], stats[:, :, 5], ALU.add))
                    dve.tensor_scalar(mean[:, :], both[:, 0, :], 0.5, None, ALU.mult)
                    dve.tensor_scalar(both[:, 2, :], both[:, 2, :], 1.0 / D, EPS, ALU.mult, ALU.add)
                    c.link(dve.tensor_tensor(both[:, 1, :], both[:, 1, :], both[:, 1, :], ALU.mult))
                    dve.scalar_tensor_tensor(veps[:, :], both[:, 1, :], 0.25, both[:, 2, :],
                                             ALU.mult, ALU.add).then_inc(sem("var_ready"), 1)
                    dve.wait_ge(sem("rstd_ready"), count)
                    for tile in range(TB):
                        ins = dve.tensor_scalar(out[:, tile, :], src[:, tile, :], mean[:, tile:tile + 1],
                                                rstd[:, tile:tile + 1], ALU.subtract, ALU.mult)
                    return ins

                def index_block(f, par):
                    dve.tensor_copy(idx_blk[:, par, :, :], index[:, :, bass.ds(4 * f, 4)])\
                        .then_inc(sem("indexed"), 1)

                def front_a(f, par, count):
                    dve.wait_ge(sem(f"gathered{par}"), 256 * count)
                    for i in range(4):
                        out = emb[:, par, :, ECOL[i]:ECOL[i + 1]]
                        m = member[:, i, bass.ds(4 * f, 4)].unsqueeze(2).broadcast_to([P, TB, DE[i]])
                        ins = dve.tensor_tensor(out, out, m, ALU.mult)
                    ins.then_inc(sem("masked"), 1)

                def front_a2(f):
                    dve.wait_ge(sem("emb_t_done"), 3 * f + 3)
                    dve.tensor_copy(emb_t[0:TAIL, 2, :], bank[2][0:TAIL, :]).then_inc(sem("emb_t_dve"), 1)

                def front_b(c, f, par, count):
                    dve.wait_ge(sem("h_ready"), 2 * f + 2)
                    layernorm(c, x1, h_sb[:, par], count).then_inc(sem("x1_ready"), 1)

                def front_c(f):
                    dve.wait_ge(sem("x1_t_done"), 2 * f + 2)
                    dve.tensor_copy(x1_t[:, 1, :], bank[1][:, :]).then_inc(sem("x1_t_dve"), 1)

                def front_d(f, par):
                    for half in range(2):
                        dve.wait_ge(sem("v_done"), 2 * f + half + 1)
                        ins = dve.tensor_copy(v_sb[:, par, 2 * half:2 * half + 2, :]
                                              .rearrange("p a b -> p (a b)"), bank[(8 + half) % 3][:, :])
                    ins.then_inc(sem("v_ready"), 1)

                def scores(n, e, c):
                    for g in range(2):
                        dve.wait_ge(sem("attn_done"), 8 * n + 2 * c + g + 1)
                        dve.tensor_tensor(attn_t[:, 4 * g:4 * g + 4, :],
                                          bank[4 + g][:, :].rearrange("p (h c) -> p h c", h=4),
                                          mask[:, :, :], ALU.mult).then_inc(sem("attn_ready"), 1)

                def new_state(n, e, c):
                    dve.wait_ge(sem("state_done"), 4 * n + c + 1)
                    ps = bank[7][:, 0:D].rearrange("p (a b) -> p a b", a=PAIRS)
                    dve.tensor_tensor(state[0:64, :, 0:DH], state[0:64, :, 0:DH], ps[0:64, :, 0:DH], ALU.add)
                    dve.tensor_tensor(state[64:128, :, DH:64], state[64:128, :, DH:64],
                                      ps[64:128, :, DH:64], ALU.add).then_inc(sem("state_ready"), 1)

                def squares(chain, n, c):
                    dve.wait_ge(sem("o_ready"), 4 * n + c + 1)
                    chain.link(dve.tensor_tensor(o_sq[:, c, :], o_sb[:, c, :], o_sb[:, c, :], ALU.mult))
                    return dve.tensor_reduce(ss[:, c * H:c * H + H],
                                             o_sq[:, c, :].rearrange("p (h d) -> p h d", h=H), AX.X, ALU.add)

                def rms(chain, n, count):
                    dve.tensor_scalar(ss[:, :], ss[:, :], QSCALE * QSCALE / DH, EPS, ALU.mult, ALU.add)\
                        .then_inc(sem("var_ready"), 1)
                    dve.wait_ge(sem("rstd_ready"), count)
                    dve.tensor_tensor(o_n[:, :, :].rearrange("p t (h d) -> p (t h) d", h=H),
                                      o_sb[:, :, :].rearrange("p t (h d) -> p (t h) d", h=H),
                                      rrms[:, :].unsqueeze(2).broadcast_to([P, TB * H, DH]), ALU.mult)\
                        .then_inc(sem("o_n_ready"), 1)

                def back_f(n):
                    dve.wait_ge(sem("o_nt_done"), 2 * n + 2)
                    dve.tensor_copy(o_nt[:, 1, :], bank[5][:, :]).then_inc(sem("o_nt_dve"), 1)

                def back_g(chain, n, par, count):
                    for half in range(2):
                        dve.wait_ge(sem("attn_out_done"), 2 * n + half + 1)
                        ins = dve.tensor_tensor(h1[:, 2 * half:2 * half + 2, :]
                                                .rearrange("p a b -> p (a b)"), bank[6 + half][:, :],
                                                h_sb[:, par, 2 * half:2 * half + 2, :]
                                                .rearrange("p a b -> p (a b)"), ALU.add)
                    chain.link(ins)
                    chain.link(layernorm(chain, x2, h1, count))
                    dve.tensor_tensor(resid[:, :, :], h1[:, :, :], x2[:, :, :], ALU.add)\
                        .then_inc(sem("resid_ready"), 1)
                    layernorm(chain, xn, x2, count + 1).then_inc(sem("xn_ready"), 1)

                def back_i(n):
                    for j, bk in enumerate((3, 5, 6, 7)):
                        dve.wait_ge(sem("hi_ready"), 4 * n + j + 1)
                        b = fq_b if j < 2 else fk_b
                        dve.scalar_tensor_tensor(lo[:, j, :], bank[bk][:, :], b[:, j % 2:j % 2 + 1],
                                                 hi[:, j, :].bitcast(F32), ALU.add, ALU.subtract)\
                            .then_inc(sem("lo_ready"), 1)
                    for half, bk in enumerate((4, 3)):
                        dve.wait_ge(sem("v2_done"), 2 * n + half + 1)
                        ins = dve.tensor_tensor(v2[:, 2 * half:2 * half + 2, :],
                                                bank[bk][:, :].rearrange("p (a b) -> p a b", a=2),
                                                fv_b[:, :].unsqueeze(1).broadcast_to([P, 2, D]), ALU.add)
                    ins.then_inc(sem("v2_ready"), 1)

                chain = Chain(dve, sem("dve_order"))
                index_block(0, 0)
                index_block(1, 1)
                front_a(0, 0, 1)
                front_a2(0)
                front_b(chain, 0, 0, 1)
                front_c(0)
                front_d(0, 0)
                base = chain.k

                def body(t, last):
                    chain = Chain(dve, sem("dve_order"), base + LINKS * t)
                    for e in range(E):
                        n = 4 * t + e
                        par = (e + 1) % 2
                        fwd = not (last and e == E - 1)
                        c1 = 1 if fwd else 0
                        if not (last and e >= E - 2):
                            index_block(n + 2, e % 2)
                        if e == 0:
                            dve.wait_ge(sem("attn_done"), 8 * n + 1)
                            dve.memset(state[:, :, :], 0.0).then_inc(sem("state_ready"), 1)
                            dve.wait_ge(sem("state_ready"), 17 * t + 1)
                        scores(n, e, 0)
                        if fwd:
                            front_a(n + 1, par, 2 * t + (e + 1) // 2 + 1)
                            front_a2(n + 1)
                        new_state(n, e, 0)
                        squares(chain, n, 0)
                        scores(n, e, 1)
                        if fwd:
                            front_b(chain, n + 1, par, 4 * n + 2)
                        new_state(n, e, 1)
                        squares(chain, n, 1)
                        scores(n, e, 2)
                        new_state(n, e, 2)
                        squares(chain, n, 2)
                        scores(n, e, 3)
                        if fwd:
                            front_c(n + 1)
                        new_state(n, e, 3)
                        chain.link(squares(chain, n, 3))
                        rms(chain, n, 4 * n + 2 + c1)
                        back_f(n)
                        back_g(chain, n, e % 2, 4 * n + 3 + c1)
                        if fwd:
                            front_d(n + 1, par)
                        back_i(n)
                        dve.wait_ge(sem("resid_stored"), 16 * (n + 1))
                        dve.wait_ge(sem("lo_stored"), 64 * (n + 1))
                        dve.wait_ge(sem("v2_stored"), 32 * (n + 1))
                    if not last:
                        assert chain.k == LINKS, chain.k
                with dve.Fori(0, B - 1) as t:
                    body(t, False)
                body(B - 1, True)




def attention_stage(nc, a, scr):
    KT = T // P
    QB = T // 512
    SCALE = float(D) ** -0.5
    RING = 8
    BY_PE = [5, 7, 10, 12, 14, 15]
    BY_POOL = [k for k in range(KT) if k not in BY_PE]
    NADD = len(BY_POOL) - 1
    HEADS = B * H
    U = 4
    NMAX = KT * QB
    MAX_TILES = 14
    ROWS = 3 * DH
    NEG = ROWS + 2

    max_end = [min(NMAX, -(-NMAX * (kt + 1) // MAX_TILES)) for kt in range(KT)]
    seq, seq_last = [], []
    for kt in range(KT):
        for j in range(QB):
            seq.append(("scores", kt, j))
            seq_last.append(("scores", kt, j))
        for r in range(QB):
            if kt == next(k for k in range(KT) if max_end[k] >= KT * (r + 1)) + 1:
                seq.append(("maxima", r))
    NU = len(seq)
    assert NU == KT * QB + QB

    def last_in_bank(i):
        return max(p for p in range(NU) if p % 3 == i % 3)

    ctx = ExitStack()
    with ctx:
        def sb(name, shape, dt=F32):
            return ctx.enter_context(nc.sbuf_tensor(name, shape, dt))

        sems = {}

        def sem(name):
            if name not in sems:
                sems[name] = ctx.enter_context(nc.semaphore("s2_" + name))
            return sems[name]

        bank = [ctx.enter_context(nc.psum_tensor(f"ab{i}", [P, 512], F32)) for i in range(8)]
        max_bank, score_bank, out_bank, sum_bank = bank[0:3], bank[3:6], bank[6], bank[7]
        qs = [sb(f"qs{i}", [P, T], F32R) for i in range(U)]
        ks = [sb(f"ks{i}", [P, T], F32R) for i in range(U)]
        vs = [sb(f"vs{i}", [P, KT, DH]) for i in range(U)]
        probs = sb("probs", [P, RING, T])
        prob_sum = sb("prob_sum", [P, 2, T])
        ones = sb("ones", [P, DH])
        ident2 = sb("ident2", [P, P])
        one_rows = sb("one_rows", [2, T])
        part_max = sb("part_max", [P, 2, KT, QB])
        neg_max = sb("neg_max", [P, 2, KT])
        neg = sb("neg", [P, 2, KT, 2], F32R)
        o_raw = sb("o_raw", [P, 512])
        inv_sum = sb("inv_sum", [P, 512])
        o_out = sb("o_out", [P, 512])

        with nc.Block() as block:
            @block.vector
            def _(dve):
                dve.memset(ones[:, :], 1.0)
                dve.memset(one_rows[:, :], 1.0).then_inc(sem("one_rows"), 1)
                dve.wait_ge(sem("one_rows"), 1)
                for u in range(U):
                    dve.tensor_copy(ks[u][ROWS:NEG, :], one_rows[:, :])

            @block.gpsimd
            def _(pool):
                pool.memset(ident2[:, :], 0.0).then_inc(sem("zero"), 1)
                pool.wait_ge(sem("zero"), 1)
                pool.affine_select(out=ident2[:, :], in_=ident2[:, :], compare_op=ALU.not_equal, fill=1.0,
                                   base=0, pattern=[[-1, P]], channel_multiplier=1)

        def turns(run):
            def all_turns(eng):
                run(0, 0, 0, False)
                with eng.Fori(0, (HEADS - U) // U) as t:
                    for u in range(1, U + 1):
                        run(4 * t + u, t, u, False)
                for u in range(1, U):
                    t = HEADS // U - 1
                    run(4 * t + u, t, u, u == U - 1)
            return all_turns

        with nc.Block() as block:
            @block.sync
            def _(sp):
                def load(t, u):
                    cols = slice(DH * u, DH * u + DH)
                    for dst, part, kind in ((qs[u][0:32, :], "hi", 0), (qs[u][32:64, :], "hi", 0),
                                            (qs[u][64:96, :], "lo", 0), (ks[u][0:32, :], "hi", 1),
                                            (ks[u][32:64, :], "lo", 1), (ks[u][64:96, :], "hi", 1)):
                        sp.dma_start(dst.bitcast(F32), scr[part][bass.ds(2 * t + kind, 1), cols, :]
                                     .rearrange("a p c -> (a p) c")).then_inc(sem(f"qk_loaded{u}"), 16)
                    for e in range(E):
                        sp.dma_start(vs[u][:, TB * e:TB * e + TB, :],
                                     scr["v"][bass.ds(4 * t + e, 1), :, :, cols]
                                     .rearrange("a p t d -> (a p) t d")).then_inc(sem(f"v_loaded{u}"), 16)

                def store(g, t, u):
                    sp.wait_ge(sem("out_ready"), g + 1)
                    for j in range(QB):
                        sp.dma_start(scr["attn"][bass.ds(4 * t + j, 1), DH * u:DH * u + DH, :]
                                     .rearrange("a d q -> (a d) q"), o_out[DH * j:DH * j + DH, :])\
                            .then_inc(sem("out_stored"), 16)

                def turn(g, t, u, last):
                    if isinstance(g, int) and g == 0:
                        return
                    if not (isinstance(t, int) and t == HEADS // U - 1):
                        sp.wait_ge(sem("pv_done"), KT * g)
                        load(t + 1, u - 1)
                    store(g - 1, t, u - 1)

                for u in range(U):
                    load(0, u)
                turns(turn)(sp)
                store(HEADS - 1, HEADS // U - 1, U - 1)
                sp.wait_ge(sem("out_stored"), 16 * QB * HEADS)

            @block.tensor
            def _(pe):
                def max_unit(g, u, i, first):
                    if i >= 3:
                        pe.wait_ge(sem("max_reduced"), NMAX * g + i - 2)
                    elif not first:
                        p = max(p for p in range(NMAX) if p % 3 == i)
                        pe.wait_ge(sem("max_reduced"), NMAX * (g - 1) + p + 1)
                    qt, j = i // QB, i % QB
                    pe.matmul(max_bank[i % 3][:, :], qs[u][0:ROWS, qt * P:qt * P + P],
                              ks[u][0:ROWS, j * 512:j * 512 + 512], start=True, stop=True)\
                        .then_inc(sem("max_done"), 1)

                def maxima(g, r, out):
                    pe.wait_ge(sem("neg_ready"), QB * g + r + 1)
                    for q in range(4):
                        mm = pe.transpose(out[0:2, q * P:q * P + P],
                                          neg[:, r % 2, 4 * r + q, :].bitcast(F32), ident2[:, :])
                    mm.then_inc(sem("unit_done"), 1)

                def total(g, par):
                    pe.wait_ge(sem("pool_added"), NADD * (g + 1))
                    for j in range(QB):
                        mm = pe.matmul(sum_bank[DH * j:DH * j + DH, :], ones[:, :],
                                       prob_sum[:, par, j * 512:j * 512 + 512], start=False, stop=True)
                    mm.then_inc(sem("sum_done"), 1)

                def sem_base(g):
                    return QB + NU * g

                def turn(g, t, u, last):
                    first = isinstance(g, int) and g == 0
                    order = seq_last if last else seq
                    made = 0
                    if not last:
                        pe.wait_ge(sem(f"qk_loaded{(u + 1) % U}"), 96 * (t + (u + 1) // U + 1))
                    pe.wait_ge(sem("unit_emptied"), sem_base(g))
                    for i, unit in enumerate(order):
                        out = score_bank[i % 3]
                        if unit[0] == "scores":
                            kt, j = unit[1], unit[2]
                            if not last:
                                goal = (max_end[kt - 1] if kt else 0)
                                goal += (max_end[kt] - goal) * (j + 1) // QB
                                while made < goal:
                                    max_unit(g + 1, (u + 1) % U, made, False)
                                    made += 1
                        if i >= 3:
                            pe.wait_ge(sem("unit_emptied"), sem_base(g) + i - 2)
                        elif not first:
                            pe.wait_ge(sem("unit_emptied"), sem_base(g) - NU + last_in_bank(i) + 1)
                        if unit[0] == "maxima":
                            maxima(g + 1, unit[1], out)
                            continue
                        pe.matmul(out[:, :], ks[u % U][0:NEG, kt * P:kt * P + P],
                                  qs[u % U][0:NEG, j * 512:j * 512 + 512], start=True, stop=True)\
                            .then_inc(sem("unit_done"), 1)
                        if j == 2 and kt >= 1:
                            values_at(g, t, u, kt - 1, first)
                        if j == 2 and kt == 0 and not first:
                            values_at(g - 1, t, u - 1, KT - 1, False)
                        if j == 3 and kt == 2 and not first:
                            total(g - 1, (u - 1) % 2)

                def values_at(g, t, u, kt, first):
                    s_list = seq_last if (isinstance(g, int) and g == HEADS - 1) else seq
                    s = s_list.index(("scores", kt, QB - 1))
                    pe.wait_ge(sem("unit_emptied"), sem_base(g) + s + 1)
                    if kt == 0:
                        pe.wait_ge(sem(f"v_loaded{u % U}"), 64 * (t + u // U + 1))
                        if not first:
                            pe.wait_ge(sem("o_copied"), g)
                    for j in range(QB):
                        mm = pe.matmul(out_bank[DH * j:DH * j + DH, :], vs[u % U][:, kt, :],
                                       probs[:, kt % RING, j * 512:j * 512 + 512],
                                       start=(kt == 0), stop=(kt == KT - 1))
                    mm.then_inc(sem("pv_done"), 1)
                    if kt in BY_PE:
                        if kt == BY_PE[0] and not first:
                            pe.wait_ge(sem("sum_inverted"), g)
                        for j in range(QB):
                            pe.matmul(sum_bank[DH * j:DH * j + DH, :], ones[:, :],
                                      probs[:, kt % RING, j * 512:j * 512 + 512],
                                      start=(kt == BY_PE[0]), stop=False)

                pe.wait_ge(sem("qk_loaded0"), 96)
                for r in range(QB):
                    for i in range(KT * r, KT * r + KT):
                        max_unit(0, 0, i, True)
                    if r == 3:
                        pe.wait_ge(sem("unit_emptied"), 1)
                    maxima(0, r, score_bank[(NU - QB + r) % 3])
                turns(turn)(pe)
                values_at(HEADS - 1, HEADS // U - 1, U - 1, KT - 1, False)
                total(HEADS - 1, (HEADS - 1) % 2)

            @block.scalar
            def _(act):
                def maxima_rows(src, u, r, count):
                    act.wait_ge(sem("unit_done"), count)
                    act.copy(qs[u % U][ROWS:NEG, r * 512:r * 512 + 512], src[0:2, :])\
                        .then_inc(sem("unit_emptied"), 1)

                def turn(g, t, u, last):
                    first = isinstance(g, int) and g == 0
                    for i, unit in enumerate(seq_last if last else seq):
                        count = QB + NU * g + i + 1
                        if unit[0] == "maxima":
                            maxima_rows(score_bank[i % 3], u + 1, unit[1], count)
                            continue
                        kt, j = unit[1], unit[2]
                        old = (kt - RING) % KT
                        if j == 0 and old in BY_POOL:
                            adds = max(BY_POOL.index(old), 1)
                            if kt >= RING:
                                act.wait_ge(sem("pool_added"), NADD * g + adds)
                            elif not first:
                                act.wait_ge(sem("pool_added"), NADD * (g - 1) + adds)
                        act.wait_ge(sem("unit_done"), count)
                        act.activation(probs[:, kt % RING, j * 512:j * 512 + 512], score_bank[i % 3][:, :],
                                       ACT.Exp, scale=SCALE).then_inc(sem("unit_emptied"), 1)

                for r in range(QB):
                    maxima_rows(score_bank[(NU - QB + r) % 3], 0, r, r + 1)
                turns(turn)(act)

            @block.gpsimd
            def _(pool):
                def turn(g, t, u, last):
                    acc = prob_sum[:, u % 2, :]
                    for n in range(1, len(BY_POOL)):
                        kt = BY_POOL[n]
                        s = (seq_last if last else seq).index(("scores", kt, QB - 1))
                        pool.wait_ge(sem("unit_emptied"), QB + NU * g + s + 1)
                        other = probs[:, BY_POOL[0] % RING, :] if n == 1 else acc
                        pool.tensor_tensor(acc, other, probs[:, kt % RING, :], ALU.add)\
                            .then_inc(sem("pool_added"), 1)
                        pool.wait_ge(sem("pool_added"), NADD * g + n)
                turns(turn)(pool)

            @block.vector
            def _(dve):
                def reduce_unit(g, i):
                    qt, j = i // QB, i % QB
                    r = qt // 4
                    dve.wait_ge(sem("max_done"), NMAX * g + i + 1)
                    dve.tensor_reduce(part_max[:, r % 2, qt, j:j + 1], max_bank[i % 3][:, :], AX.X, ALU.max)\
                        .then_inc(sem("max_reduced"), 1)
                    if i % KT == KT - 1:
                        c = Chain(dve, sem("dve_order"), 2 * (QB * g + r))
                        dve.wait_ge(sem("max_reduced"), NMAX * g + i + 1)
                        cols = slice(4 * r, 4 * r + 4)
                        c.link(dve.tensor_reduce(neg_max[:, r % 2, cols], part_max[:, r % 2, cols, :], AX.X,
                                                 ALU.max, negate=True))
                        c.link(dve.tensor_copy(neg[:, r % 2, cols, 0], neg_max[:, r % 2, cols]))
                        dve.tensor_tensor(neg[:, r % 2, cols, 1], neg_max[:, r % 2, cols],
                                          neg[:, r % 2, cols, 0].bitcast(F32), ALU.subtract)\
                            .then_inc(sem("neg_ready"), 1)

                def copy_out(g):
                    dve.wait_ge(sem("pv_done"), KT * (g + 1))
                    dve.tensor_copy(o_raw[:, :], out_bank[:, :]).then_inc(sem("o_copied"), 1)

                def normalise(g):
                    dve.wait_ge(sem("sum_done"), g + 1)
                    dve.reciprocal(inv_sum[:, :], sum_bank[:, :]).then_inc(sem("sum_inverted"), 1)
                    dve.wait_ge(sem("sum_inverted"), g + 1)
                    dve.tensor_tensor(o_out[:, :], o_raw[:, :], inv_sum[:, :], ALU.mult)\
                        .then_inc(sem("out_ready"), 1)

                def turn(g, t, u, last):
                    first = isinstance(g, int) and g == 0
                    for kt in range(KT):
                        if not last:
                            for i in range(max_end[kt - 1] if kt else 0, max_end[kt]):
                                reduce_unit(g + 1, i)
                        if kt == 0 and not first:
                            copy_out(g - 1)
                        if kt == 3 and not first:
                            normalise(g - 1)
                    if not first:
                        dve.wait_ge(sem("out_stored"), 16 * QB * g)

                for i in range(NMAX):
                    reduce_unit(0, i)
                turns(turn)(dve)
                copy_out(HEADS - 1)
                normalise(HEADS - 1)


def output_stage(nc, a, scr, out):
    ctx = ExitStack()
    with ctx:
        def sb(name, shape, dt=F32):
            return ctx.enter_context(nc.sbuf_tensor(name, shape, dt))

        sems = {}

        def sem(name):
            if name not in sems:
                sems[name] = ctx.enter_context(nc.semaphore("s3_" + name))
            return sems[name]

        bank = [ctx.enter_context(nc.psum_tensor(f"ob{i}", [P, 2, D], F32)) for i in range(8)]
        w_t = sb("ow_t", [P, KD, D])
        bias = sb("o_bias", [P, D])
        attn = [sb(f"attn{e}", [P, NK[e], NB]) for e in range(E)]
        res = [sb(f"res{e}", [P, TB, D]) for e in range(E)]
        rows = out.rearrange("b (e t p) d -> (b e) p t d", e=E, p=P)

        with nc.Block() as block:
            @block.sync
            def _(sp):
                sp.dma_start(w_t[:, :, :], a["o_w_t"].rearrange("(k p) n -> p k n", p=P))\
                    .then_inc(sem("weights"), 16)
                sp.dma_start(bias[:, :], a["o_b"].rearrange("(a n) -> a n", a=1).broadcast_to([P, D]))\
                    .then_inc(sem("weights"), 16)

                def load(b, e):
                    for k, m in enumerate(MK[e]):
                        sp.dma_start(attn[e][0:m, k, :], scr["attn"][bass.ds(8 * b + 4 * k + e, 1), 0:m, :]
                                     .rearrange("a d q -> (a d) q")).then_inc(sem(f"attn_loaded{e}"), 16)
                    sp.dma_start(res[e][:, :, :], scr["resid"][bass.ds(4 * b + e, 1)]
                                 .rearrange("a p t d -> (a p) t d")).then_inc(sem(f"res_loaded{e}"), 16)

                for e in range(E):
                    load(0, e)
                with sp.Fori(0, B - 1) as b:
                    for e in range(E):
                        sp.wait_ge(sem(f"stored{e}"), 16 * (b + 1))
                        load(b + 1, e)

            @block.scalar
            def _(act):
                with act.Fori(0, B) as b:
                    for e in range(E):
                        act.wait_ge(sem("sum_ready"), 4 * b + e + 1)
                        act.dma_start(rows[bass.ds(4 * b + e, 1)].rearrange("a p t d -> (a p) t d"),
                                      res[e][:, :, :]).then_inc(sem(f"stored{e}"), 16)
                for e in range(E):
                    act.wait_ge(sem(f"stored{e}"), 16 * B)

            @block.tensor
            def _(pe):
                pe.wait_ge(sem("weights"), 32)
                def body(b, first):
                    for e in range(E):
                        m = D >> e
                        pe.wait_ge(sem(f"attn_loaded{e}"), 16 * NK[e] * (b + 1))
                        if not first:
                            pe.wait_ge(sem("sum_ready"), 4 * b + e - 3)
                        for tile in range(TB):
                            for k, mk in enumerate(MK[e]):
                                mm = pe.matmul(bank[2 * e + tile // 2][:, tile % 2, 0:m],
                                               attn[e][0:mk, k, tile * P:tile * P + P], w_t[0:mk, k, 0:m],
                                               start=(k == 0), stop=(k == NK[e] - 1))
                        mm.then_inc(sem("proj_done"), 1)
                body(0, True)
                with pe.Fori(1, B) as b:
                    body(b, False)

            @block.vector
            def _(dve):
                dve.wait_ge(sem("weights"), 32)
                with dve.Fori(0, B) as b:
                    for e in range(E):
                        m = D >> e
                        dve.wait_ge(sem(f"res_loaded{e}"), 16 * (b + 1))
                        dve.tensor_tensor(res[e][:, :, 0:m], res[e][:, :, 0:m],
                                          bias[:, 0:m].unsqueeze(1).broadcast_to([P, TB, m]), ALU.add)\
                            .then_inc(sem("biased"), 1)
                        dve.wait_ge(sem("biased"), 4 * b + e + 1)
                        dve.wait_ge(sem("proj_done"), 4 * b + e + 1)
                        for half in range(2):
                            x = res[e][:, 2 * half:2 * half + 2, 0:m]
                            ins = dve.tensor_tensor(x, bank[2 * e + half][:, :, 0:m], x, ALU.add)
                        ins.then_inc(sem("sum_ready"), 1)


def build(nc, a, out):
    def scratch(name, shape):
        return nc.dram_tensor(name, shape, F32, kind="Internal").ap()
    scr = {
        "hi": scratch("scr_hi", (B * 2 * 2, P, T)),
        "lo": scratch("scr_lo", (B * 2 * 2, P, T)),
        "v": scratch("scr_v", (B * 2 * E, P, TB, P)),
        "resid": scratch("scr_resid", (B * E, P, TB, D)),
        "attn": scratch("scr_attn", (B * 2 * E, P, NB)),
    }
    token_stage(nc, a, scr)
    attention_stage(nc, a, scr)
    output_stage(nc, a, scr, out)


_ARRAYS = {
    "tokens": None,
    "emb_0": "L0_tok_emb_0", "emb_1": "L0_tok_emb_1", "emb_2": "L0_tok_emb_2", "emb_3": "L0_tok_emb_3",
    "proj_0_t": "L0_tok_proj_0", "proj_1_t": "L0_tok_proj_1", "proj_2_t": "L0_tok_proj_2",
    "proj_3_t": "L0_tok_proj_3",
    "Wq": "L0_attn_Wq", "Wk": "L0_attn_Wk", "Wv_t": "L0_attn_Wv", "Wo_t": "L0_attn_Wo",
    "fmq_w_t": "L0_attn_fmq_w", "fmk_w_t": "L0_attn_fmk_w", "fmq_b": "L0_attn_fmq_b",
    "fmk_b": "L0_attn_fmk_b", "rms_w": "L0_attn_rms_w",
    "norm_w": "L0_ffn_norm_w", "norm_b": "L0_ffn_norm_b",
    "q_w_t": "L0_ffn_q_w", "q_b": "L0_ffn_q_b", "k_w_t": "L0_ffn_k_w", "k_b": "L0_ffn_k_b",
    "v_w_t": "L0_ffn_v_w", "v_b": "L0_ffn_v_b", "o_w_t": "L0_ffn_o_w", "o_b": "L0_ffn_o_b",
}


def kernel(**inputs):
    import concourse.bacc as _bacc
    from concourse.bass_utils import run_bass_kernel_spmd as _run

    nc = _bacc.Bacc("TRN2", target_bir_lowering=False, num_devices=1)
    arrays, aps = {}, {}
    for name, source in _ARRAYS.items():
        if source is None:
            x = np.asarray(inputs["x"]).reshape(B * T // P, P).T
        else:
            x = np.asarray(inputs[source])
            if name.endswith("_t"):
                x = x.T
        x = np.ascontiguousarray(x)
        arrays["in_" + name] = x
        aps[name] = nc.dram_tensor("in_" + name, x.shape, mybir.dt.from_np(x.dtype), kind="ExternalInput").ap()
    out = nc.dram_tensor("out_0", (B, T, D), F32, kind="ExternalOutput").ap()
    build(nc, aps, out)
    r = _run(nc, [arrays], core_ids=[0])
    return r.results[0]["out_0"]
```

```python
import concourse.bass as bass
from concourse import mybir
from contextlib import ExitStack
import numpy as np

F32 = mybir.dt.float32
F32R = mybir.dt.float32r
I32 = mybir.dt.int32
ALU = mybir.AluOpType
ACT = mybir.ActivationFunctionType
AX = mybir.AxisListType

P = 128
B, T, D, H, E = 4, 2048, 256, 8, 4
DH = D // H
KD = D // P
NB = T // E
TB = NB // P
CUT = [0, 5000, 10000, 25000, 32000]
DE = [256, 64, 16, 4]
ECOL = [0, 256, 320, 336, 340]
TAIL = ECOL[4] - 256
EPS = 1e-5
QSCALE = float(2 * DH) ** -0.5
PAIRS = H // 2
NK = [2, 1, 1, 1]
MK = [[128, 128], [128], [64], [32]]
NKSUM = [0, 2, 3, 4, 5]


class Chain:

    def __init__(self, eng, sem, base=0):
        self.eng, self.sem, self.base, self.k = eng, sem, base, 0

    def link(self, ins):
        self.k += 1
        ins.then_inc(self.sem, 1)
        self.eng.wait_ge(self.sem, self.base + self.k)


def rsqrt(dve, chain, out, v, half):
    chain.link(dve.tensor_scalar(out.bitcast(I32), v.bitcast(I32), -0.5, float(0x5F3759DF),
                                 ALU.mult, ALU.add))
    for step in range(4):
        chain.link(dve.tensor_tensor(half, v, out, ALU.mult))
        chain.link(dve.scalar_tensor_tensor(half, half, -0.5, out, ALU.mult, ALU.mult))
        chain.link(dve.scalar_tensor_tensor(out, half, 1.5, out, ALU.add, ALU.mult))


def split_product(pe, out, left, right, first, last):
    pe.matmul(out, left[0], right[0], start=first, stop=False)
    pe.matmul(out, left[0], right[1], start=False, stop=False)
    return pe.matmul(out, left[1], right[0], start=False, stop=last)


def token_stage(nc, a, scr):
    ctx = ExitStack()
    with ctx:
        def sb(name, shape, dt=F32):
            return ctx.enter_context(nc.sbuf_tensor(name, shape, dt))

        sems = {}

        def sem(name):
            if name not in sems:
                sems[name] = ctx.enter_context(nc.semaphore("s1_" + name))
            return sems[name]

        bank = [ctx.enter_context(nc.psum_tensor(f"tb{i}", [P, 512], F32)) for i in range(8)]

        ident = sb("ident", [P, P])
        mask = sb("mask", [P, 4, P])
        bq_feat = sb("bq_feat", [P, 1])
        bk_feat = sb("bk_feat", [P, 1])
        fq_b = sb("fq_b", [P, KD])
        fk_b = sb("fk_b", [P, KD])
        fv_b = sb("fv_b", [P, D])
        nw = sb("nw", [P, KD])
        nb = sb("nb", [P, KD])
        index = sb("index", [P, 4, B * T // P], I32)
        member = sb("member", [P, 4, B * T // P])
        s_proj = [sb(f"s_proj{i}", [P, 3, D], F32R) for i in range(2)]
        s_wq = [sb(f"s_wq{i}", [P, KD, 2 * D], F32R) for i in range(2)]
        s_wk = [sb(f"s_wk{i}", [P, KD, 2 * D], F32R) for i in range(2)]
        s_wv, s_wo, s_fq, s_fk, s_fv = ([sb(f"{n}{i}", [P, KD, D], F32R) for i in range(2)]
                                        for n in ("s_wv", "s_wo", "s_fq", "s_fk", "s_fv"))
        state = sb("state", [P, PAIRS, 2 * DH])

        with ExitStack() as setup:
            def tmp(name, shape, dt=F32):
                return setup.enter_context(nc.sbuf_tensor(name, shape, dt))

            tokens = tmp("tokens", [P, B * T // P], I32)
            lower = tmp("lower", [P, B * T // P])
            proj_t = tmp("proj_t", [P, 3, D])
            wq_rows = tmp("wq_rows", [P, KD, D])
            wk_rows = tmp("wk_rows", [P, KD, D])
            fm_q = tmp("fm_q", [P, 4, 2, DH])
            fm_k = tmp("fm_k", [P, 4, 2, DH])
            rms_col = tmp("rms_col", [P, 1])
            wv_t = tmp("wv_t", [P, KD, D])
            wo_t = tmp("wo_t", [P, KD, D])
            wo_s = tmp("wo_s", [P, KD, D])
            fq_t = tmp("fq_t", [P, KD, D])
            fk_t = tmp("fk_t", [P, KD, D])
            fv_t = tmp("fv_t", [P, KD, D])

            with nc.Block() as block:
                @block.sync
                def _(sp):
                    def load(dst, src):
                        sp.dma_start(dst, src).then_inc(sem("loaded"), 16)
                    n = 0
                    rows = lambda w: w.rearrange("(k p) n -> p k n", p=P)
                    sp.wait_ge(sem("zeroed"), 3)
                    for dst, src in [(tokens[:, :], a["tokens"]),
                                     (proj_t[:, 0:2, :], rows(a["proj_0_t"])),
                                     (proj_t[0:64, 2, :], a["proj_1_t"]),
                                     (proj_t[64:80, 2, :], a["proj_2_t"]),
                                     (proj_t[80:84, 2, :], a["proj_3_t"]),
                                     (wq_rows[:, :, :], rows(a["Wq"])), (wk_rows[:, :, :], rows(a["Wk"])),
                                     (wv_t[:, :, :], rows(a["Wv_t"])), (wo_t[:, :, :], rows(a["Wo_t"])),
                                     (fq_t[:, :, :], rows(a["q_w_t"])), (fk_t[:, :, :], rows(a["k_w_t"])),
                                     (fv_t[:, :, :], rows(a["v_w_t"])),
                                     (fv_b[:, :], a["v_b"].rearrange("(a n) -> a n", a=1).broadcast_to([P, D]))]:
                        load(dst, src)
                        n += 1
                    for dst, src in [(fq_b, "q_b"), (fk_b, "k_b"), (nw, "norm_w"), (nb, "norm_b")]:
                        for k in range(KD):
                            load(dst[:, k:k + 1], a[src][k * P:(k + 1) * P].rearrange("(p a) -> p a", a=1))
                            n += 1
                    for j in range(4):
                        rows32 = slice(DH * j, DH * j + DH)
                        load(rms_col[rows32, :], a["rms_w"].rearrange("(p a) -> p a", a=1))
                        load(bq_feat[rows32, :], a["fmq_b"].rearrange("(p a) -> p a", a=1))
                        load(bk_feat[rows32, :], a["fmk_b"].rearrange("(p a) -> p a", a=1))
                        n += 3
                    assert n == 33
                    for j in range(4):
                        rows32 = slice(DH * j, DH * j + DH)
                        sp.dma_start(fm_q[rows32, j, 0, :], a["fmq_w_t"]).then_inc(sem("fm_loaded"), 16)
                        sp.dma_start(fm_k[rows32, j, 0, :], a["fmk_w_t"]).then_inc(sem("fm_loaded"), 16)

                @block.gpsimd
                def _(pool):
                    pool.memset(ident[:, :], 0.0).then_inc(sem("const"), 1)
                    pool.memset(mask[:, :, :], 1.0).then_inc(sem("const"), 1)
                    pool.wait_ge(sem("const"), 2)
                    pool.affine_select(out=ident[:, :], in_=ident[:, :], compare_op=ALU.not_equal, fill=1.0,
                                       base=0, pattern=[[-1, P]], channel_multiplier=1).then_inc(sem("const"), 1)
                    pool.affine_select(out=mask[:, :, :], in_=mask[:, :, :], compare_op=ALU.is_ge, fill=0.0,
                                       base=0, pattern=[[0, 4], [1, P]], channel_multiplier=-1)\
                        .then_inc(sem("const"), 1)

                @block.vector
                def _(dve):
                    dve.memset(fm_q[:, :, :, :], 0.0).then_inc(sem("zeroed"), 1)
                    dve.memset(fm_k[:, :, :, :], 0.0).then_inc(sem("zeroed"), 1)
                    dve.memset(state[:, :, :], 0.0).then_inc(sem("zeroed"), 1)
                    dve.wait_ge(sem("loaded"), 33 * 16)
                    dve.wait_ge(sem("fm_loaded"), 8 * 16)
                    c = Chain(dve, sem("setup_dve"))
                    for fm in (fm_q, fm_k):
                        c.link(dve.tensor_scalar(fm[:, :, 1, :], fm[:, :, 0, :], -1.0, None, ALU.mult))
                    for b in (bq_feat, bk_feat):
                        for r in (DH, 3 * DH):
                            c.link(dve.tensor_scalar(b[r:r + DH, :], b[r:r + DH, :], -1.0, None, ALU.mult))
                    for k in range(KD):
                        c.link(dve.tensor_scalar(wo_s[:, k, :], wo_t[:, k, :], rms_col[:, 0:1], QSCALE,
                                                 ALU.mult, ALU.mult))
                    for i in range(4):
                        c.link(dve.tensor_scalar(lower[:, :], tokens[:, :], float(CUT[i]), 0.0,
                                                 ALU.subtract, ALU.max))
                        c.link(dve.tensor_scalar(index[:, i, :], lower[:, :], float(CUT[i + 1] - CUT[i] - 1), None,
                                                 ALU.min))
                        c.link(dve.tensor_scalar(lower[:, :], tokens[:, :], float(CUT[i]), None, ALU.is_ge))
                        c.link(dve.tensor_scalar(member[:, i, :], tokens[:, :], float(CUT[i + 1]), None, ALU.is_lt))
                        c.link(dve.tensor_tensor(member[:, i, :], member[:, i, :], lower[:, :], ALU.mult))

                    def split(dst, src):
                        c.link(dve.tensor_copy(dst[0], src))
                        c.link(dve.tensor_tensor(dst[1], src, dst[0].bitcast(F32), ALU.subtract))

                    for dst, src in ((s_wv, wv_t), (s_wo, wo_s), (s_fq, fq_t), (s_fk, fk_t), (s_fv, fv_t)):
                        split([x[:, :, :] for x in dst], src[:, :, :])
                    split([x[:, 0:2, :] for x in s_proj], proj_t[:, 0:2, :])
                    split([x[0:TAIL, 2, :] for x in s_proj], proj_t[0:TAIL, 2, :])
                    for k in range(KD):
                        dve.wait_ge(sem("feat_w"), k + 1)
                        split([x[:, k, :] for x in s_wq], bank[2 * k][:, :])
                        split([x[:, k, :] for x in s_wk], bank[2 * k + 1][:, :])

                @block.tensor
                def _(pe):
                    pe.wait_ge(sem("setup_dve"), 2)
                    for k in range(KD):
                        for j in range(KD):
                            pe.matmul(bank[2 * k][:, j * 256:j * 256 + 256], wq_rows[:, j, k * P:k * P + P],
                                      fm_q[:, :, :, :].rearrange("p a b c -> p (a b c)"), start=True, stop=True)
                            last = pe.matmul(bank[2 * k + 1][:, j * 256:j * 256 + 256],
                                             wk_rows[:, j, k * P:k * P + P],
                                             fm_k[:, :, :, :].rearrange("p a b c -> p (a b c)"),
                                             start=True, stop=True)
                        last.then_inc(sem("feat_w"), 1)

        idx_blk = sb("idx_blk", [P, 2, 4, TB], I32)
        emb = sb("emb", [P, 2, TB, ECOL[4]])
        emb_t = [sb(f"emb_t{i}", [P, 3, NB], F32R) for i in range(2)]
        h_sb = sb("h_sb", [P, 2, TB, D])
        stats = sb("stats", [P, TB, 6])
        both = sb("both", [P, 3, TB])
        mean = sb("mean", [P, TB])
        veps = sb("veps", [P, TB])
        rstd = sb("rstd", [P, TB])
        x1 = sb("x1", [P, TB, D])
        x1_t = [sb(f"x1_t{i}", [P, KD, NB], F32R) for i in range(2)]
        feat_q = sb("feat_q", [P, 2, PAIRS, NB])
        feat_k = sb("feat_k", [P, 2, PAIRS, NB])
        v_sb = sb("v_sb", [P, 2, TB, D])
        k_tok = sb("k_tok", [P, 2, 512])
        attn_t = sb("attn_t", [P, H, P])
        o_t = sb("o_t", [P, D])
        o_sb = sb("o_sb", [P, TB, D])
        o_sq = sb("o_sq", [P, D])
        ss = sb("ss", [P, TB * H])
        rrms = sb("rrms", [P, TB * H])
        o_n = sb("o_n", [P, TB, D])
        o_nt = [sb(f"o_nt{i}", [P, KD, NB], F32R) for i in range(2)]
        h1 = sb("h1", [P, TB, D])
        x2 = sb("x2", [P, TB, D])
        resid = sb("resid", [P, TB, D])
        xn = sb("xn", [P, TB, D])
        xn_f = sb("xn_f", [P, KD, NB])
        xn_t = [sb(f"xn_t{i}", [P, KD, NB], F32R) for i in range(2)]
        newton = sb("newton", [P, TB * H])
        hi = sb("hi", [P, 4, NB], F32R)
        lo = sb("lo", [P, 4, NB], F32R)
        v2 = sb("v2", [P, TB, D])

        BLOCKS = B * E

        def turns(run):
            def all_turns(eng):
                run(0, 0, 0)
                run(1, 0, 1)
                with eng.Fori(0, (BLOCKS - E) // E) as t:
                    for u in range(2, E + 2):
                        run(4 * t + u, t, u)
                for u in (2, 3):
                    run(BLOCKS - E + u, BLOCKS // E - 1, u)
            return all_turns

        def place(t, u):
            return t + u // E, u % E

        def is_last(n):
            return isinstance(n, int) and n == BLOCKS - 1

        FRONT_LINKS, LINKS, OLD_LINKS, LAST_LINKS = 17, 74, 35, 57
        with nc.Block() as block:
            @block.gpsimd
            def _(pool):
                tables = [a[f"emb_{i}"] for i in range(4)]

                def gather(par):
                    for tile in range(TB):
                        for i in range(4):
                            pool.indirect_dma_start(
                                emb[:, par, tile, ECOL[i]:ECOL[i + 1]], None, tables[i],
                                bass.IndirectOffsetOnAxis(ap=idx_blk[:, par, i, tile:tile + 1], axis=0),
                            ).then_inc(sem(f"gathered{par}"), 16)

                def residual(n):
                    pool.wait_ge(sem("x2_ready"), n + 1)
                    pool.tensor_tensor(resid[:, :, :], h1[:, :, :], x2[:, :, :], ALU.add)\
                        .then_inc(sem("resid_ready"), 1)

                def turn(n, t, u):
                    if not (isinstance(n, int) and n == 0):
                        residual(n - 1)
                    if not (isinstance(n, int) and n + 2 >= BLOCKS):
                        gather(u % 2)

                pool.wait_ge(sem("indexed"), 2)
                gather(0)
                gather(1)
                pool.wait_ge(sem("indexed"), 3)
                turns(turn)(pool)
                residual(BLOCKS - 1)

            @block.sync
            def _(sp):
                def turn(n, t, u):
                    b, e = place(t, u)
                    cols = slice(e * NB, e * NB + NB)
                    sp.wait_ge(sem("resid_ready"), n + 1)
                    sp.dma_start(scr["resid"][bass.ds(n, 1)].rearrange("a p t d -> (a p) t d"),
                                 resid[:, :, :]).then_inc(sem("resid_stored"), 16)
                    for j in range(4):
                        row = 4 * b + 2 * (j % 2) + j // 2
                        sp.wait_ge(sem("hi_ready"), 4 * n + j + 1)
                        sp.dma_start(scr["hi"][bass.ds(row, 1), :, cols].rearrange("a p c -> (a p) c"),
                                     hi[:, j, :].bitcast(F32)).then_inc(sem("hi_stored"), 16)
                        sp.wait_ge(sem("lo_ready"), 4 * n + j + 1)
                        sp.dma_start(scr["lo"][bass.ds(row, 1), :, cols].rearrange("a p c -> (a p) c"),
                                     lo[:, j, :].bitcast(F32)).then_inc(sem("lo_stored"), 16)
                    sp.wait_ge(sem("v2_ready"), n + 1)
                    for k in range(KD):
                        sp.dma_start(scr["v"][bass.ds(8 * b + 4 * k + e, 1)].rearrange("a p t d -> (a p) t d"),
                                     v2[:, :, k * P:k * P + P]).then_inc(sem("v2_stored"), 16)
                turns(turn)(sp)
                sp.wait_ge(sem("resid_stored"), 16 * 4 * B)
                sp.wait_ge(sem("hi_stored"), 64 * 4 * B)
                sp.wait_ge(sem("lo_stored"), 64 * 4 * B)
                sp.wait_ge(sem("v2_stored"), 32 * 4 * B)

            @block.tensor
            def _(pe):
                def front_a(f, par, first):
                    pe.wait_ge(sem("masked"), f + 1)
                    if not first:
                        pe.wait_ge(sem("exp_done"), 8 * f)
                        pe.wait_ge(sem("v_ready"), f)
                    for k in range(3):
                        w = P if k < 2 else TAIL
                        for tile in range(TB):
                            mm = pe.transpose(bank[k][0:w, tile * P:tile * P + P],
                                              emb[:, par, tile, k * P:k * P + w], ident[:, :])
                        mm.then_inc(sem("emb_t_done"), 1)

                def front_b(f):
                    pe.wait_ge(sem("emb_t_ready"), f + 1)
                    for tile in range(TB):
                        out = bank[tile // 2][:, (tile % 2) * D:(tile % 2) * D + D]
                        for k in range(3):
                            w = P if k < 2 else TAIL
                            mm = split_product(pe, out, [x[0:w, k, tile * P:tile * P + P] for x in emb_t],
                                               [x[0:w, k, :] for x in s_proj], k == 0, k == 2)
                        if tile % 2:
                            mm.then_inc(sem("h_done"), 1)

                def front_c(f):
                    pe.wait_ge(sem("x1_ready"), f + 1)
                    if not (isinstance(f, int) and f < 2):
                        pe.wait_ge(sem("lo_ready"), 4 * (f - 1))
                        pe.wait_ge(sem("v2_ready"), f - 1)
                    for k in range(KD):
                        for tile in range(TB):
                            mm = pe.transpose(bank[k][:, tile * P:tile * P + P], x1[:, tile, k * P:k * P + P],
                                              ident[:, :])
                        mm.then_inc(sem("x1_t_done"), 1)

                def front_d(f, part):
                    if part == "queries":
                        pe.wait_ge(sem("x1_t_ready"), f + 1)
                    for j in {"queries": range(PAIRS), "keys": range(PAIRS, 2 * PAIRS), "values": ()}[part]:
                        if j >= 3:
                            pe.wait_ge(sem("exp_done"), 8 * f + j - 2)
                        w = s_wq if j < PAIRS else s_wk
                        cols = slice(j % PAIRS * P, j % PAIRS * P + P)
                        for k in range(KD):
                            mm = split_product(pe, bank[j % 3][:, :], [x[:, k, cols] for x in w],
                                               [x[:, k, :] for x in x1_t], k == 0, k == KD - 1)
                        mm.then_inc(sem("y_done"), 1)
                    for half in range(2) if part == "values" else ():
                        pe.wait_ge(sem("exp_done"), 8 * f + 6 + half)
                        for tile in (2 * half, 2 * half + 1):
                            out = bank[(8 + half) % 3][:, (tile % 2) * D:(tile % 2) * D + D]
                            for k in range(KD):
                                mm = split_product(pe, out, [x[:, k, tile * P:tile * P + P] for x in x1_t],
                                                   [x[:, k, :] for x in s_wv], k == 0, k == KD - 1)
                        mm.then_inc(sem("v_done"), 1)

                def chunk_scores(n, e, c):
                    par = e % 2
                    if c == 0:
                        pe.wait_ge(sem("exp_done"), 8 * n + 8)
                    else:
                        pe.wait_ge(sem("k_tok_ready"), 4 * n + c)
                        pe.wait_ge(sem("attn_ready"), 8 * n + 2 * c)
                    cols = slice(c * P, c * P + P)
                    for pair in range(PAIRS):
                        mm = pe.transpose(bank[3][:, pair * P:pair * P + P], feat_k[:, par, pair, cols],
                                          ident[:, :])
                    mm.then_inc(sem("k_tok_done"), 1)
                    for h in range(H):
                        r = slice(64 * (h % 2), 64 * (h % 2) + 64)
                        mm = pe.matmul(bank[4 + h % 2][:, (h // 2) * P:(h // 2) * P + P],
                                       feat_k[r, par, h // 2, cols], feat_q[r, par, h // 2, cols],
                                       start=True, stop=True)
                        if h >= H - 2:
                            mm.then_inc(sem("attn_done"), 1)

                def chunk_outputs(n, b, e, c):
                    par = e % 2
                    if c == 0:
                        pe.wait_ge(sem("v_ready"), n + 1)
                    pe.wait_ge(sem("attn_ready"), 8 * n + 2 * c + 2)
                    pe.wait_ge(sem("k_tok_ready"), 4 * n + c + 1)
                    pe.wait_ge(sem("state_ready"), 17 * b + 4 * e + c + 1)
                    for m in range(KD):
                        out = bank[6][:, m * P:m * P + P]
                        for i in range(2):
                            pe.matmul(out[64 * i:64 * i + 64, :], state[:, 2 * m + i, :],
                                      feat_q[:, par, 2 * m + i, c * P:c * P + P], start=True, stop=False)
                        for i in range(4):
                            h = 4 * m + i
                            mm = pe.matmul(out[DH * i:DH * i + DH, :], v_sb[:, par, c, h * DH:h * DH + DH],
                                           attn_t[:, (h % 2) * 4 + h // 2, :], start=False, stop=True)
                    mm.then_inc(sem("o_t_done"), 1)
                    for pair in range(PAIRS):
                        for i in range(2):
                            h = 2 * pair + i
                            mm = pe.matmul(bank[7][64 * i:64 * i + 64, pair * DH:pair * DH + DH],
                                           k_tok[:, c % 2, 64 * h:64 * h + 64],
                                           v_sb[:, par, c, h * DH:h * DH + DH], start=True, stop=True)
                    mm.then_inc(sem("state_done"), 1)

                def chunk_tokens(n, c):
                    pe.wait_ge(sem("o_t_ready"), 4 * n + c + 1)
                    if c:
                        pe.wait_ge(sem("o_ready"), 4 * n + c)
                    for m in range(KD):
                        mm = pe.transpose(bank[6][:, D + m * P:D + m * P + P], o_t[:, m * P:m * P + P],
                                          ident[:, :])
                    mm.then_inc(sem("o_done"), 1)

                def back_f(n):
                    pe.wait_ge(sem("o_n_ready"), n + 1)
                    for k in range(KD):
                        for tile in range(TB):
                            mm = pe.transpose(bank[4 + k][:, tile * P:tile * P + P],
                                              o_n[:, tile, k * P:k * P + P], ident[:, :])
                        mm.then_inc(sem("o_nt_done"), 1)

                def back_g(n, b, e):
                    pe.wait_ge(sem("o_nt_ready"), n + 1)
                    pe.wait_ge(sem("o_ready"), 4 * n + 4)
                    pe.wait_ge(sem("state_ready"), 17 * b + 4 * e + 5)
                    for tile in range(TB):
                        out = bank[6 + tile // 2][:, (tile % 2) * D:(tile % 2) * D + D]
                        for k in range(KD):
                            mm = split_product(pe, out, [x[:, k, tile * P:tile * P + P] for x in o_nt],
                                               [x[:, k, :] for x in s_wo], k == 0, k == KD - 1)
                        if tile % 2:
                            mm.then_inc(sem("attn_out_done"), 1)

                def back_h(n, e, front):
                    pe.wait_ge(sem("xn_ready"), n + 1)
                    for k in range(NK[e]):
                        if k and front:
                            pe.wait_ge(sem("h_ready"), 2 * n + 5)
                        for tile in range(TB):
                            mm = pe.transpose(bank[2 - 2 * k][:, tile * P:tile * P + P],
                                              xn[:, tile, k * P:k * P + P], ident[:, :])
                        mm.then_inc(sem("xn_t_done"), 1)

                def back_i(n, b, e, front):
                    pe.wait_ge(sem("xn_t_ready"), 5 * b + NKSUM[e + 1])
                    if front:
                        pe.wait_ge(sem("h_ready"), 2 * n + 6)
                    for j in range(4):
                        if j == 3:
                            pe.wait_ge(sem("lo_ready"), 4 * n + 1)
                        w = s_fq if j < 2 else s_fk
                        cols = slice(j % 2 * P, j % 2 * P + P)
                        for k, m in enumerate(MK[e]):
                            mm = split_product(pe, bank[(j + 1) % 3][:, :], [x[0:m, k, cols] for x in w],
                                               [x[0:m, k, :] for x in xn_t], k == 0, k == NK[e] - 1)
                        mm.then_inc(sem("qk_done"), 1)
                    for half in range(2):
                        pe.wait_ge(sem("lo_ready"), 4 * n + 2 + half)
                        for tile in (2 * half, 2 * half + 1):
                            out = bank[2 - 2 * half][:, (tile % 2) * D:(tile % 2) * D + D]
                            for k, m in enumerate(MK[e]):
                                mm = split_product(pe, out, [x[0:m, k, tile * P:tile * P + P] for x in xn_t],
                                                   [x[0:m, k, :] for x in s_fv], k == 0, k == NK[e] - 1)
                        mm.then_inc(sem("v2_done"), 1)

                def turn(n, t, u):
                    (b, e), (old_b, old_e) = place(t, u), place(t, u - 1)
                    old = not (isinstance(n, int) and n == 0)
                    new = not is_last(n)
                    chunk_scores(n, e, 0)
                    if new:
                        front_a(n + 1, (e + 1) % 2, False)
                    chunk_outputs(n, b, e, 0)
                    chunk_scores(n, e, 1)
                    chunk_tokens(n, 0)
                    if new:
                        front_b(n + 1)
                    chunk_outputs(n, b, e, 1)
                    chunk_scores(n, e, 2)
                    chunk_tokens(n, 1)
                    if old:
                        back_h(n - 1, old_e, new)
                    chunk_outputs(n, b, e, 2)
                    chunk_scores(n, e, 3)
                    chunk_tokens(n, 2)
                    if old:
                        back_i(n - 1, old_b, old_e, new)
                    if new:
                        front_c(n + 1)
                    chunk_outputs(n, b, e, 3)
                    if new:
                        front_d(n + 1, "queries")
                    chunk_tokens(n, 3)
                    if new:
                        front_d(n + 1, "keys")
                    back_f(n)
                    if new:
                        front_d(n + 1, "values")
                    back_g(n, b, e)

                front_a(0, 0, True)
                front_b(0)
                front_c(0)
                for part in ("queries", "keys", "values"):
                    front_d(0, part)
                turns(turn)(pe)
                back_h(BLOCKS - 1, E - 1, False)
                back_i(BLOCKS - 1, B - 1, E - 1, False)

            @block.scalar
            def _(act):
                def front_a(f):
                    for k in range(3):
                        w = P if k < 2 else TAIL
                        act.wait_ge(sem("emb_t_done"), 3 * f + k + 1)
                        act.copy(emb_t[0][0:w, k, :], bank[k][0:w, :]).then_inc(sem("emb_t_rounded"), 1)

                def front_b(f, par):
                    for half in range(2):
                        act.wait_ge(sem("h_done"), 2 * f + half + 1)
                        act.mul(h_sb[:, par, 2 * half:2 * half + 2, :].rearrange("p a b -> p (a b)"),
                                bank[half][:, :], float(D) ** 0.5).then_inc(sem("h_ready"), 1)

                def front_c(f):
                    for k in range(KD):
                        act.wait_ge(sem("x1_t_done"), 2 * f + k + 1)
                        act.copy(x1_t[0][:, k, :], bank[k][:, :]).then_inc(sem("x1_t_rounded"), 1)

                def front_d(f, par, part):
                    for j in {"queries": range(PAIRS), "keys": range(PAIRS, 2 * PAIRS), "values": ()}[part]:
                        act.wait_ge(sem("y_done"), 8 * f + j + 1)
                        feat, b = (feat_q, bq_feat) if j < PAIRS else (feat_k, bk_feat)
                        act.activation(feat[:, par, j % PAIRS, :], bank[j % 3][:, :], ACT.Exp,
                                       bias=b[:, 0:1]).then_inc(sem("exp_done"), 1)
                    for half in range(2) if part == "values" else ():
                        act.wait_ge(sem("v_done"), 2 * f + half + 1)
                        ins = act.copy(v_sb[:, par, 2 * half:2 * half + 2, :]
                                       .rearrange("p a b -> p (a b)"), bank[(8 + half) % 3][:, :])
                    if part == "values":
                        ins.then_inc(sem("v_ready"), 1)

                def keys(n, c):
                    act.wait_ge(sem("k_tok_done"), 4 * n + c + 1)
                    act.copy(k_tok[:, c % 2, :], bank[3][:, :]).then_inc(sem("k_tok_ready"), 1)

                def outputs(n, c):
                    act.wait_ge(sem("o_t_done"), 4 * n + c + 1)
                    act.copy(o_t[:, :], bank[6][:, 0:D]).then_inc(sem("o_t_ready"), 1)

                def by_token(n, c):
                    act.wait_ge(sem("o_done"), 4 * n + c + 1)
                    act.copy(o_sb[:, c, :], bank[6][:, D:2 * D]).then_inc(sem("o_ready"), 1)

                def back_f(n):
                    for k in range(KD):
                        act.wait_ge(sem("o_nt_done"), 2 * n + k + 1)
                        act.copy(o_nt[0][:, k, :], bank[4 + k][:, :]).then_inc(sem("o_nt_rounded"), 1)

                def back_h(n, b, e):
                    for k, m in enumerate(MK[e]):
                        act.wait_ge(sem("xn_t_done"), 5 * b + NKSUM[e] + k + 1)
                        act.activation(xn_f[0:m, k, :], bank[2 - 2 * k][0:m, :], ACT.Identity,
                                       scale=nw[0:m, k:k + 1], bias=nb[0:m, k:k + 1])\
                            .then_inc(sem("xn_f_ready"), 1)
                        act.wait_ge(sem("xn_f_ready"), 5 * b + NKSUM[e] + k + 1)
                        act.copy(xn_t[0][0:m, k, :], xn_f[0:m, k, :]).then_inc(sem("xn_t_rounded"), 1)

                def back_i(n):
                    if not (isinstance(n, int) and n == 0):
                        act.wait_ge(sem("hi_stored"), 64 * n)
                    for j in range(4):
                        act.wait_ge(sem("qk_done"), 4 * n + j + 1)
                        b = fq_b if j < 2 else fk_b
                        act.activation(hi[:, j, :], bank[(j + 1) % 3][:, :], ACT.Identity,
                                       bias=b[:, j % 2:j % 2 + 1]).then_inc(sem("hi_ready"), 1)

                def turn(n, t, u):
                    par = (u + 1) % 2
                    old = not (isinstance(n, int) and n == 0)
                    new = not is_last(n)
                    keys(n, 0)
                    if new:
                        front_a(n + 1)
                    outputs(n, 0)
                    keys(n, 1)
                    by_token(n, 0)
                    if new:
                        front_b(n + 1, par)
                    outputs(n, 1)
                    keys(n, 2)
                    by_token(n, 1)
                    if old:
                        back_h(n - 1, *place(t, u - 1))
                    outputs(n, 2)
                    keys(n, 3)
                    by_token(n, 2)
                    if old:
                        back_i(n - 1)
                    if new:
                        front_c(n + 1)
                    outputs(n, 3)
                    if new:
                        front_d(n + 1, par, "queries")
                    by_token(n, 3)
                    if new:
                        front_d(n + 1, par, "keys")
                    back_f(n)
                    if new:
                        front_d(n + 1, par, "values")

                front_a(0)
                front_b(0, 0)
                front_c(0)
                for part in ("queries", "keys", "values"):
                    front_d(0, 0, part)
                turns(turn)(act)
                back_h(BLOCKS - 1, B - 1, E - 1)
                back_i(BLOCKS - 1)

            @block.vector
            def _(dve):
                def layernorm(c, out, src):
                    for tile in range(TB):
                        ins = dve.bn_stats(stats[:, tile, :], src[:, tile, :])
                    c.link(ins)
                    dve.tensor_tensor(both[:, 0, :], stats[:, :, 1], stats[:, :, 4], ALU.add)
                    dve.tensor_tensor(both[:, 1, :], stats[:, :, 1], stats[:, :, 4], ALU.subtract)
                    c.link(dve.tensor_tensor(both[:, 2, :], stats[:, :, 2], stats[:, :, 5], ALU.add))
                    dve.tensor_scalar(mean[:, :], both[:, 0, :], 0.5, None, ALU.mult)
                    dve.tensor_scalar(both[:, 2, :], both[:, 2, :], 1.0 / D, EPS, ALU.mult, ALU.add)
                    c.link(dve.tensor_tensor(both[:, 1, :], both[:, 1, :], both[:, 1, :], ALU.mult))
                    c.link(dve.scalar_tensor_tensor(veps[:, :], both[:, 1, :], 0.25, both[:, 2, :],
                                                    ALU.mult, ALU.add))
                    rsqrt(dve, c, rstd[:, :], veps[:, :], newton[:, 0:TB])
                    for tile in range(TB):
                        ins = dve.tensor_scalar(out[:, tile, :], src[:, tile, :], mean[:, tile:tile + 1],
                                                rstd[:, tile:tile + 1], ALU.subtract, ALU.mult)
                    return ins

                def index_block(f, par):
                    dve.tensor_copy(idx_blk[:, par, :, :], index[:, :, bass.ds(4 * f, 4)])\
                        .then_inc(sem("indexed"), 1)

                def front_a(f, par, count):
                    dve.wait_ge(sem(f"gathered{par}"), 256 * count)
                    for i in range(4):
                        out = emb[:, par, :, ECOL[i]:ECOL[i + 1]]
                        m = member[:, i, bass.ds(4 * f, 4)].unsqueeze(2).broadcast_to([P, TB, DE[i]])
                        ins = dve.tensor_tensor(out, out, m, ALU.mult)
                    ins.then_inc(sem("masked"), 1)

                def front_a2(f):
                    for k in range(3):
                        w = P if k < 2 else TAIL
                        dve.wait_ge(sem("emb_t_rounded"), 3 * f + k + 1)
                        ins = dve.tensor_tensor(emb_t[1][0:w, k, :], bank[k][0:w, :],
                                                emb_t[0][0:w, k, :].bitcast(F32), ALU.subtract)
                    ins.then_inc(sem("emb_t_ready"), 1)

                def front_b(c, f, par):
                    dve.wait_ge(sem("h_ready"), 2 * f + 2)
                    layernorm(c, x1, h_sb[:, par]).then_inc(sem("x1_ready"), 1)

                def front_c(f):
                    for k in range(KD):
                        dve.wait_ge(sem("x1_t_rounded"), 2 * f + k + 1)
                        ins = dve.tensor_tensor(x1_t[1][:, k, :], bank[k][:, :],
                                                x1_t[0][:, k, :].bitcast(F32), ALU.subtract)
                    ins.then_inc(sem("x1_t_ready"), 1)

                def scores(n, e, c):
                    for g in range(2):
                        dve.wait_ge(sem("attn_done"), 8 * n + 2 * c + g + 1)
                        dve.tensor_tensor(attn_t[:, 4 * g:4 * g + 4, :],
                                          bank[4 + g][:, :].rearrange("p (h c) -> p h c", h=4),
                                          mask[:, :, :], ALU.mult).then_inc(sem("attn_ready"), 1)

                def new_state(n, e, c):
                    dve.wait_ge(sem("state_done"), 4 * n + c + 1)
                    ps = bank[7][:, 0:PAIRS * DH].rearrange("p (a b) -> p a b", a=PAIRS)
                    dve.tensor_tensor(state[0:64, :, 0:DH], state[0:64, :, 0:DH], ps[0:64, :, :], ALU.add)
                    dve.tensor_tensor(state[64:128, :, DH:64], state[64:128, :, DH:64],
                                      ps[64:128, :, :], ALU.add).then_inc(sem("state_ready"), 1)

                def squares(chain, n, c):
                    dve.wait_ge(sem("o_ready"), 4 * n + c + 1)
                    chain.link(dve.tensor_tensor(o_sq[:, :], o_sb[:, c, :], o_sb[:, c, :], ALU.mult))
                    chain.link(dve.tensor_reduce(ss[:, c * H:c * H + H],
                                                 o_sq[:, :].rearrange("p (h d) -> p h d", h=H), AX.X, ALU.add))

                def rms(chain, n):
                    chain.link(dve.tensor_scalar(ss[:, :], ss[:, :], QSCALE * QSCALE / DH, EPS,
                                                 ALU.mult, ALU.add))
                    rsqrt(dve, chain, rrms[:, :], ss[:, :], newton[:, :])
                    dve.tensor_tensor(o_n[:, :, :].rearrange("p t (h d) -> p (t h) d", h=H),
                                      o_sb[:, :, :].rearrange("p t (h d) -> p (t h) d", h=H),
                                      rrms[:, :].unsqueeze(2).broadcast_to([P, TB * H, DH]), ALU.mult)\
                        .then_inc(sem("o_n_ready"), 1)

                def back_f(n):
                    for k in range(KD):
                        dve.wait_ge(sem("o_nt_rounded"), 2 * n + k + 1)
                        ins = dve.tensor_tensor(o_nt[1][:, k, :], bank[4 + k][:, :],
                                                o_nt[0][:, k, :].bitcast(F32), ALU.subtract)
                    ins.then_inc(sem("o_nt_ready"), 1)

                def back_g(chain, n, par):
                    if not (isinstance(n, int) and n == 0):
                        dve.wait_ge(sem("resid_ready"), n)
                    for half in range(2):
                        dve.wait_ge(sem("attn_out_done"), 2 * n + half + 1)
                        ins = dve.tensor_tensor(h1[:, 2 * half:2 * half + 2, :]
                                                .rearrange("p a b -> p (a b)"), bank[6 + half][:, :],
                                                h_sb[:, par, 2 * half:2 * half + 2, :]
                                                .rearrange("p a b -> p (a b)"), ALU.add)
                    chain.link(ins)

                def back_g2(chain, n):
                    if not (isinstance(n, int) and n == 0):
                        dve.wait_ge(sem("resid_stored"), 16 * n)
                    layernorm(chain, x2, h1).then_inc(sem("x2_ready"), 1)

                def back_g3(chain, n):
                    dve.wait_ge(sem("x2_ready"), n + 1)
                    layernorm(chain, xn, x2).then_inc(sem("xn_ready"), 1)

                def back_h(b, e):
                    for k, m in enumerate(MK[e]):
                        dve.wait_ge(sem("xn_t_rounded"), 5 * b + NKSUM[e] + k + 1)
                        dve.tensor_tensor(xn_t[1][0:m, k, :], xn_f[0:m, k, :],
                                          xn_t[0][0:m, k, :].bitcast(F32), ALU.subtract)\
                            .then_inc(sem("xn_t_ready"), 1)

                def back_i(n):
                    if not (isinstance(n, int) and n == 0):
                        dve.wait_ge(sem("lo_stored"), 64 * n)
                        dve.wait_ge(sem("v2_stored"), 32 * n)
                    for j in range(4):
                        dve.wait_ge(sem("hi_ready"), 4 * n + j + 1)
                        b = fq_b if j < 2 else fk_b
                        dve.scalar_tensor_tensor(lo[:, j, :], bank[(j + 1) % 3][:, :],
                                                 b[:, j % 2:j % 2 + 1], hi[:, j, :].bitcast(F32),
                                                 ALU.add, ALU.subtract).then_inc(sem("lo_ready"), 1)
                    for half in range(2):
                        dve.wait_ge(sem("v2_done"), 2 * n + half + 1)
                        ins = dve.tensor_tensor(v2[:, 2 * half:2 * half + 2, :],
                                                bank[2 - 2 * half][:, :].rearrange("p (a b) -> p a b", a=2),
                                                fv_b[:, :].unsqueeze(1).broadcast_to([P, 2, D]), ALU.add)
                    ins.then_inc(sem("v2_ready"), 1)

                def turn(n, t, u):
                    (b, e), (old_b, old_e) = place(t, u), place(t, u - 1)
                    old = not (isinstance(n, int) and n == 0)
                    new = not is_last(n)
                    chain = Chain(dve, sem("dve_order"), FRONT_LINKS + (LINKS * n - OLD_LINKS if old else 0))
                    if old:
                        back_g(chain, n - 1, old_e % 2)
                    if e == 0:
                        dve.wait_ge(sem("attn_done"), 8 * n + 1)
                        dve.memset(state[:, :, :], 0.0).then_inc(sem("state_ready"), 1)
                        dve.wait_ge(sem("state_ready"), 17 * b + 1)
                    scores(n, e, 0)
                    if not (isinstance(n, int) and n + 2 >= BLOCKS):
                        index_block(n + 2, e % 2)
                    if old:
                        back_g2(chain, n - 1)
                    if new:
                        front_a2(n + 1)
                    new_state(n, e, 0)
                    squares(chain, n, 0)
                    scores(n, e, 1)
                    if old:
                        back_g3(chain, n - 1)
                    new_state(n, e, 1)
                    squares(chain, n, 1)
                    scores(n, e, 2)
                    if new:
                        front_b(chain, n + 1, (e + 1) % 2)
                    if old:
                        back_h(old_b, old_e)
                    new_state(n, e, 2)
                    squares(chain, n, 2)
                    scores(n, e, 3)
                    if old:
                        back_i(n - 1)
                    if new:
                        front_c(n + 1)
                    new_state(n, e, 3)
                    if not (isinstance(n, int) and n + 2 >= BLOCKS):
                        front_a(n + 2, e % 2, 2 * t + u // 2 + 2)
                    squares(chain, n, 3)
                    rms(chain, n)
                    back_f(n)
                    assert not (old and new) or chain.k == LINKS, chain.k
                    assert old or chain.k == LINKS - OLD_LINKS, chain.k
                    assert new or chain.k == LAST_LINKS, chain.k

                chain = Chain(dve, sem("dve_order"))
                index_block(0, 0)
                index_block(1, 1)
                front_a(0, 0, 1)
                front_a2(0)
                front_a(1, 1, 1)
                front_b(chain, 0, 0)
                front_c(0)
                assert chain.k == FRONT_LINKS, chain.k
                turns(turn)(dve)
                n = BLOCKS - 1
                chain = Chain(dve, sem("dve_order"), FRONT_LINKS + LINKS * n - OLD_LINKS + LAST_LINKS)
                back_g(chain, n, n % 2)
                back_g2(chain, n)
                back_g3(chain, n)
                back_h(B - 1, E - 1)
                back_i(n)


def attention_stage(nc, a, scr):
    KT = T // P
    QB = T // 512
    SCALE = float(D) ** -0.5
    RING = 8
    BY_PE = [9, 10, 13, 14, 15]
    BY_POOL = [k for k in range(KT) if k not in BY_PE]
    NADD = len(BY_POOL) - 1
    HEADS = B * H
    U = 4
    NMAX = KT * QB
    MAX_TILES = 15
    ORDER = "SASAVASASP"
    ROWS = 3 * DH
    NEG = ROWS + 2

    max_end = [min(NMAX, -(-NMAX * (kt + 1) // MAX_TILES)) for kt in range(KT)]
    seq, seq_last = [], []
    for kt in range(KT):
        for j in range(QB):
            seq.append(("scores", kt, j))
            seq_last.append(("scores", kt, j))
            for r in range(QB):
                if j == 0 and kt == next(k for k in range(KT) if max_end[k] >= KT * (r + 1)) + 1:
                    seq.append(("maxima", r))
    NU = len(seq)
    assert NU == KT * QB + QB

    def last_in_bank(i):
        return max(p for p in range(NU) if p % 3 == i % 3)

    ctx = ExitStack()
    with ctx:
        def sb(name, shape, dt=F32):
            return ctx.enter_context(nc.sbuf_tensor(name, shape, dt))

        sems = {}

        def sem(name):
            if name not in sems:
                sems[name] = ctx.enter_context(nc.semaphore("s2_" + name))
            return sems[name]

        bank = [ctx.enter_context(nc.psum_tensor(f"ab{i}", [P, 512], F32)) for i in range(8)]
        max_bank, score_bank, out_bank, sum_bank = bank[0:3], bank[3:6], bank[6], bank[7]
        qs = [sb(f"qs{i}", [P, T], F32R) for i in range(U)]
        ks = [sb(f"ks{i}", [P, T], F32R) for i in range(U)]
        vs = [sb(f"vs{i}", [P, KT, DH]) for i in range(U)]
        probs = sb("probs", [P, RING, T])
        prob_sum = sb("prob_sum", [P, 2, T])
        ones = sb("ones", [P, DH])
        ident2 = sb("ident2", [P, P])
        one_rows = sb("one_rows", [2, T])
        part_max = sb("part_max", [P, 2, KT, QB])
        neg_max = sb("neg_max", [P, 2, KT])
        neg = sb("neg", [P, 2, KT, 2], F32R)
        o_raw = sb("o_raw", [P, 512])
        sums_t = sb("sums_t", [P, 512])
        inv = sb("inv", [P, 512 // DH])
        inv_wide = sb("inv_wide", [P, 512 // DH, DH])
        inv_rows = sb("inv_rows", [P, 512])
        o_out = sb("o_out", [P, 512])

        with nc.Block() as block:
            @block.vector
            def _(dve):
                dve.memset(ones[:, :], 1.0)
                dve.memset(one_rows[:, :], 1.0).then_inc(sem("one_rows"), 1)
                dve.wait_ge(sem("one_rows"), 1)
                for u in range(U):
                    dve.tensor_copy(ks[u][ROWS:NEG, :], one_rows[:, :])

            @block.gpsimd
            def _(pool):
                pool.memset(ident2[:, :], 0.0).then_inc(sem("zero"), 1)
                pool.wait_ge(sem("zero"), 1)
                pool.affine_select(out=ident2[:, :], in_=ident2[:, :], compare_op=ALU.not_equal, fill=1.0,
                                   base=0, pattern=[[-1, P]], channel_multiplier=1)

        def turns(run):
            def all_turns(eng):
                run(0, 0, 0, False)
                with eng.Fori(0, (HEADS - U) // U) as t:
                    for u in range(1, U + 1):
                        run(4 * t + u, t, u, False)
                for u in range(1, U):
                    t = HEADS // U - 1
                    run(4 * t + u, t, u, u == U - 1)
            return all_turns

        with nc.Block() as block:
            @block.sync
            def _(sp):
                def load(t, u):
                    cols = slice(DH * u, DH * u + DH)
                    for dst, part, kind in ((qs[u][0:32, :], "hi", 0), (qs[u][32:64, :], "hi", 0),
                                            (qs[u][64:96, :], "lo", 0), (ks[u][0:32, :], "hi", 1),
                                            (ks[u][32:64, :], "lo", 1), (ks[u][64:96, :], "hi", 1)):
                        sp.dma_start(dst.bitcast(F32), scr[part][bass.ds(2 * t + kind, 1), cols, :]
                                     .rearrange("a p c -> (a p) c")).then_inc(sem(f"qk_loaded{u}"), 16)
                    for e in range(E):
                        sp.dma_start(vs[u][:, TB * e:TB * e + TB, :],
                                     scr["v"][bass.ds(4 * t + e, 1), :, :, cols]
                                     .rearrange("a p t d -> (a p) t d")).then_inc(sem(f"v_loaded{u}"), 16)

                def store(g, t, u):
                    sp.wait_ge(sem("out_ready"), g + 1)
                    for j in range(QB):
                        sp.dma_start(scr["attn"][bass.ds(4 * t + j, 1), DH * u:DH * u + DH, :]
                                     .rearrange("a d q -> (a d) q"), o_out[DH * j:DH * j + DH, :])\
                            .then_inc(sem("out_stored"), 16)

                def turn(g, t, u, last):
                    if isinstance(g, int) and g == 0:
                        return
                    if not (isinstance(t, int) and t == HEADS // U - 1):
                        sp.wait_ge(sem("pv_done"), KT * g)
                        load(t + 1, u - 1)
                    store(g - 1, t, u - 1)

                for u in range(U):
                    load(0, u)
                turns(turn)(sp)
                store(HEADS - 1, HEADS // U - 1, U - 1)
                sp.wait_ge(sem("out_stored"), 16 * QB * HEADS)

            @block.tensor
            def _(pe):
                def max_unit(g, u, i, first):
                    if i >= 3:
                        pe.wait_ge(sem("max_reduced"), NMAX * g + i - 2)
                    elif not first:
                        p = max(p for p in range(NMAX) if p % 3 == i)
                        pe.wait_ge(sem("max_reduced"), NMAX * (g - 1) + p + 1)
                    qt, j = i // QB, i % QB
                    pe.matmul(max_bank[i % 3][:, :], qs[u][0:ROWS, qt * P:qt * P + P],
                              ks[u][0:ROWS, j * 512:j * 512 + 512], start=True, stop=True)\
                        .then_inc(sem("max_done"), 1)

                def maxima(g, r, out):
                    pe.wait_ge(sem("neg_ready"), QB * g + r + 1)
                    for q in range(4):
                        mm = pe.transpose(out[0:2, q * P:q * P + P],
                                          neg[:, r % 2, 4 * r + q, :].bitcast(F32), ident2[:, :])
                    mm.then_inc(sem("unit_done"), 1)

                def total(g, par):
                    pe.wait_ge(sem("pool_added"), NADD * (g + 1))
                    for j in range(QB):
                        mm = pe.matmul(sum_bank[DH * j:DH * j + DH, :], ones[:, :],
                                       prob_sum[:, par, j * 512:j * 512 + 512], start=False, stop=True)
                    mm.then_inc(sem("sum_done"), 1)

                def sem_base(g):
                    return QB + NU * g

                def values(g, t, u, kt, first):
                    s = (seq_last if u == U - 1 and isinstance(g, int) else seq).index(("scores", kt, QB - 1))
                    pe.wait_ge(sem("unit_emptied"), sem_base(g) + s + 1)
                    if kt == 0:
                        pe.wait_ge(sem(f"v_loaded{u % U}"), 64 * (t + u // U + 1))
                        if not first:
                            pe.wait_ge(sem("o_copied"), g)
                    for j in range(QB):
                        mm = pe.matmul(out_bank[DH * j:DH * j + DH, :], vs[u % U][:, kt, :],
                                       probs[:, kt % RING, j * 512:j * 512 + 512],
                                       start=(kt == 0), stop=(kt == KT - 1))
                    mm.then_inc(sem("pv_done"), 1)

                def sums(g, kt, first):
                    if kt == BY_PE[0] and not first:
                        pe.wait_ge(sem("sum_read"), g)
                    for j in range(QB):
                        mm = pe.matmul(sum_bank[DH * j:DH * j + DH, :], ones[:, :],
                                       probs[:, kt % RING, j * 512:j * 512 + 512],
                                       start=(kt == BY_PE[0]), stop=False)
                    mm.then_inc(sem("tile_summed"), 1)

                def turn(g, t, u, last):
                    first = isinstance(g, int) and g == 0
                    order = seq_last if last else seq
                    made = [0]

                    def max_units(goal):
                        while not last and made[0] < goal:
                            max_unit(g + 1, (u + 1) % U, made[0], False)
                            made[0] += 1

                    def through(unit):
                        i = order.index(unit)
                        if i >= 3:
                            pe.wait_ge(sem("unit_emptied"), sem_base(g) + i - 2)
                        elif not first:
                            pe.wait_ge(sem("unit_emptied"), sem_base(g) - NU + last_in_bank(i) + 1)
                        return score_bank[i % 3]

                    if not last:
                        pe.wait_ge(sem(f"qk_loaded{(u + 1) % U}"), 96 * (t + (u + 1) // U + 1))
                    for kt in range(KT):
                        made_before = max_end[kt - 1] if kt else 0
                        a = j = 0
                        for step in ORDER:
                            if step == "A":
                                a += 1
                                max_units(min(made_before + a, max_end[kt]))
                            elif step == "S":
                                if kt == 0 and j == 0:
                                    pe.wait_ge(sem("unit_emptied"), sem_base(g))
                                out = through(("scores", kt, j))
                                pe.matmul(out[:, :], ks[u % U][0:NEG, kt * P:kt * P + P],
                                          qs[u % U][0:NEG, j * 512:j * 512 + 512], start=True, stop=True)\
                                    .then_inc(sem("unit_done"), 1)
                                i = order.index(("scores", kt, j)) + 1
                                if i < len(order) and order[i][0] == "maxima":
                                    maxima(g + 1, order[i][1], through(order[i]))
                                j += 1
                            elif step == "V" and kt >= 1:
                                values(g, t, u, kt - 1, first)
                            elif step == "V" and not first:
                                values(g - 1, t, u - 1, KT - 1, False)
                            elif step == "P" and kt - 1 in BY_PE:
                                sums(g, kt - 1, first)
                            elif step == "P" and kt == 0 and not first:
                                sums(g - 1, KT - 1, False)
                            elif step == "P" and kt == 2 and not first:
                                total(g - 1, (u - 1) % 2)
                        max_units(max_end[kt])

                pe.wait_ge(sem("qk_loaded0"), 96)
                for r in range(QB):
                    for i in range(KT * r, KT * r + KT):
                        max_unit(0, 0, i, True)
                    if r == 3:
                        pe.wait_ge(sem("unit_emptied"), 1)
                    maxima(0, r, score_bank[(NU - QB + r) % 3])
                turns(turn)(pe)
                values(HEADS - 1, HEADS // U - 1, U - 1, KT - 1, False)
                sums(HEADS - 1, KT - 1, False)
                total(HEADS - 1, (HEADS - 1) % 2)

            @block.scalar
            def _(act):
                def maxima_rows(src, u, r, count):
                    act.wait_ge(sem("unit_done"), count)
                    act.copy(qs[u % U][ROWS:NEG, r * 512:r * 512 + 512], src[0:2, :])\
                        .then_inc(sem("unit_emptied"), 1)

                def copy_out(g):
                    act.wait_ge(sem("pv_done"), KT * (g + 1))
                    act.copy(o_raw[:, :], out_bank[:, :]).then_inc(sem("o_copied"), 1)

                def spread(g):
                    act.wait_ge(sem("inv_ready"), g + 1)
                    act.copy(inv_wide[:, :, :], inv[:, :].unsqueeze(2).broadcast_to([P, 512 // DH, DH]))\
                        .then_inc(sem("inv_spread"), 1)

                def turn(g, t, u, last):
                    first = isinstance(g, int) and g == 0
                    for i, unit in enumerate(seq_last if last else seq):
                        if unit == ("scores", 0, 3) and not first:
                            copy_out(g - 1)
                        if unit == ("scores", 4, 0) and not first:
                            spread(g - 1)
                        count = QB + NU * g + i + 1
                        if unit[0] == "maxima":
                            maxima_rows(score_bank[i % 3], u + 1, unit[1], count)
                            continue
                        kt, j = unit[1], unit[2]
                        old = (kt - RING) % KT
                        if j == 0 and old in BY_POOL:
                            adds = max(BY_POOL.index(old), 1)
                            if kt >= RING:
                                act.wait_ge(sem("pool_added"), NADD * g + adds)
                            elif not first:
                                act.wait_ge(sem("pool_added"), NADD * (g - 1) + adds)
                        act.wait_ge(sem("unit_done"), count)
                        act.activation(probs[:, kt % RING, j * 512:j * 512 + 512], score_bank[i % 3][:, :],
                                       ACT.Exp, scale=SCALE).then_inc(sem("unit_emptied"), 1)

                for r in range(QB):
                    maxima_rows(score_bank[(NU - QB + r) % 3], 0, r, r + 1)
                turns(turn)(act)
                act.wait_ge(sem("out_ready"), HEADS - 1)
                copy_out(HEADS - 1)
                spread(HEADS - 1)

            @block.gpsimd
            def _(pool):
                def turn(g, t, u, last):
                    acc = prob_sum[:, u % 2, :]
                    for n in range(1, len(BY_POOL)):
                        kt = BY_POOL[n]
                        s = (seq_last if last else seq).index(("scores", kt, QB - 1))
                        pool.wait_ge(sem("unit_emptied"), QB + NU * g + s + 1)
                        other = probs[:, BY_POOL[0] % RING, :] if n == 1 else acc
                        pool.tensor_tensor(acc, other, probs[:, kt % RING, :], ALU.add)\
                            .then_inc(sem("pool_added"), 1)
                        pool.wait_ge(sem("pool_added"), NADD * g + n)
                turns(turn)(pool)

            @block.vector
            def _(dve):
                def reduce_unit(g, i):
                    qt, j = i // QB, i % QB
                    r = qt // 4
                    dve.wait_ge(sem("max_done"), NMAX * g + i + 1)
                    dve.tensor_reduce(part_max[:, r % 2, qt, j:j + 1], max_bank[i % 3][:, :], AX.X, ALU.max)\
                        .then_inc(sem("max_reduced"), 1)
                    if i % KT == KT - 1:
                        c = Chain(dve, sem("dve_order"), 2 * (QB * g + r))
                        dve.wait_ge(sem("max_reduced"), NMAX * g + i + 1)
                        cols = slice(4 * r, 4 * r + 4)
                        c.link(dve.tensor_reduce(neg_max[:, r % 2, cols], part_max[:, r % 2, cols, :], AX.X,
                                                 ALU.max, negate=True))
                        c.link(dve.tensor_copy(neg[:, r % 2, cols, 0], neg_max[:, r % 2, cols]))
                        dve.tensor_tensor(neg[:, r % 2, cols, 1], neg_max[:, r % 2, cols],
                                          neg[:, r % 2, cols, 0].bitcast(F32), ALU.subtract)\
                            .then_inc(sem("neg_ready"), 1)

                def invert(g):
                    dve.wait_ge(sem("sum_done"), g + 1)
                    dve.transpose(sums_t[:, :], sum_bank[:, :]).then_inc(sem("sum_read"), 1)
                    dve.wait_ge(sem("sum_read"), g + 1)
                    dve.reciprocal(inv[:, :], sums_t[:, 0:512:DH]).then_inc(sem("inv_ready"), 1)

                def normalise(g):
                    dve.wait_ge(sem("inv_spread"), g + 1)
                    dve.transpose(inv_rows[:, :], inv_wide[:, :, :].rearrange("p a b -> p (a b)"))\
                        .then_inc(sem("inv_back"), 1)
                    dve.wait_ge(sem("inv_back"), g + 1)
                    dve.tensor_tensor(o_out[:, :], o_raw[:, :], inv_rows[:, :], ALU.mult)\
                        .then_inc(sem("out_ready"), 1)

                def turn(g, t, u, last):
                    first = isinstance(g, int) and g == 0
                    for kt in range(KT):
                        if not last:
                            for i in range(max_end[kt - 1] if kt else 0, max_end[kt]):
                                reduce_unit(g + 1, i)
                        if kt == 2 and not first:
                            invert(g - 1)
                        if kt == 5 and not first:
                            normalise(g - 1)
                    if not first:
                        dve.wait_ge(sem("out_stored"), 16 * QB * g)

                for i in range(NMAX):
                    reduce_unit(0, i)
                turns(turn)(dve)
                invert(HEADS - 1)
                normalise(HEADS - 1)


def output_stage(nc, a, scr, out):
    ctx = ExitStack()
    with ctx:
        def sb(name, shape, dt=F32):
            return ctx.enter_context(nc.sbuf_tensor(name, shape, dt))

        sems = {}

        def sem(name):
            if name not in sems:
                sems[name] = ctx.enter_context(nc.semaphore("s3_" + name))
            return sems[name]

        bank = [ctx.enter_context(nc.psum_tensor(f"ob{i}", [P, 2, D], F32)) for i in range(8)]
        w_t = sb("ow_t", [P, KD, D])
        bias = sb("o_bias", [P, D])
        attn = [sb(f"attn{e}", [P, NK[e], NB]) for e in range(E)]
        res = [sb(f"res{e}", [P, TB, D]) for e in range(E)]
        rows = out.rearrange("b (e t p) d -> (b e) p t d", e=E, p=P)

        with nc.Block() as block:
            @block.sync
            def _(sp):
                sp.dma_start(w_t[:, :, :], a["o_w_t"].rearrange("(k p) n -> p k n", p=P))\
                    .then_inc(sem("weights"), 16)
                sp.dma_start(bias[:, :], a["o_b"].rearrange("(a n) -> a n", a=1).broadcast_to([P, D]))\
                    .then_inc(sem("weights"), 16)

                def load(b, e):
                    for k, m in enumerate(MK[e]):
                        sp.dma_start(attn[e][0:m, k, :], scr["attn"][bass.ds(8 * b + 4 * k + e, 1), 0:m, :]
                                     .rearrange("a d q -> (a d) q")).then_inc(sem(f"attn_loaded{e}"), 16)
                    sp.dma_start(res[e][:, :, :], scr["resid"][bass.ds(4 * b + e, 1)]
                                 .rearrange("a p t d -> (a p) t d")).then_inc(sem(f"res_loaded{e}"), 16)

                for e in range(E):
                    load(0, e)
                with sp.Fori(0, B - 1) as b:
                    for e in range(E):
                        sp.wait_ge(sem(f"stored{e}"), 16 * (b + 1))
                        load(b + 1, e)

            @block.scalar
            def _(act):
                with act.Fori(0, B) as b:
                    for e in range(E):
                        act.wait_ge(sem("sum_ready"), 4 * b + e + 1)
                        act.dma_start(rows[bass.ds(4 * b + e, 1)].rearrange("a p t d -> (a p) t d"),
                                      res[e][:, :, :]).then_inc(sem(f"stored{e}"), 16)
                for e in range(E):
                    act.wait_ge(sem(f"stored{e}"), 16 * B)

            @block.tensor
            def _(pe):
                pe.wait_ge(sem("weights"), 32)
                def body(b, first):
                    for e in range(E):
                        m = D >> e
                        pe.wait_ge(sem(f"attn_loaded{e}"), 16 * NK[e] * (b + 1))
                        if not first:
                            pe.wait_ge(sem("sum_ready"), 4 * b + e - 3)
                        for tile in range(TB):
                            for k, mk in enumerate(MK[e]):
                                mm = pe.matmul(bank[2 * e + tile // 2][:, tile % 2, 0:m],
                                               attn[e][0:mk, k, tile * P:tile * P + P], w_t[0:mk, k, 0:m],
                                               start=(k == 0), stop=(k == NK[e] - 1))
                        mm.then_inc(sem("proj_done"), 1)
                body(0, True)
                with pe.Fori(1, B) as b:
                    body(b, False)

            @block.vector
            def _(dve):
                dve.wait_ge(sem("weights"), 32)
                with dve.Fori(0, B) as b:
                    for e in range(E):
                        m = D >> e
                        dve.wait_ge(sem(f"res_loaded{e}"), 16 * (b + 1))
                        dve.tensor_tensor(res[e][:, :, 0:m], res[e][:, :, 0:m],
                                          bias[:, 0:m].unsqueeze(1).broadcast_to([P, TB, m]), ALU.add)\
                            .then_inc(sem("biased"), 1)
                        dve.wait_ge(sem("biased"), 4 * b + e + 1)
                        dve.wait_ge(sem("proj_done"), 4 * b + e + 1)
                        for half in range(2):
                            x = res[e][:, 2 * half:2 * half + 2, 0:m]
                            ins = dve.tensor_tensor(x, bank[2 * e + half][:, :, 0:m], x, ALU.add)
                        ins.then_inc(sem("sum_ready"), 1)


def build(nc, a, out):
    def scratch(name, shape):
        return nc.dram_tensor(name, shape, F32, kind="Internal").ap()
    scr = {
        "hi": scratch("scr_hi", (B * 2 * 2, P, T)),
        "lo": scratch("scr_lo", (B * 2 * 2, P, T)),
        "v": scratch("scr_v", (B * 2 * E, P, TB, P)),
        "resid": scratch("scr_resid", (B * E, P, TB, D)),
        "attn": scratch("scr_attn", (B * 2 * E, P, NB)),
    }
    token_stage(nc, a, scr)
    attention_stage(nc, a, scr)
    output_stage(nc, a, scr, out)


_ARRAYS = {
    "tokens": None,
    "emb_0": "L0_tok_emb_0", "emb_1": "L0_tok_emb_1", "emb_2": "L0_tok_emb_2", "emb_3": "L0_tok_emb_3",
    "proj_0_t": "L0_tok_proj_0", "proj_1_t": "L0_tok_proj_1", "proj_2_t": "L0_tok_proj_2",
    "proj_3_t": "L0_tok_proj_3",
    "Wq": "L0_attn_Wq", "Wk": "L0_attn_Wk", "Wv_t": "L0_attn_Wv", "Wo_t": "L0_attn_Wo",
    "fmq_w_t": "L0_attn_fmq_w", "fmk_w_t": "L0_attn_fmk_w", "fmq_b": "L0_attn_fmq_b",
    "fmk_b": "L0_attn_fmk_b", "rms_w": "L0_attn_rms_w",
    "norm_w": "L0_ffn_norm_w", "norm_b": "L0_ffn_norm_b",
    "q_w_t": "L0_ffn_q_w", "q_b": "L0_ffn_q_b", "k_w_t": "L0_ffn_k_w", "k_b": "L0_ffn_k_b",
    "v_w_t": "L0_ffn_v_w", "v_b": "L0_ffn_v_b", "o_w_t": "L0_ffn_o_w", "o_b": "L0_ffn_o_b",
}


def kernel(**inputs):
    import concourse.bacc as _bacc
    from concourse.bass_utils import run_bass_kernel_spmd as _run

    nc = _bacc.Bacc("TRN2", target_bir_lowering=False, num_devices=1)
    arrays, aps = {}, {}
    for name, source in _ARRAYS.items():
        if source is None:
            x = np.asarray(inputs["x"]).reshape(B * T // P, P).T
        else:
            x = np.asarray(inputs[source])
            if name.endswith("_t"):
                x = x.T
        x = np.ascontiguousarray(x)
        arrays["in_" + name] = x
        aps[name] = nc.dram_tensor("in_" + name, x.shape, mybir.dt.from_np(x.dtype), kind="ExternalInput").ap()
    out = nc.dram_tensor("out_0", (B, T, D), F32, kind="ExternalOutput").ap()
    build(nc, aps, out)
    r = _run(nc, [arrays], core_ids=[0])
    return r.results[0]["out_0"]
```

```python
import concourse.bass as bass
from concourse import mybir
from contextlib import ExitStack
import numpy as np

F32 = mybir.dt.float32
F32R = mybir.dt.float32r
I32 = mybir.dt.int32
ALU = mybir.AluOpType
ACT = mybir.ActivationFunctionType
AX = mybir.AxisListType

P = 128
B, T, D, H, E = 4, 2048, 256, 8, 4
DH = D // H
KD = D // P
NB = T // E
TB = NB // P
CUT = [0, 5000, 10000, 25000, 32000]
DE = [256, 64, 16, 4]
ECOL = [0, 256, 320, 336, 340]
TAIL = ECOL[4] - 256
EPS = 1e-5
QSCALE = float(2 * DH) ** -0.5
PAIRS = H // 2
NK = [2, 1, 1, 1]
MK = [[128, 128], [128], [64], [32]]
NKSUM = [0, 2, 3, 4, 5]


class Chain:

    def __init__(self, eng, sem, base=0):
        self.eng, self.sem, self.base, self.k = eng, sem, base, 0

    def link(self, ins):
        self.k += 1
        ins.then_inc(self.sem, 1)
        self.eng.wait_ge(self.sem, self.base + self.k)


def rsqrt(dve, chain, out, v, half):
    chain.link(dve.tensor_scalar(out.bitcast(I32), v.bitcast(I32), -0.5, float(0x5F3759DF),
                                 ALU.mult, ALU.add))
    for step in range(3):
        chain.link(dve.tensor_tensor(half, v, out, ALU.mult))
        chain.link(dve.scalar_tensor_tensor(half, half, -0.5, out, ALU.mult, ALU.mult))
        chain.link(dve.scalar_tensor_tensor(out, half, 1.5, out, ALU.add, ALU.mult))


def split_product(pe, out, left, right, first, last):
    pe.matmul(out, left[0], right[0], start=first, stop=False)
    pe.matmul(out, left[0], right[1], start=False, stop=False)
    return pe.matmul(out, left[1], right[0], start=False, stop=last)


def token_stage(nc, a, scr):
    ctx = ExitStack()
    with ctx:
        def sb(name, shape, dt=F32):
            return ctx.enter_context(nc.sbuf_tensor(name, shape, dt))

        sems = {}

        def sem(name):
            if name not in sems:
                sems[name] = ctx.enter_context(nc.semaphore("s1_" + name))
            return sems[name]

        bank = [ctx.enter_context(nc.psum_tensor(f"tb{i}", [P, 512], F32)) for i in range(8)]

        ident = sb("ident", [P, P])
        mask = sb("mask", [P, 4, P])
        bq_feat = sb("bq_feat", [P, 1])
        bk_feat = sb("bk_feat", [P, 1])
        fq_b = sb("fq_b", [P, KD])
        fk_b = sb("fk_b", [P, KD])
        fv_b = sb("fv_b", [P, D])
        nw = sb("nw", [P, KD])
        nb = sb("nb", [P, KD])
        index = sb("index", [P, 4, B * T // P], I32)
        member = sb("member", [P, 4, B * T // P])
        s_proj = [sb(f"s_proj{i}", [P, 3, D], F32R) for i in range(2)]
        s_wq = [sb(f"s_wq{i}", [P, KD, 2 * D], F32R) for i in range(2)]
        s_wk = [sb(f"s_wk{i}", [P, KD, 2 * D], F32R) for i in range(2)]
        s_wv, s_wo, s_fq, s_fk, s_fv = ([sb(f"{n}{i}", [P, KD, D], F32R) for i in range(2)]
                                        for n in ("s_wv", "s_wo", "s_fq", "s_fk", "s_fv"))
        state = sb("state", [P, PAIRS, 2 * DH])
        idx_blk = sb("idx_blk", [P, 2, 4, TB], I32)
        emb = sb("emb", [P, 2, TB, ECOL[4]])
        tables = [a[f"emb_{i}"] for i in range(4)]

        def index_block(dve, f, par):
            dve.tensor_copy(idx_blk[:, par, :, :], index[:, :, bass.ds(4 * f, 4)]).then_inc(sem("indexed"), 1)

        def gather(pool, par):
            for tile in range(TB):
                for i in range(4):
                    pool.indirect_dma_start(
                        emb[:, par, tile, ECOL[i]:ECOL[i + 1]], None, tables[i],
                        bass.IndirectOffsetOnAxis(ap=idx_blk[:, par, i, tile:tile + 1], axis=0),
                    ).then_inc(sem(f"gathered{par}"), 16)

        with ExitStack() as setup:
            def tmp(name, shape, dt=F32):
                return setup.enter_context(nc.sbuf_tensor(name, shape, dt))

            tokens = tmp("tokens", [P, B * T // P], I32)
            lower = tmp("lower", [P, 4, B * T // P])
            above = tmp("above", [P, 4, B * T // P])
            proj_t = tmp("proj_t", [P, 3, D])
            wq_rows = tmp("wq_rows", [P, KD, D])
            wk_rows = tmp("wk_rows", [P, KD, D])
            fm_q = tmp("fm_q", [P, 4, 2, DH])
            fm_k = tmp("fm_k", [P, 4, 2, DH])
            rms_col = tmp("rms_col", [P, 1])
            wv_t = tmp("wv_t", [P, KD, D])
            wo_t = tmp("wo_t", [P, KD, D])
            wo_s = tmp("wo_s", [P, KD, D])
            fq_t = tmp("fq_t", [P, KD, D])
            fk_t = tmp("fk_t", [P, KD, D])
            fv_t = tmp("fv_t", [P, KD, D])
            LOADS = 20

            with nc.Block() as block:
                loaded_splits = [([x[:, :, :] for x in dst], src[:, :, :]) for dst, src in (
                    (s_wv, wv_t), (s_fq, fq_t), (s_fk, fk_t), (s_fv, fv_t))]
                loaded_splits.append(([x[:, 0:2, :] for x in s_proj], proj_t[:, 0:2, :]))
                loaded_splits.append(([x[0:TAIL, 2, :] for x in s_proj], proj_t[0:TAIL, 2, :]))
                loaded_splits.append(([x[:, :, :] for x in s_wo], wo_s[:, :, :]))
                combined_splits = [([x[:, k, :] for x in dst], bank[2 * k + i][:, :])
                                   for k in range(KD) for i, dst in enumerate((s_wq, s_wk))]

                rows = lambda w: w.rearrange("(k p) n -> p k n", p=P)
                column = lambda v: v.rearrange("(p a) -> p a", a=1)

                @block.sync
                def _(sp):
                    sp.dma_start(tokens[:, :], a["tokens"]).then_inc(sem("tokens_loaded"), 16)
                    loads = [(wq_rows[:, :, :], rows(a["Wq"])), (wk_rows[:, :, :], rows(a["Wk"])),
                             (wv_t[:, :, :], rows(a["Wv_t"])), (fq_t[:, :, :], rows(a["q_w_t"])),
                             (fk_t[:, :, :], rows(a["k_w_t"])), (fv_t[:, :, :], rows(a["v_w_t"])),
                             (wo_t[:, :, :], rows(a["Wo_t"])),
                             (proj_t[:, 0:2, :], rows(a["proj_0_t"])), (proj_t[0:64, 2, :], a["proj_1_t"]),
                             (proj_t[64:80, 2, :], a["proj_2_t"]), (proj_t[80:84, 2, :], a["proj_3_t"]),
                             (fv_b[:, :], a["v_b"].rearrange("(a n) -> a n", a=1).broadcast_to([P, D]))]
                    for dst, src in [(fq_b, "q_b"), (fk_b, "k_b"), (nw, "norm_w"), (nb, "norm_b")]:
                        loads += [(dst[:, k:k + 1], column(a[src][k * P:(k + 1) * P])) for k in range(KD)]
                    assert len(loads) == LOADS
                    for dst, src in loads:
                        sp.dma_start(dst, src).then_inc(sem("loaded"), 16)

                @block.gpsimd
                def _(pool):
                    pool.memset(ident[:, :], 0.0).then_inc(sem("const"), 1)
                    pool.memset(mask[:, :, :], 1.0).then_inc(sem("const"), 1)
                    pool.wait_ge(sem("const"), 2)
                    pool.affine_select(out=ident[:, :], in_=ident[:, :], compare_op=ALU.not_equal, fill=1.0,
                                       base=0, pattern=[[-1, P]], channel_multiplier=1).then_inc(sem("const"), 1)
                    pool.affine_select(out=mask[:, :, :], in_=mask[:, :, :], compare_op=ALU.is_ge, fill=0.0,
                                       base=0, pattern=[[0, 4], [1, P]], channel_multiplier=-1)\
                        .then_inc(sem("const"), 1)
                    pool.wait_ge(sem("indexed"), 1)
                    gather(pool, 0)

                @block.scalar
                def _(act):
                    act.wait_ge(sem("zeroed"), 2)
                    for j in range(4):
                        rows32 = slice(DH * j, DH * j + DH)
                        act.dma_start(fm_q[rows32, j, 0, :], a["fmq_w_t"]).then_inc(sem("fm_loaded"), 16)
                        act.dma_start(fm_k[rows32, j, 0, :], a["fmk_w_t"]).then_inc(sem("fm_loaded"), 16)
                    for j in range(4):
                        rows32 = slice(DH * j, DH * j + DH)
                        for dst, src in ((rms_col, "rms_w"), (bq_feat, "fmq_b"), (bk_feat, "fmk_b")):
                            act.dma_start(dst[rows32, :], column(a[src])).then_inc(sem("by_head_loaded"), 16)
                    act.wait_ge(sem("loaded"), LOADS * 16)
                    for n, (dst, src) in enumerate(loaded_splits):
                        if n == len(loaded_splits) - 1:
                            act.wait_ge(sem("wo_scaled"), 1)
                        act.copy(dst[0], src).then_inc(sem("rounded"), 1)
                    for k in range(KD):
                        act.wait_ge(sem("feat_w"), k + 1)
                        for dst, src in combined_splits[2 * k:2 * k + 2]:
                            act.copy(dst[0], src).then_inc(sem("rounded"), 1)

                @block.vector
                def _(dve):
                    c = Chain(dve, sem("setup_dve"))
                    dve.memset(fm_q[:, :, :, :], 0.0).then_inc(sem("zeroed"), 1)
                    dve.memset(fm_k[:, :, :, :], 0.0).then_inc(sem("zeroed"), 1)
                    dve.memset(state[:, :, :], 0.0).then_inc(sem("zeroed"), 1)
                    dve.wait_ge(sem("tokens_loaded"), 16)
                    for i in range(4):
                        dve.tensor_scalar(lower[:, i, :], tokens[:, :], float(CUT[i]), 0.0,
                                          ALU.subtract, ALU.max)
                        dve.tensor_scalar(above[:, i, :], tokens[:, :], float(CUT[i]), None, ALU.is_ge)
                        ins = dve.tensor_scalar(member[:, i, :], tokens[:, :], float(CUT[i + 1]), None,
                                                ALU.is_lt)
                    c.link(ins)
                    for i in range(4):
                        ins = dve.tensor_scalar(index[:, i, :], lower[:, i, :],
                                                float(CUT[i + 1] - CUT[i] - 1), None, ALU.min)
                    c.link(ins)
                    index_block(dve, 0, 0)
                    index_block(dve, 1, 1)
                    c.link(dve.tensor_tensor(member[:, :, :], member[:, :, :], above[:, :, :], ALU.mult))
                    dve.wait_ge(sem("fm_loaded"), 8 * 16)
                    for fm in (fm_q, fm_k):
                        dve.tensor_scalar(fm[:, :, 1, :], fm[:, :, 0, :], -1.0, None, ALU.mult)\
                            .then_inc(sem("negated"), 1)
                    dve.wait_ge(sem("by_head_loaded"), 12 * 16)
                    for b in (bq_feat, bk_feat):
                        for r in (DH, 3 * DH):
                            dve.tensor_scalar(b[r:r + DH, :], b[r:r + DH, :], -1.0, None, ALU.mult)
                    dve.wait_ge(sem("loaded"), LOADS * 16)
                    dve.tensor_scalar(wo_s[:, :, :], wo_t[:, :, :], rms_col[:, 0:1], QSCALE,
                                      ALU.mult, ALU.mult).then_inc(sem("wo_scaled"), 1)
                    dve.wait_ge(sem("wo_scaled"), 1)
                    for n, (dst, src) in enumerate(loaded_splits + combined_splits):
                        dve.wait_ge(sem("rounded"), n + 1)
                        dve.tensor_tensor(dst[1], src, dst[0].bitcast(F32), ALU.subtract)

                @block.tensor
                def _(pe):
                    pe.wait_ge(sem("negated"), 2)
                    pe.wait_ge(sem("loaded"), LOADS * 16)
                    for k in range(KD):
                        for j in range(KD):
                            pe.matmul(bank[2 * k][:, j * 256:j * 256 + 256], wq_rows[:, j, k * P:k * P + P],
                                      fm_q[:, :, :, :].rearrange("p a b c -> p (a b c)"), start=True, stop=True)
                            last = pe.matmul(bank[2 * k + 1][:, j * 256:j * 256 + 256],
                                             wk_rows[:, j, k * P:k * P + P],
                                             fm_k[:, :, :, :].rearrange("p a b c -> p (a b c)"),
                                             start=True, stop=True)
                        last.then_inc(sem("feat_w"), 1)

        emb_t = [sb(f"emb_t{i}", [P, 3, NB], F32R) for i in range(2)]
        h_sb = sb("h_sb", [P, 2, TB, D])
        stats = sb("stats", [P, TB, 6])
        both = sb("both", [P, 3, TB])
        mean = sb("mean", [P, TB])
        var = sb("var", [P, TB])
        veps = sb("veps", [P, 2, TB])
        scale_1, shift_1 = sb("scale_1", [P, TB]), sb("shift_1", [P, TB])
        scale_2, shift_2 = sb("scale_2", [P, 2, TB]), sb("shift_2", [P, 2, TB])
        x1 = sb("x1", [P, TB, D])
        x1_t = [sb(f"x1_t{i}", [P, KD, NB], F32R) for i in range(2)]
        feat_q = sb("feat_q", [P, 2, PAIRS, NB])
        feat_k = sb("feat_k", [P, 2, PAIRS, NB])
        v_sb = sb("v_sb", [P, 2, TB, D])
        k_tok = sb("k_tok", [P, 2, 512])
        attn_t = sb("attn_t", [P, H, P])
        o_t = sb("o_t", [P, D])
        o_sb = sb("o_sb", [P, TB, D])
        o_sq = sb("o_sq", [P, D])
        ss = sb("ss", [P, TB * H])
        rrms = sb("rrms", [P, TB * H])
        o_n = sb("o_n", [P, TB, D])
        o_nt = [sb(f"o_nt{i}", [P, KD, NB], F32R) for i in range(2)]
        h1 = sb("h1", [P, TB, D])
        x2 = sb("x2", [P, TB, D])
        resid = sb("resid", [P, TB, D])
        xn = sb("xn", [P, TB, D])
        xn_f = sb("xn_f", [P, KD, NB])
        xn_t = [sb(f"xn_t{i}", [P, KD, NB], F32R) for i in range(2)]
        newton = sb("newton", [P, TB * H])
        hi = sb("hi", [P, 4, NB], F32R)
        lo = sb("lo", [P, 4, NB], F32R)
        v2 = sb("v2", [P, TB, D])

        BLOCKS = B * E

        def turns(run):
            def all_turns(eng):
                run(0, 0, 0)
                run(1, 0, 1)
                with eng.Fori(0, (BLOCKS - E) // E) as t:
                    for u in range(2, E + 2):
                        run(4 * t + u, t, u)
                for u in (2, 3):
                    run(BLOCKS - E + u, BLOCKS // E - 1, u)
            return all_turns

        def place(t, u):
            return t + u // E, u % E

        def is_last(n):
            return isinstance(n, int) and n == BLOCKS - 1

        FRONT_LINKS, LINKS, OLD_LINKS, LAST_LINKS = 15, 50, 16, 35
        with nc.Block() as block:
            @block.gpsimd
            def _(pool):
                def residual(n):
                    pool.wait_ge(sem("x2_ready"), n + 1)
                    pool.tensor_tensor(resid[:, :, :], h1[:, :, :], x2[:, :, :], ALU.add)\
                        .then_inc(sem("resid_ready"), 1)

                def turn(n, t, u):
                    if not (isinstance(n, int) and n == 0):
                        residual(n - 1)
                    if not (isinstance(n, int) and n + 2 >= BLOCKS):
                        gather(pool, u % 2)

                gather(pool, 1)
                pool.wait_ge(sem("indexed"), 3)
                turns(turn)(pool)
                residual(BLOCKS - 1)

            @block.sync
            def _(sp):
                def turn(n, t, u):
                    b, e = place(t, u)
                    cols = slice(e * NB, e * NB + NB)
                    sp.wait_ge(sem("resid_ready"), n + 1)
                    sp.dma_start(scr["resid"][bass.ds(n, 1)].rearrange("a p t d -> (a p) t d"),
                                 resid[:, :, :]).then_inc(sem("resid_stored"), 16)
                    for j in range(4):
                        row = 4 * b + 2 * (j % 2) + j // 2
                        sp.wait_ge(sem("hi_ready"), 4 * n + j + 1)
                        sp.dma_start(scr["hi"][bass.ds(row, 1), :, cols].rearrange("a p c -> (a p) c"),
                                     hi[:, j, :].bitcast(F32)).then_inc(sem("hi_stored"), 16)
                        sp.wait_ge(sem("lo_ready"), 4 * n + j + 1)
                        sp.dma_start(scr["lo"][bass.ds(row, 1), :, cols].rearrange("a p c -> (a p) c"),
                                     lo[:, j, :].bitcast(F32)).then_inc(sem("lo_stored"), 16)
                    sp.wait_ge(sem("v2_ready"), n + 1)
                    for k in range(KD):
                        sp.dma_start(scr["v"][bass.ds(8 * b + 4 * k + e, 1)].rearrange("a p t d -> (a p) t d"),
                                     v2[:, :, k * P:k * P + P]).then_inc(sem("v2_stored"), 16)
                turns(turn)(sp)
                sp.wait_ge(sem("resid_stored"), 16 * 4 * B)
                sp.wait_ge(sem("hi_stored"), 64 * 4 * B)
                sp.wait_ge(sem("lo_stored"), 64 * 4 * B)
                sp.wait_ge(sem("v2_stored"), 32 * 4 * B)

            @block.tensor
            def _(pe):
                def front_a(f, par, first):
                    pe.wait_ge(sem("masked"), f + 1)
                    if not first:
                        pe.wait_ge(sem("exp_done"), 8 * f)
                        pe.wait_ge(sem("v_ready"), f)
                    for k in range(3):
                        w = P if k < 2 else TAIL
                        for tile in range(TB):
                            mm = pe.transpose(bank[k][0:w, tile * P:tile * P + P],
                                              emb[:, par, tile, k * P:k * P + w], ident[:, :])
                        mm.then_inc(sem("emb_t_done"), 1)

                def front_b(f):
                    pe.wait_ge(sem("emb_t_ready"), f + 1)
                    for tile in range(TB):
                        out = bank[tile // 2][:, (tile % 2) * D:(tile % 2) * D + D]
                        for k in range(3):
                            w = P if k < 2 else TAIL
                            mm = split_product(pe, out, [x[0:w, k, tile * P:tile * P + P] for x in emb_t],
                                               [x[0:w, k, :] for x in s_proj], k == 0, k == 2)
                        if tile % 2:
                            mm.then_inc(sem("h_done"), 1)

                def front_c(f):
                    pe.wait_ge(sem("x1_ready"), f + 1)
                    if not (isinstance(f, int) and f < 2):
                        pe.wait_ge(sem("lo_ready"), 4 * (f - 1))
                        pe.wait_ge(sem("v2_ready"), f - 1)
                    for k in range(KD):
                        for tile in range(TB):
                            mm = pe.transpose(bank[k][:, tile * P:tile * P + P], x1[:, tile, k * P:k * P + P],
                                              ident[:, :])
                        mm.then_inc(sem("x1_t_done"), 1)

                def front_d(f, part):
                    if part == "queries":
                        pe.wait_ge(sem("x1_t_ready"), f + 1)
                    for j in {"queries": range(PAIRS), "keys": range(PAIRS, 2 * PAIRS), "values": ()}[part]:
                        if j >= 3:
                            pe.wait_ge(sem("exp_done"), 8 * f + j - 2)
                        w = s_wq if j < PAIRS else s_wk
                        cols = slice(j % PAIRS * P, j % PAIRS * P + P)
                        for k in range(KD):
                            mm = split_product(pe, bank[j % 3][:, :], [x[:, k, cols] for x in w],
                                               [x[:, k, :] for x in x1_t], k == 0, k == KD - 1)
                        mm.then_inc(sem("y_done"), 1)
                    for half in range(2) if part == "values" else ():
                        pe.wait_ge(sem("exp_done"), 8 * f + 6 + half)
                        for tile in (2 * half, 2 * half + 1):
                            out = bank[(8 + half) % 3][:, (tile % 2) * D:(tile % 2) * D + D]
                            for k in range(KD):
                                mm = split_product(pe, out, [x[:, k, tile * P:tile * P + P] for x in x1_t],
                                                   [x[:, k, :] for x in s_wv], k == 0, k == KD - 1)
                        mm.then_inc(sem("v_done"), 1)

                def chunk_scores(n, e, c):
                    par = e % 2
                    if c == 0:
                        pe.wait_ge(sem("exp_done"), 8 * n + 8)
                    else:
                        pe.wait_ge(sem("k_tok_ready"), 4 * n + c)
                        pe.wait_ge(sem("attn_ready"), 8 * n + 2 * c)
                    cols = slice(c * P, c * P + P)
                    for pair in range(PAIRS):
                        mm = pe.transpose(bank[3][:, pair * P:pair * P + P], feat_k[:, par, pair, cols],
                                          ident[:, :])
                    mm.then_inc(sem("k_tok_done"), 1)
                    for h in range(H):
                        r = slice(64 * (h % 2), 64 * (h % 2) + 64)
                        mm = pe.matmul(bank[4 + h % 2][:, (h // 2) * P:(h // 2) * P + P],
                                       feat_k[r, par, h // 2, cols], feat_q[r, par, h // 2, cols],
                                       start=True, stop=True)
                        if h >= H - 2:
                            mm.then_inc(sem("attn_done"), 1)

                def chunk_outputs(n, b, e, c):
                    par = e % 2
                    if c == 0:
                        pe.wait_ge(sem("v_ready"), n + 1)
                    else:
                        pe.wait_ge(sem("o_ready"), 4 * n + c)
                    pe.wait_ge(sem("attn_ready"), 8 * n + 2 * c + 2)
                    pe.wait_ge(sem("k_tok_ready"), 4 * n + c + 1)
                    pe.wait_ge(sem("state_ready"), 17 * b + 4 * e + c + 1)
                    for m in range(KD):
                        out = bank[6][:, m * P:m * P + P]
                        for i in range(2):
                            pe.matmul(out[64 * i:64 * i + 64, :], state[:, 2 * m + i, :],
                                      feat_q[:, par, 2 * m + i, c * P:c * P + P], start=True, stop=False)
                        for i in range(4):
                            h = 4 * m + i
                            mm = pe.matmul(out[DH * i:DH * i + DH, :], v_sb[:, par, c, h * DH:h * DH + DH],
                                           attn_t[:, (h % 2) * 4 + h // 2, :], start=False, stop=True)
                    mm.then_inc(sem("o_t_done"), 1)
                    for pair in range(PAIRS):
                        for i in range(2):
                            h = 2 * pair + i
                            mm = pe.matmul(bank[7][64 * i:64 * i + 64, pair * DH:pair * DH + DH],
                                           k_tok[:, c % 2, 64 * h:64 * h + 64],
                                           v_sb[:, par, c, h * DH:h * DH + DH], start=True, stop=True)
                    mm.then_inc(sem("state_done"), 1)

                def chunk_tokens(n, c):
                    pe.wait_ge(sem("o_t_ready"), 4 * n + c + 1)
                    if c:
                        pe.wait_ge(sem("o_ready"), 4 * n + c)
                    for m in range(KD):
                        mm = pe.transpose(bank[6][:, D + m * P:D + m * P + P], o_t[:, m * P:m * P + P],
                                          ident[:, :])
                    mm.then_inc(sem("o_done"), 1)

                def back_f(n):
                    pe.wait_ge(sem("o_n_ready"), n + 1)
                    for k in range(KD):
                        for tile in range(TB):
                            mm = pe.transpose(bank[4 + k][:, tile * P:tile * P + P],
                                              o_n[:, tile, k * P:k * P + P], ident[:, :])
                        mm.then_inc(sem("o_nt_done"), 1)

                def back_g(n, b, e):
                    pe.wait_ge(sem("o_nt_ready"), n + 1)
                    pe.wait_ge(sem("o_ready"), 4 * n + 4)
                    pe.wait_ge(sem("state_ready"), 17 * b + 4 * e + 5)
                    for tile in range(TB):
                        out = bank[6 + tile // 2][:, (tile % 2) * D:(tile % 2) * D + D]
                        for k in range(KD):
                            mm = split_product(pe, out, [x[:, k, tile * P:tile * P + P] for x in o_nt],
                                               [x[:, k, :] for x in s_wo], k == 0, k == KD - 1)
                        if tile % 2:
                            mm.then_inc(sem("attn_out_done"), 1)

                def back_h(n, e, front):
                    pe.wait_ge(sem("xn_ready"), n + 1)
                    for k in range(NK[e]):
                        if k and front:
                            pe.wait_ge(sem("h_ready"), 2 * n + 5)
                        for tile in range(TB):
                            mm = pe.transpose(bank[2 - 2 * k][:, tile * P:tile * P + P],
                                              xn[:, tile, k * P:k * P + P], ident[:, :])
                        mm.then_inc(sem("xn_t_done"), 1)

                def back_i(n, b, e, front):
                    pe.wait_ge(sem("xn_t_ready"), 5 * b + NKSUM[e + 1])
                    if front:
                        pe.wait_ge(sem("h_ready"), 2 * n + 6)
                    for j in range(4):
                        if j == 3:
                            pe.wait_ge(sem("lo_ready"), 4 * n + 1)
                        w = s_fq if j < 2 else s_fk
                        cols = slice(j % 2 * P, j % 2 * P + P)
                        for k, m in enumerate(MK[e]):
                            mm = split_product(pe, bank[(j + 1) % 3][:, :], [x[0:m, k, cols] for x in w],
                                               [x[0:m, k, :] for x in xn_t], k == 0, k == NK[e] - 1)
                        mm.then_inc(sem("qk_done"), 1)
                    for half in range(2):
                        pe.wait_ge(sem("lo_ready"), 4 * n + 2 + half)
                        for tile in (2 * half, 2 * half + 1):
                            out = bank[2 - 2 * half][:, (tile % 2) * D:(tile % 2) * D + D]
                            for k, m in enumerate(MK[e]):
                                mm = split_product(pe, out, [x[0:m, k, tile * P:tile * P + P] for x in xn_t],
                                                   [x[0:m, k, :] for x in s_fv], k == 0, k == NK[e] - 1)
                        mm.then_inc(sem("v2_done"), 1)

                def turn(n, t, u):
                    (b, e), (old_b, old_e) = place(t, u), place(t, u - 1)
                    old = not (isinstance(n, int) and n == 0)
                    new = not is_last(n)
                    chunk_scores(n, e, 0)
                    if new:
                        front_a(n + 1, (e + 1) % 2, False)
                    chunk_outputs(n, b, e, 0)
                    chunk_scores(n, e, 1)
                    chunk_tokens(n, 0)
                    if new:
                        front_b(n + 1)
                    chunk_outputs(n, b, e, 1)
                    chunk_scores(n, e, 2)
                    chunk_tokens(n, 1)
                    if old:
                        back_h(n - 1, old_e, new)
                    chunk_outputs(n, b, e, 2)
                    chunk_scores(n, e, 3)
                    chunk_tokens(n, 2)
                    if old:
                        back_i(n - 1, old_b, old_e, new)
                    if new:
                        front_c(n + 1)
                    chunk_outputs(n, b, e, 3)
                    if new:
                        front_d(n + 1, "queries")
                    chunk_tokens(n, 3)
                    if new:
                        front_d(n + 1, "keys")
                    back_f(n)
                    if new:
                        front_d(n + 1, "values")
                    back_g(n, b, e)

                front_a(0, 0, True)
                front_b(0)
                front_c(0)
                for part in ("queries", "keys", "values"):
                    front_d(0, part)
                turns(turn)(pe)
                back_h(BLOCKS - 1, E - 1, False)
                back_i(BLOCKS - 1, B - 1, E - 1, False)

            @block.scalar
            def _(act):
                def normalize(name, out, src, scale, shift):
                    for tile in range(TB):
                        ins = act.activation(out[:, tile, :], src[:, tile, :], ACT.Identity,
                                             scale=scale[:, tile:tile + 1], bias=shift[:, tile:tile + 1])
                    ins.then_inc(sem(name + "_ready"), 1)

                def make_x1(n, par):
                    act.wait_ge(sem("x1_stats"), n + 1)
                    normalize("x1", x1, h_sb[:, par], scale_1, shift_1)

                def make_x2(n):
                    act.wait_ge(sem("x2_stats"), n + 1)
                    normalize("x2", x2, h1, scale_2[:, 0], shift_2[:, 0])

                def make_xn(n):
                    normalize("xn", xn, h1, scale_2[:, 1], shift_2[:, 1])

                def front_a(f):
                    for k in range(3):
                        w = P if k < 2 else TAIL
                        act.wait_ge(sem("emb_t_done"), 3 * f + k + 1)
                        act.copy(emb_t[0][0:w, k, :], bank[k][0:w, :]).then_inc(sem("emb_t_rounded"), 1)

                def front_b(f, par):
                    for half in range(2):
                        act.wait_ge(sem("h_done"), 2 * f + half + 1)
                        act.mul(h_sb[:, par, 2 * half:2 * half + 2, :].rearrange("p a b -> p (a b)"),
                                bank[half][:, :], float(D) ** 0.5).then_inc(sem("h_ready"), 1)

                def front_c(f):
                    for k in range(KD):
                        act.wait_ge(sem("x1_t_done"), 2 * f + k + 1)
                        act.copy(x1_t[0][:, k, :], bank[k][:, :]).then_inc(sem("x1_t_rounded"), 1)

                def front_d(f, par, part):
                    for j in {"queries": range(PAIRS), "keys": range(PAIRS, 2 * PAIRS), "values": ()}[part]:
                        act.wait_ge(sem("y_done"), 8 * f + j + 1)
                        feat, b = (feat_q, bq_feat) if j < PAIRS else (feat_k, bk_feat)
                        act.activation(feat[:, par, j % PAIRS, :], bank[j % 3][:, :], ACT.Exp,
                                       bias=b[:, 0:1]).then_inc(sem("exp_done"), 1)
                    for half in range(2) if part == "values" else ():
                        act.wait_ge(sem("v_done"), 2 * f + half + 1)
                        ins = act.copy(v_sb[:, par, 2 * half:2 * half + 2, :]
                                       .rearrange("p a b -> p (a b)"), bank[(8 + half) % 3][:, :])
                    if part == "values":
                        ins.then_inc(sem("v_ready"), 1)

                def keys(n, c):
                    act.wait_ge(sem("k_tok_done"), 4 * n + c + 1)
                    act.copy(k_tok[:, c % 2, :], bank[3][:, :]).then_inc(sem("k_tok_ready"), 1)

                def outputs(n, c):
                    act.wait_ge(sem("o_t_done"), 4 * n + c + 1)
                    act.copy(o_t[:, :], bank[6][:, 0:D]).then_inc(sem("o_t_ready"), 1)

                def by_token(n, c):
                    act.wait_ge(sem("o_done"), 4 * n + c + 1)
                    act.copy(o_sb[:, c, :], bank[6][:, D:2 * D]).then_inc(sem("o_ready"), 1)

                def back_f(n):
                    for k in range(KD):
                        act.wait_ge(sem("o_nt_done"), 2 * n + k + 1)
                        act.copy(o_nt[0][:, k, :], bank[4 + k][:, :]).then_inc(sem("o_nt_rounded"), 1)

                def back_h(n, b, e):
                    for k, m in enumerate(MK[e]):
                        act.wait_ge(sem("xn_t_done"), 5 * b + NKSUM[e] + k + 1)
                        act.activation(xn_f[0:m, k, :], bank[2 - 2 * k][0:m, :], ACT.Identity,
                                       scale=nw[0:m, k:k + 1], bias=nb[0:m, k:k + 1])\
                            .then_inc(sem("xn_f_ready"), 1)
                        act.wait_ge(sem("xn_f_ready"), 5 * b + NKSUM[e] + k + 1)
                        act.copy(xn_t[0][0:m, k, :], xn_f[0:m, k, :]).then_inc(sem("xn_t_rounded"), 1)

                def back_i(n):
                    if not (isinstance(n, int) and n == 0):
                        act.wait_ge(sem("hi_stored"), 64 * n)
                    for j in range(4):
                        act.wait_ge(sem("qk_done"), 4 * n + j + 1)
                        b = fq_b if j < 2 else fk_b
                        act.activation(hi[:, j, :], bank[(j + 1) % 3][:, :], ACT.Identity,
                                       bias=b[:, j % 2:j % 2 + 1]).then_inc(sem("hi_ready"), 1)

                def turn(n, t, u):
                    par = (u + 1) % 2
                    old = not (isinstance(n, int) and n == 0)
                    new = not is_last(n)
                    if new:
                        front_a(n + 1)
                    keys(n, 0)
                    outputs(n, 0)
                    keys(n, 1)
                    by_token(n, 0)
                    if new:
                        front_b(n + 1, par)
                    if old:
                        make_x2(n - 1)
                    outputs(n, 1)
                    keys(n, 2)
                    if old:
                        make_xn(n - 1)
                    by_token(n, 1)
                    if old:
                        back_h(n - 1, *place(t, u - 1))
                    outputs(n, 2)
                    keys(n, 3)
                    if new:
                        make_x1(n + 1, par)
                    by_token(n, 2)
                    if old:
                        back_i(n - 1)
                    if new:
                        front_c(n + 1)
                    outputs(n, 3)
                    if new:
                        front_d(n + 1, par, "queries")
                    by_token(n, 3)
                    if new:
                        front_d(n + 1, par, "keys")
                    back_f(n)
                    if new:
                        front_d(n + 1, par, "values")

                front_a(0)
                front_b(0, 0)
                make_x1(0, 0)
                front_c(0)
                for part in ("queries", "keys", "values"):
                    front_d(0, 0, part)
                turns(turn)(act)
                make_x2(BLOCKS - 1)
                make_xn(BLOCKS - 1)
                back_h(BLOCKS - 1, B - 1, E - 1)
                back_i(BLOCKS - 1)

            @block.vector
            def _(dve):
                def moments(c, src):
                    for tile in range(TB):
                        ins = dve.bn_stats(stats[:, tile, :], src[:, tile, :])
                    c.link(ins)
                    dve.tensor_tensor(both[:, 0, :], stats[:, :, 1], stats[:, :, 4], ALU.add)
                    dve.tensor_tensor(both[:, 1, :], stats[:, :, 1], stats[:, :, 4], ALU.subtract)
                    c.link(dve.tensor_tensor(both[:, 2, :], stats[:, :, 2], stats[:, :, 5], ALU.add))
                    dve.tensor_scalar(mean[:, :], both[:, 0, :], -0.5, None, ALU.mult)
                    dve.tensor_scalar(both[:, 2, :], both[:, 2, :], 1.0 / D, None, ALU.mult)
                    c.link(dve.tensor_tensor(both[:, 1, :], both[:, 1, :], both[:, 1, :], ALU.mult))
                    c.link(dve.scalar_tensor_tensor(var[:, :], both[:, 1, :], 0.25, both[:, 2, :],
                                                    ALU.mult, ALU.add))

                def layernorm(c, src):
                    moments(c, src)
                    c.link(dve.tensor_scalar(veps[:, 0, :], var[:, :], EPS, None, ALU.add))
                    rsqrt(dve, c, scale_1[:, :], veps[:, 0, :], newton[:, 0:TB])
                    dve.tensor_tensor(shift_1[:, :], mean[:, :], scale_1[:, :], ALU.mult)\
                        .then_inc(sem("x1_stats"), 1)

                def two_layernorms(c, src):
                    moments(c, src)
                    dve.tensor_scalar(veps[:, 0, :], var[:, :], EPS, None, ALU.add)
                    c.link(dve.tensor_scalar(veps[:, 1, :], var[:, :], 1.0 + EPS, EPS * EPS,
                                             ALU.mult, ALU.add))
                    flat = lambda x: x[:, :, :].rearrange("p a b -> p (a b)")
                    rsqrt(dve, c, flat(scale_2), flat(veps), newton[:, 0:2 * TB])
                    dve.tensor_tensor(shift_2[:, :, :], scale_2[:, :, :],
                                      mean[:, :].unsqueeze(1).broadcast_to([P, 2, TB]), ALU.mult)\
                        .then_inc(sem("x2_stats"), 1)

                def front_a(f, par, count):
                    dve.wait_ge(sem(f"gathered{par}"), 256 * count)
                    for i in range(4):
                        out = emb[:, par, :, ECOL[i]:ECOL[i + 1]]
                        m = member[:, i, bass.ds(4 * f, 4)].unsqueeze(2).broadcast_to([P, TB, DE[i]])
                        ins = dve.tensor_tensor(out, out, m, ALU.mult)
                    ins.then_inc(sem("masked"), 1)

                def front_a2(f):
                    for k in range(3):
                        w = P if k < 2 else TAIL
                        dve.wait_ge(sem("emb_t_rounded"), 3 * f + k + 1)
                        ins = dve.tensor_tensor(emb_t[1][0:w, k, :], bank[k][0:w, :],
                                                emb_t[0][0:w, k, :].bitcast(F32), ALU.subtract)
                    ins.then_inc(sem("emb_t_ready"), 1)

                def front_b(c, f, par):
                    dve.wait_ge(sem("h_ready"), 2 * f + 2)
                    layernorm(c, h_sb[:, par])

                def front_c(f):
                    for k in range(KD):
                        dve.wait_ge(sem("x1_t_rounded"), 2 * f + k + 1)
                        ins = dve.tensor_tensor(x1_t[1][:, k, :], bank[k][:, :],
                                                x1_t[0][:, k, :].bitcast(F32), ALU.subtract)
                    ins.then_inc(sem("x1_t_ready"), 1)

                def scores(n, e, c):
                    for g in range(2):
                        dve.wait_ge(sem("attn_done"), 8 * n + 2 * c + g + 1)
                        dve.tensor_tensor(attn_t[:, 4 * g:4 * g + 4, :],
                                          bank[4 + g][:, :].rearrange("p (h c) -> p h c", h=4),
                                          mask[:, :, :], ALU.mult).then_inc(sem("attn_ready"), 1)

                def new_state(n, e, c):
                    dve.wait_ge(sem("state_done"), 4 * n + c + 1)
                    ps = bank[7][:, 0:PAIRS * DH].rearrange("p (a b) -> p a b", a=PAIRS)
                    dve.tensor_tensor(state[0:64, :, 0:DH], state[0:64, :, 0:DH], ps[0:64, :, :], ALU.add)
                    dve.tensor_tensor(state[64:128, :, DH:64], state[64:128, :, DH:64],
                                      ps[64:128, :, :], ALU.add).then_inc(sem("state_ready"), 1)

                def squares(chain, n, c):
                    dve.wait_ge(sem("o_ready"), 4 * n + c + 1)
                    chain.link(dve.tensor_tensor(o_sq[:, :], o_sb[:, c, :], o_sb[:, c, :], ALU.mult))
                    chain.link(dve.tensor_reduce(ss[:, c * H:c * H + H],
                                                 o_sq[:, :].rearrange("p (h d) -> p h d", h=H), AX.X, ALU.add))

                def rms(chain, n):
                    chain.link(dve.tensor_scalar(ss[:, :], ss[:, :], QSCALE * QSCALE / DH, EPS,
                                                 ALU.mult, ALU.add))
                    rsqrt(dve, chain, rrms[:, :], ss[:, :], newton[:, :])
                    dve.tensor_tensor(o_n[:, :, :].rearrange("p t (h d) -> p (t h) d", h=H),
                                      o_sb[:, :, :].rearrange("p t (h d) -> p (t h) d", h=H),
                                      rrms[:, :].unsqueeze(2).broadcast_to([P, TB * H, DH]), ALU.mult)\
                        .then_inc(sem("o_n_ready"), 1)

                def back_f(n):
                    for k in range(KD):
                        dve.wait_ge(sem("o_nt_rounded"), 2 * n + k + 1)
                        ins = dve.tensor_tensor(o_nt[1][:, k, :], bank[4 + k][:, :],
                                                o_nt[0][:, k, :].bitcast(F32), ALU.subtract)
                    ins.then_inc(sem("o_nt_ready"), 1)

                def back_g(chain, n, par):
                    if not (isinstance(n, int) and n == 0):
                        dve.wait_ge(sem("resid_ready"), n)
                    for half in range(2):
                        dve.wait_ge(sem("attn_out_done"), 2 * n + half + 1)
                        ins = dve.tensor_tensor(h1[:, 2 * half:2 * half + 2, :]
                                                .rearrange("p a b -> p (a b)"), bank[6 + half][:, :],
                                                h_sb[:, par, 2 * half:2 * half + 2, :]
                                                .rearrange("p a b -> p (a b)"), ALU.add)
                    chain.link(ins)

                def back_g2(chain, n):
                    if not (isinstance(n, int) and n == 0):
                        dve.wait_ge(sem("resid_stored"), 16 * n)
                    two_layernorms(chain, h1)

                def back_h(b, e):
                    for k, m in enumerate(MK[e]):
                        dve.wait_ge(sem("xn_t_rounded"), 5 * b + NKSUM[e] + k + 1)
                        dve.tensor_tensor(xn_t[1][0:m, k, :], xn_f[0:m, k, :],
                                          xn_t[0][0:m, k, :].bitcast(F32), ALU.subtract)\
                            .then_inc(sem("xn_t_ready"), 1)

                def back_i(n):
                    if not (isinstance(n, int) and n == 0):
                        dve.wait_ge(sem("lo_stored"), 64 * n)
                        dve.wait_ge(sem("v2_stored"), 32 * n)
                    for j in range(4):
                        dve.wait_ge(sem("hi_ready"), 4 * n + j + 1)
                        b = fq_b if j < 2 else fk_b
                        dve.scalar_tensor_tensor(lo[:, j, :], bank[(j + 1) % 3][:, :],
                                                 b[:, j % 2:j % 2 + 1], hi[:, j, :].bitcast(F32),
                                                 ALU.add, ALU.subtract).then_inc(sem("lo_ready"), 1)
                    for half in range(2):
                        dve.wait_ge(sem("v2_done"), 2 * n + half + 1)
                        ins = dve.tensor_tensor(v2[:, 2 * half:2 * half + 2, :],
                                                bank[2 - 2 * half][:, :].rearrange("p (a b) -> p a b", a=2),
                                                fv_b[:, :].unsqueeze(1).broadcast_to([P, 2, D]), ALU.add)
                    ins.then_inc(sem("v2_ready"), 1)

                def turn(n, t, u):
                    (b, e), (old_b, old_e) = place(t, u), place(t, u - 1)
                    old = not (isinstance(n, int) and n == 0)
                    new = not is_last(n)
                    chain = Chain(dve, sem("dve_order"), FRONT_LINKS + (LINKS * n - OLD_LINKS if old else 0))
                    if old:
                        back_g(chain, n - 1, old_e % 2)
                    if e == 0:
                        dve.wait_ge(sem("attn_done"), 8 * n + 1)
                        dve.memset(state[:, :, :], 0.0).then_inc(sem("state_ready"), 1)
                        dve.wait_ge(sem("state_ready"), 17 * b + 1)
                    if not (isinstance(n, int) and n + 2 >= BLOCKS):
                        index_block(dve, n + 2, e % 2)
                    scores(n, e, 0)
                    if old:
                        back_g2(chain, n - 1)
                    if new:
                        front_a2(n + 1)
                    new_state(n, e, 0)
                    scores(n, e, 1)
                    squares(chain, n, 0)
                    new_state(n, e, 1)
                    scores(n, e, 2)
                    squares(chain, n, 1)
                    if new:
                        front_b(chain, n + 1, (e + 1) % 2)
                    if old:
                        back_h(old_b, old_e)
                    new_state(n, e, 2)
                    scores(n, e, 3)
                    squares(chain, n, 2)
                    if old:
                        back_i(n - 1)
                    if new:
                        front_c(n + 1)
                    new_state(n, e, 3)
                    if not (isinstance(n, int) and n + 2 >= BLOCKS):
                        front_a(n + 2, e % 2, 2 * t + u // 2 + 2)
                    squares(chain, n, 3)
                    rms(chain, n)
                    back_f(n)
                    assert not (old and new) or chain.k == LINKS, chain.k
                    assert old or chain.k == LINKS - OLD_LINKS, chain.k
                    assert new or chain.k == LAST_LINKS, chain.k

                chain = Chain(dve, sem("dve_order"))
                front_a(0, 0, 1)
                front_a2(0)
                front_b(chain, 0, 0)
                front_c(0)
                front_a(1, 1, 1)
                assert chain.k == FRONT_LINKS, chain.k
                turns(turn)(dve)
                n = BLOCKS - 1
                chain = Chain(dve, sem("dve_order"), FRONT_LINKS + LINKS * n - OLD_LINKS + LAST_LINKS)
                back_g(chain, n, n % 2)
                back_g2(chain, n)
                back_h(B - 1, E - 1)
                back_i(n)


def attention_stage(nc, a, scr, prefetch):
    KT = T // P
    QB = T // 512
    SCALE = float(D) ** -0.5
    RING = 8
    BY_PE = [10, 13, 14, 15]
    BY_POOL = [k for k in range(KT) if k not in BY_PE]
    NADD = len(BY_POOL) - 1
    HEADS = B * H
    U = 4
    NMAX = KT * QB
    MAX_TILES = 15
    ORDER = "ASASAVSASP"
    ROWS = 3 * DH
    NEG = ROWS + 2

    max_end = [min(NMAX, -(-NMAX * (kt + 1) // MAX_TILES)) for kt in range(KT)]
    seq, seq_last = [], []
    for kt in range(KT):
        for j in range(QB):
            seq.append(("scores", kt, j))
            seq_last.append(("scores", kt, j))
            for r in range(QB):
                if j == 1 and kt == next(k for k in range(KT) if max_end[k] >= KT * (r + 1)) + 1:
                    seq.append(("maxima", r))
    NU = len(seq)
    assert NU == KT * QB + QB

    def last_in_bank(i):
        return max(p for p in range(NU) if p % 3 == i % 3)

    ctx = ExitStack()
    with ctx:
        def sb(name, shape, dt=F32):
            return ctx.enter_context(nc.sbuf_tensor(name, shape, dt))

        sems = {}

        def sem(name):
            if name not in sems:
                sems[name] = ctx.enter_context(nc.semaphore("s2_" + name))
            return sems[name]

        bank = [ctx.enter_context(nc.psum_tensor(f"ab{i}", [P, 512], F32)) for i in range(8)]
        max_bank, score_bank, out_bank, sum_bank = bank[0:3], bank[3:6], bank[6], bank[7]
        qs = [sb(f"qs{i}", [P, T], F32R) for i in range(U)]
        ks = [sb(f"ks{i}", [P, T], F32R) for i in range(U)]
        vs = [sb(f"vs{i}", [P, KT, DH]) for i in range(U)]
        probs = sb("probs", [P, RING, T])
        prob_sum = sb("prob_sum", [P, 2, T])
        ones = sb("ones", [P, DH])
        ident2 = sb("ident2", [P, P])
        one_rows = sb("one_rows", [2, 512])
        part_max = sb("part_max", [P, 2, KT, QB])
        neg_max = sb("neg_max", [P, 2, KT])
        neg = sb("neg", [P, 2, 2, 4], F32R)
        neg_rows = sb("neg_rows", [8, QB, P], F32R)
        o_raw = sb("o_raw", [P, 512])
        sums_t = sb("sums_t", [P, 512])
        inv = sb("inv", [P, 512 // DH])
        inv_wide = sb("inv_wide", [P, 512 // DH, DH])
        inv_rows = sb("inv_rows", [P, 512])
        o_out = sb("o_out", [P, 512])

        with nc.Block() as block:
            @block.vector
            def _(dve):
                dve.memset(ones[:, :], 1.0)
                dve.memset(one_rows[:, :], 1.0).then_inc(sem("one_rows"), 1)
                dve.wait_ge(sem("one_rows"), 1)
                for u in range(U):
                    for j in range(QB):
                        dve.tensor_copy(ks[u][ROWS:NEG, j * 512:j * 512 + 512], one_rows[:, :])

            @block.gpsimd
            def _(pool):
                pool.memset(ident2[:, :], 0.0).then_inc(sem("zero"), 1)
                pool.wait_ge(sem("zero"), 1)
                pool.affine_select(out=ident2[:, :], in_=ident2[:, :], compare_op=ALU.not_equal, fill=1.0,
                                   base=0, pattern=[[-1, P]], channel_multiplier=1)

        def turns(run):
            def all_turns(eng):
                run(0, 0, 0, False)
                with eng.Fori(0, (HEADS - U) // U) as t:
                    for u in range(1, U + 1):
                        run(4 * t + u, t, u, False)
                for u in range(1, U):
                    t = HEADS // U - 1
                    run(4 * t + u, t, u, u == U - 1)
            return all_turns

        with nc.Block() as block:
            @block.sync
            def _(sp):
                def load(t, u):
                    cols = slice(DH * u, DH * u + DH)
                    for dst, part, kind in ((qs[u][0:32, :], "hi", 0), (qs[u][32:64, :], "hi", 0),
                                            (qs[u][64:96, :], "lo", 0), (ks[u][0:32, :], "hi", 1),
                                            (ks[u][32:64, :], "lo", 1), (ks[u][64:96, :], "hi", 1)):
                        sp.dma_start(dst.bitcast(F32), scr[part][bass.ds(2 * t + kind, 1), cols, :]
                                     .rearrange("a p c -> (a p) c")).then_inc(sem(f"qk_loaded{u}"), 16)
                    for e in range(E):
                        sp.dma_start(vs[u][:, TB * e:TB * e + TB, :],
                                     scr["v"][bass.ds(4 * t + e, 1), :, :, cols]
                                     .rearrange("a p t d -> (a p) t d")).then_inc(sem(f"v_loaded{u}"), 16)

                def store(g, t, u):
                    sp.wait_ge(sem("out_ready"), g + 1)
                    for j in range(QB):
                        sp.dma_start(scr["attn"][bass.ds(4 * t + j, 1), DH * u:DH * u + DH, :]
                                     .rearrange("a d q -> (a d) q"), o_out[DH * j:DH * j + DH, :])\
                            .then_inc(sem("out_stored"), 16)

                def maxima(g, u):
                    for r in range(QB):
                        sp.wait_ge(sem("unit_emptied"), r + 1 if isinstance(g, int) and g == 0 else
                                   QB + NU * (g - 1) + seq.index(("maxima", r)) + 1)
                        sp.dma_start(qs[u % U][ROWS:NEG, r * 512:r * 512 + 512].bitcast(F32),
                                     neg_rows[:, r, :].bitcast(F32))\
                            .then_inc(sem("rows_loaded" if r < QB - 1 else "last_rows_loaded"), 16)

                def turn(g, t, u, last):
                    if not (isinstance(g, int) and g == 0):
                        if not (isinstance(t, int) and t == HEADS // U - 1):
                            sp.wait_ge(sem("pv_done"), KT * g)
                            load(t + 1, u - 1)
                        store(g - 1, t, u - 1)
                    if not last:
                        maxima(g + 1, u + 1)

                for u in range(U):
                    load(0, u)
                maxima(0, 0)
                turns(turn)(sp)
                prefetch(sp)
                store(HEADS - 1, HEADS // U - 1, U - 1)
                sp.wait_ge(sem("out_stored"), 16 * QB * HEADS)

            @block.tensor
            def _(pe):
                def max_unit(g, u, i, first):
                    if i >= 3:
                        pe.wait_ge(sem("max_reduced"), NMAX * g + i - 2)
                    elif not first:
                        p = max(p for p in range(NMAX) if p % 3 == i)
                        pe.wait_ge(sem("max_reduced"), NMAX * (g - 1) + p + 1)
                    qt, j = i // QB, i % QB
                    pe.matmul(max_bank[i % 3][:, :], qs[u][0:ROWS, qt * P:qt * P + P],
                              ks[u][0:ROWS, j * 512:j * 512 + 512], start=True, stop=True)\
                        .then_inc(sem("max_done"), 1)

                def maxima(g, r, out):
                    pe.wait_ge(sem("neg_ready"), QB * g + r + 1)
                    pe.transpose(out[0:8, 0:P], neg[:, r % 2].rearrange("p a q -> p (a q)").bitcast(F32),
                                 ident2[:, :]).then_inc(sem("unit_done"), 1)

                def total(g, par):
                    pe.wait_ge(sem("pool_added"), NADD * (g + 1))
                    for j in range(QB):
                        mm = pe.matmul(sum_bank[DH * j:DH * j + DH, :], ones[:, :],
                                       prob_sum[:, par, j * 512:j * 512 + 512], start=False, stop=True)
                    mm.then_inc(sem("sum_done"), 1)

                def sem_base(g):
                    return QB + NU * g

                def values(g, t, u, kt, first):
                    s = (seq_last if isinstance(g, int) and g == HEADS - 1 else seq).index(("scores", kt, QB - 1))
                    pe.wait_ge(sem("unit_emptied"), sem_base(g) + s + 1)
                    if kt == 0:
                        pe.wait_ge(sem(f"v_loaded{u % U}"), 64 * (t + u // U + 1))
                        if not first:
                            pe.wait_ge(sem("o_copied"), g)
                    for j in range(QB):
                        mm = pe.matmul(out_bank[DH * j:DH * j + DH, :], vs[u % U][:, kt, :],
                                       probs[:, kt % RING, j * 512:j * 512 + 512],
                                       start=(kt == 0), stop=(kt == KT - 1))
                    mm.then_inc(sem("pv_done"), 1)

                def sums(g, kt, first):
                    if kt == BY_PE[0] and not first:
                        pe.wait_ge(sem("sum_read"), g)
                    for j in range(QB):
                        mm = pe.matmul(sum_bank[DH * j:DH * j + DH, :], ones[:, :],
                                       probs[:, kt % RING, j * 512:j * 512 + 512],
                                       start=(kt == BY_PE[0]), stop=False)
                    mm.then_inc(sem("tile_summed"), 1)

                def turn(g, t, u, last):
                    first = isinstance(g, int) and g == 0
                    order = seq_last if last else seq
                    made = [0]

                    def max_units(goal):
                        while not last and made[0] < goal:
                            max_unit(g + 1, (u + 1) % U, made[0], False)
                            made[0] += 1

                    def through(unit):
                        i = order.index(unit)
                        if i >= 3:
                            pe.wait_ge(sem("unit_emptied"), sem_base(g) + i - 2)
                        elif not first:
                            pe.wait_ge(sem("unit_emptied"), sem_base(g) - NU + last_in_bank(i) + 1)
                        return score_bank[i % 3]

                    if not last:
                        pe.wait_ge(sem(f"qk_loaded{(u + 1) % U}"), 96 * (t + (u + 1) // U + 1))
                    for kt in range(KT):
                        made_before = max_end[kt - 1] if kt else 0
                        a = j = 0
                        for step in ORDER:
                            if step == "A":
                                a += 1
                                max_units(min(made_before + a, max_end[kt]))
                            elif step == "S":
                                if kt == 0 and j == 0:
                                    if first:
                                        pe.wait_ge(sem("unit_emptied"), QB)
                                    pe.wait_ge(sem("rows_loaded"), 48 * (g + 1))
                                if kt == 0 and j == QB - 1:
                                    pe.wait_ge(sem("last_rows_loaded"), 16 * (g + 1))
                                out = through(("scores", kt, j))
                                pe.matmul(out[:, :], ks[u % U][0:NEG, kt * P:kt * P + P],
                                          qs[u % U][0:NEG, j * 512:j * 512 + 512], start=True, stop=True)\
                                    .then_inc(sem("unit_done"), 1)
                                i = order.index(("scores", kt, j)) + 1
                                if i < len(order) and order[i][0] == "maxima":
                                    maxima(g + 1, order[i][1], through(order[i]))
                                j += 1
                            elif step == "V" and kt >= 1:
                                values(g, t, u, kt - 1, first)
                            elif step == "V" and not first:
                                values(g - 1, t, u - 1, KT - 1, False)
                            elif step == "P" and kt - 1 in BY_PE:
                                sums(g, kt - 1, first)
                            elif step == "P" and kt == 0 and not first:
                                sums(g - 1, KT - 1, False)
                            elif step == "P" and kt == 2 and not first:
                                total(g - 1, (u - 1) % 2)
                        max_units(max_end[kt])

                pe.wait_ge(sem("qk_loaded0"), 96)
                for r in range(QB):
                    for i in range(KT * r, KT * r + KT):
                        max_unit(0, 0, i, True)
                    if r == 3:
                        pe.wait_ge(sem("unit_emptied"), 1)
                    maxima(0, r, score_bank[(NU - QB + r) % 3])
                turns(turn)(pe)
                values(HEADS - 1, HEADS // U - 1, U - 1, KT - 1, False)
                sums(HEADS - 1, KT - 1, False)
                total(HEADS - 1, (HEADS - 1) % 2)

            @block.scalar
            def _(act):
                def maxima_rows(src, r, count):
                    act.wait_ge(sem("unit_done"), count)
                    act.copy(neg_rows[:, r, :], src[0:8, 0:P]).then_inc(sem("unit_emptied"), 1)

                def copy_out(g):
                    act.wait_ge(sem("pv_done"), KT * (g + 1))
                    act.copy(o_raw[:, :], out_bank[:, :]).then_inc(sem("o_copied"), 1)

                def spread(g):
                    act.wait_ge(sem("inv_ready"), g + 1)
                    act.copy(inv_wide[:, :, :], inv[:, :].unsqueeze(2).broadcast_to([P, 512 // DH, DH]))\
                        .then_inc(sem("inv_spread"), 1)

                def turn(g, t, u, last):
                    first = isinstance(g, int) and g == 0
                    for i, unit in enumerate(seq_last if last else seq):
                        if unit == ("scores", 0, 3) and not first:
                            copy_out(g - 1)
                        if unit == ("scores", 4, 0) and not first:
                            spread(g - 1)
                        count = QB + NU * g + i + 1
                        if unit[0] == "maxima":
                            maxima_rows(score_bank[i % 3], unit[1], count)
                            continue
                        kt, j = unit[1], unit[2]
                        old = (kt - RING) % KT
                        if j == 0 and old in BY_POOL:
                            adds = max(BY_POOL.index(old), 1)
                            if kt >= RING:
                                act.wait_ge(sem("pool_added"), NADD * g + adds)
                            elif not first:
                                act.wait_ge(sem("pool_added"), NADD * (g - 1) + adds)
                        act.wait_ge(sem("unit_done"), count)
                        act.activation(probs[:, kt % RING, j * 512:j * 512 + 512], score_bank[i % 3][:, :],
                                       ACT.Exp, scale=SCALE).then_inc(sem("unit_emptied"), 1)

                for r in range(QB):
                    maxima_rows(score_bank[(NU - QB + r) % 3], r, r + 1)
                turns(turn)(act)
                act.wait_ge(sem("out_ready"), HEADS - 1)
                copy_out(HEADS - 1)
                spread(HEADS - 1)

            @block.gpsimd
            def _(pool):
                def turn(g, t, u, last):
                    acc = prob_sum[:, u % 2, :]
                    for n in range(1, len(BY_POOL)):
                        kt = BY_POOL[n]
                        s = (seq_last if last else seq).index(("scores", kt, QB - 1))
                        pool.wait_ge(sem("unit_emptied"), QB + NU * g + s + 1)
                        other = probs[:, BY_POOL[0] % RING, :] if n == 1 else acc
                        pool.tensor_tensor(acc, other, probs[:, kt % RING, :], ALU.add)\
                            .then_inc(sem("pool_added"), 1)
                        pool.wait_ge(sem("pool_added"), NADD * g + n)
                turns(turn)(pool)

            @block.vector
            def _(dve):
                def reduce_unit(g, i):
                    qt, j = i // QB, i % QB
                    r = qt // 4
                    dve.wait_ge(sem("max_done"), NMAX * g + i + 1)
                    dve.tensor_reduce(part_max[:, r % 2, qt, j:j + 1], max_bank[i % 3][:, :], AX.X, ALU.max)\
                        .then_inc(sem("max_reduced"), 1)
                    if i % KT == KT - 1:
                        c = Chain(dve, sem("dve_order"), 2 * (QB * g + r))
                        dve.wait_ge(sem("max_reduced"), NMAX * g + i + 1)
                        cols = slice(4 * r, 4 * r + 4)
                        c.link(dve.tensor_reduce(neg_max[:, r % 2, cols], part_max[:, r % 2, cols, :], AX.X,
                                                 ALU.max, negate=True))
                        c.link(dve.tensor_copy(neg[:, r % 2, 0, :], neg_max[:, r % 2, cols]))
                        dve.tensor_tensor(neg[:, r % 2, 1, :], neg_max[:, r % 2, cols],
                                          neg[:, r % 2, 0, :].bitcast(F32), ALU.subtract)\
                            .then_inc(sem("neg_ready"), 1)

                def invert(g):
                    dve.wait_ge(sem("sum_done"), g + 1)
                    dve.transpose(sums_t[:, :], sum_bank[:, :]).then_inc(sem("sum_read"), 1)
                    dve.wait_ge(sem("sum_read"), g + 1)
                    dve.reciprocal(inv[:, :], sums_t[:, 0:512:DH]).then_inc(sem("inv_ready"), 1)

                def normalise(g):
                    dve.wait_ge(sem("inv_spread"), g + 1)
                    dve.transpose(inv_rows[:, :], inv_wide[:, :, :].rearrange("p a b -> p (a b)"))\
                        .then_inc(sem("inv_back"), 1)
                    dve.wait_ge(sem("inv_back"), g + 1)
                    dve.tensor_tensor(o_out[:, :], o_raw[:, :], inv_rows[:, :], ALU.mult)\
                        .then_inc(sem("out_ready"), 1)

                def turn(g, t, u, last):
                    first = isinstance(g, int) and g == 0
                    for kt in range(KT):
                        if not last:
                            for i in range(max_end[kt - 1] if kt else 0, max_end[kt]):
                                reduce_unit(g + 1, i)
                        if kt == 2 and not first:
                            invert(g - 1)
                        if kt == 5 and not first:
                            normalise(g - 1)
                    if not first:
                        dve.wait_ge(sem("out_stored"), 16 * QB * g)

                for i in range(NMAX):
                    reduce_unit(0, i)
                turns(turn)(dve)
                invert(HEADS - 1)
                normalise(HEADS - 1)


class OutputBuffers:

    def __init__(self, nc, ctx, a, scr):
        self.a, self.scr = a, scr
        self.w_t = ctx.enter_context(nc.sbuf_tensor("ow_t", [P, KD, D], F32))
        self.bias = ctx.enter_context(nc.sbuf_tensor("o_bias", [P, D], F32))
        self.res = [[ctx.enter_context(nc.sbuf_tensor(f"res{i}{e}", [P, TB, D], F32)) for e in range(E)]
                    for i in range(2)]
        self.weights = ctx.enter_context(nc.semaphore("s3_weights"))
        self.res_loaded = [[ctx.enter_context(nc.semaphore(f"s3_res_loaded{i}{e}")) for e in range(E)]
                           for i in range(2)]

    def load_residual(self, eng, b, i, e):
        eng.dma_start(self.res[i][e][:, :, :], self.scr["resid"][bass.ds(4 * b + e, 1)]
                      .rearrange("a p t d -> (a p) t d")).then_inc(self.res_loaded[i][e], 16)

    def prefetch(self, eng):
        eng.dma_start(self.w_t[:, :, :], self.a["o_w_t"].rearrange("(k p) n -> p k n", p=P))\
            .then_inc(self.weights, 16)
        eng.dma_start(self.bias[:, :], self.a["o_b"].rearrange("(a n) -> a n", a=1).broadcast_to([P, D]))\
            .then_inc(self.weights, 16)
        for b in range(2):
            for e in range(E):
                self.load_residual(eng, b, b, e)


def output_stage(nc, scr, out, early):
    ctx = ExitStack()
    with ctx:
        def sb(name, shape, dt=F32):
            return ctx.enter_context(nc.sbuf_tensor(name, shape, dt))

        sems = {}

        def sem(name):
            if name not in sems:
                sems[name] = ctx.enter_context(nc.semaphore("s3_" + name))
            return sems[name]

        bank = [ctx.enter_context(nc.psum_tensor(f"ob{i}", [P, 2, D], F32)) for i in range(8)]
        w_t, bias, res = early.w_t, early.bias, early.res
        attn = [[sb(f"attn{j}{e}", [P, NK[e], NB]) for e in range(E)] for j in range(2)]
        rows = out.rearrange("b (e t p) d -> (b e) p t d", e=E, p=P)

        with nc.Block() as block:
            @block.sync
            def _(sp):
                def load(b, j, e):
                    for k, m in enumerate(MK[e]):
                        sp.dma_start(attn[j][e][0:m, k, :], scr["attn"][bass.ds(8 * b + 4 * k + e, 1), 0:m, :]
                                     .rearrange("a d q -> (a d) q")).then_inc(sem(f"attn_loaded{j}{e}"), 16)

                for j in range(2):
                    for e in range(E):
                        load(j, j, e)
                with sp.Fori(1, B // 2) as i:
                    for j in range(2):
                        for e in range(E):
                            sp.wait_ge(sem(f"stored{j}{e}"), 16 * i)
                            load(2 * i + j, j, e)
                            early.load_residual(sp, 2 * i + j, j, e)

            @block.scalar
            def _(act):
                with act.Fori(0, B // 2) as i:
                    for j in range(2):
                        for e in range(E):
                            n = 8 * i + 4 * j + e
                            act.wait_ge(sem("sum_ready"), n + 1)
                            act.dma_start(rows[bass.ds(n, 1)].rearrange("a p t d -> (a p) t d"),
                                          res[j][e][:, :, :]).then_inc(sem(f"stored{j}{e}"), 16)
                for j in range(2):
                    for e in range(E):
                        act.wait_ge(sem(f"stored{j}{e}"), 16 * B // 2)

            @block.tensor
            def _(pe):
                pe.wait_ge(early.weights, 32)

                def batch(i, j, first):
                    for e in range(E):
                        m = D >> e
                        pe.wait_ge(sem(f"attn_loaded{j}{e}"), 16 * NK[e] * (i + 1))
                        if not first:
                            pe.wait_ge(sem("sum_ready"), 8 * i + 4 * j + e - 3)
                        for tile in range(TB):
                            for k, mk in enumerate(MK[e]):
                                mm = pe.matmul(bank[2 * e + tile // 2][:, tile % 2, 0:m],
                                               attn[j][e][0:mk, k, tile * P:tile * P + P], w_t[0:mk, k, 0:m],
                                               start=(k == 0), stop=(k == NK[e] - 1))
                        mm.then_inc(sem("proj_done"), 1)

                batch(0, 0, True)
                batch(0, 1, False)
                with pe.Fori(1, B // 2) as i:
                    batch(i, 0, False)
                    batch(i, 1, False)

            @block.vector
            def _(dve):
                dve.wait_ge(early.weights, 32)
                with dve.Fori(0, B // 2) as i:
                    for j in range(2):
                        for e in range(E):
                            n, m = 8 * i + 4 * j + e, D >> e
                            dve.wait_ge(early.res_loaded[j][e], 16 * (i + 1))
                            dve.tensor_tensor(res[j][e][:, :, 0:m], res[j][e][:, :, 0:m],
                                              bias[:, 0:m].unsqueeze(1).broadcast_to([P, TB, m]), ALU.add)\
                                .then_inc(sem("biased"), 1)
                            dve.wait_ge(sem("biased"), n + 1)
                            dve.wait_ge(sem("proj_done"), n + 1)
                            for half in range(2):
                                x = res[j][e][:, 2 * half:2 * half + 2, 0:m]
                                ins = dve.tensor_tensor(x, bank[2 * e + half][:, :, 0:m], x, ALU.add)
                            ins.then_inc(sem("sum_ready"), 1)




def build(nc, a, out):
    def scratch(name, shape):
        return nc.dram_tensor(name, shape, F32, kind="Internal").ap()
    scr = {
        "hi": scratch("scr_hi", (B * 2 * 2, P, T)),
        "lo": scratch("scr_lo", (B * 2 * 2, P, T)),
        "v": scratch("scr_v", (B * 2 * E, P, TB, P)),
        "resid": scratch("scr_resid", (B * E, P, TB, D)),
        "attn": scratch("scr_attn", (B * 2 * E, P, NB)),
    }
    token_stage(nc, a, scr)
    with ExitStack() as ctx:
        early = OutputBuffers(nc, ctx, a, scr)
        attention_stage(nc, a, scr, early.prefetch)
        output_stage(nc, scr, out, early)


_ARRAYS = {
    "tokens": None,
    "emb_0": "L0_tok_emb_0", "emb_1": "L0_tok_emb_1", "emb_2": "L0_tok_emb_2", "emb_3": "L0_tok_emb_3",
    "proj_0_t": "L0_tok_proj_0", "proj_1_t": "L0_tok_proj_1", "proj_2_t": "L0_tok_proj_2",
    "proj_3_t": "L0_tok_proj_3",
    "Wq": "L0_attn_Wq", "Wk": "L0_attn_Wk", "Wv_t": "L0_attn_Wv", "Wo_t": "L0_attn_Wo",
    "fmq_w_t": "L0_attn_fmq_w", "fmk_w_t": "L0_attn_fmk_w", "fmq_b": "L0_attn_fmq_b",
    "fmk_b": "L0_attn_fmk_b", "rms_w": "L0_attn_rms_w",
    "norm_w": "L0_ffn_norm_w", "norm_b": "L0_ffn_norm_b",
    "q_w_t": "L0_ffn_q_w", "q_b": "L0_ffn_q_b", "k_w_t": "L0_ffn_k_w", "k_b": "L0_ffn_k_b",
    "v_w_t": "L0_ffn_v_w", "v_b": "L0_ffn_v_b", "o_w_t": "L0_ffn_o_w", "o_b": "L0_ffn_o_b",
}


def kernel(**inputs):
    import concourse.bacc as _bacc
    from concourse.bass_utils import run_bass_kernel_spmd as _run

    nc = _bacc.Bacc("TRN2", target_bir_lowering=False, num_devices=1)
    arrays, aps = {}, {}
    for name, source in _ARRAYS.items():
        if source is None:
            x = np.asarray(inputs["x"]).reshape(B * T // P, P).T
        else:
            x = np.asarray(inputs[source])
            if name.endswith("_t"):
                x = x.T
        x = np.ascontiguousarray(x)
        arrays["in_" + name] = x
        aps[name] = nc.dram_tensor("in_" + name, x.shape, mybir.dt.from_np(x.dtype), kind="ExternalInput").ap()
    out = nc.dram_tensor("out_0", (B, T, D), F32, kind="ExternalOutput").ap()
    build(nc, aps, out)
    r = _run(nc, [arrays], core_ids=[0])
    return r.results[0]["out_0"]
```
